# Optimizing a Trainium2 kernel written in Bass

```python
import numpy as np
import jax
import jax.numpy as jnp

def _softmax(x, axis=-1):
    return jax.nn.softmax(x, axis=axis)

def _gelu(x):
    return jax.nn.gelu(x, approximate=True)

def _silu(x):
    return jax.nn.silu(x)

def _sigmoid(x):
    return jax.nn.sigmoid(x)

def _layernorm(x, axis=-1, eps=1e-05):
    m = jnp.mean(x, axis=axis, keepdims=True)
    v = jnp.var(x, axis=axis, keepdims=True)
    return (x - m) / jnp.sqrt(v + eps)

def _scatter_add(tgt, idx, src, axis=0):
    return tgt.at[idx].add(src)

def _segment_sum(src, seg, n):
    return jax.ops.segment_sum(src, seg, n)
kernel_name = 'mk_adj_ffn_d4_adj_r2_59c9f6'

def setup_inputs(seed: int=0):
    np.random.seed(seed)
    _w = jnp.asarray

    def _rec_inputs():
        import jax
        import jax.numpy as jnp
        _gk = jax.random.key(seed)
        x = -0.0002928 + 1 * jax.random.normal(jax.random.fold_in(_gk, 1), (64, 128, 128), jnp.float32)
        _a = jax.random.bernoulli(jax.random.fold_in(_gk, 2), 0.125, (64, 128, 128))
        adj = _a.astype(jnp.int32)
        return (x, adj)
    x, adj = _rec_inputs()

    def _L0_gnn_setup():
        import jax, jax.numpy as jnp
        import numpy as np
        NEG_BIG = -9000000000000000.0
        ALPHA = 0.2
        key = jax.random.key(seed)
        k1, k2, k3, k4 = jax.random.split(key, 4)
        B, N, Fin, Fout = (8, 1024, 128, 128)
        h = jax.random.normal(k1, (B, N, Fin), dtype=jnp.float32)
        adj = jax.random.randint(k2, (B, N, N), 0, 2, dtype=jnp.int32)
        limW = 1.414 * np.sqrt(6.0 / (Fin + Fout))
        W = jax.random.uniform(k3, (Fin, Fout), jnp.float32, -limW, limW)
        lima = 1.414 * np.sqrt(6.0 / (2 * Fout + 1))
        a = jax.random.uniform(k4, (2 * Fout, 1), jnp.float32, -lima, lima)
        return {'h': h, 'adj': adj, 'W': W, 'a': a}
    _L0_gnn_all = _L0_gnn_setup()
    _L0_gnn_in = {k: v for k, v in _L0_gnn_all.items() if k in ('W', 'a')}
    del _L0_gnn_all

    def _L0_ffn_setup():
        import jax, jax.numpy as jnp
        import numpy as np
        D_MODEL = 128
        D_STATE = 64
        D_CONV = 4
        EXPAND = 2
        HEADDIM = 64
        D_INNER = EXPAND * D_MODEL
        NHEADS = D_INNER // HEADDIM
        CONV_DIM = D_INNER + 2 * D_STATE
        D_IN_PROJ = 2 * D_INNER + 2 * D_STATE + NHEADS
        CHUNK = 128
        EPS = 1e-05

        def segsum(a):
            T = a.shape[-1]
            cs = jnp.cumsum(a, axis=-1)
            ss = cs[..., :, None] - cs[..., None, :]
            mask = jnp.tril(jnp.ones((T, T), dtype=bool))
            return jnp.where(mask, ss, -jnp.inf)

        def mamba2_block(x, W_in, conv_w, conv_b, dt_bias, A_log, D, norm_w, W_out, W_lin, b_lin):
            Bsz, L, _ = x.shape
            zxbcdt = x @ W_in
            z, xBC, dt = jnp.split(zxbcdt, [D_INNER, D_INNER + CONV_DIM], axis=-1)
            xp = jnp.pad(xBC, ((0, 0), (D_CONV - 1, 0), (0, 0)))
            conv = conv_b + sum((xp[:, k:k + L, :] * conv_w[:, k] for k in range(D_CONV)))
            xBC = jax.nn.silu(conv)
            xh, Bmat, Cmat = jnp.split(xBC, [D_INNER, D_INNER + D_STATE], axis=-1)
            dt = jax.nn.softplus(dt + dt_bias)
            A = -jnp.exp(A_log)
            nc = L // CHUNK
            xh = xh.reshape(Bsz, nc, CHUNK, NHEADS, HEADDIM)
            Bc = Bmat.reshape(Bsz, nc, CHUNK, D_STATE)
            Cc = Cmat.reshape(Bsz, nc, CHUNK, D_STATE)
            dtc = dt.reshape(Bsz, nc, CHUNK, NHEADS)
            dA = jnp.einsum('bclh,h->bhcl', dtc, A)
            A_cum = jnp.cumsum(dA, axis=-1)
            Lmat = jnp.exp(segsum(dA))
            xdt = xh * dtc[..., None]
            Y_diag = jnp.einsum('bcln,bcsn,bhcls,bcshp->bclhp', Cc, Bc, Lmat, xdt)
            decay_states = jnp.exp(A_cum[..., -1:] - A_cum)
            states = jnp.einsum('bcln,bhcl,bclhp->bchpn', Bc, decay_states, xdt)
            chunk_decay = jnp.exp(A_cum[..., -1])

            def step(h, inp):
                s, d = inp
                return (h * d[..., None, None] + s, h)
            _, prevs = jax.lax.scan(step, jnp.zeros_like(states[:, 0]), (jnp.moveaxis(states, 1, 0), jnp.moveaxis(chunk_decay, 2, 0)))
            prevs = jnp.moveaxis(prevs, 0, 1)
            Y_off = jnp.einsum('bcln,bchpn,bhcl->bclhp', Cc, prevs, jnp.exp(A_cum))
            Y = (Y_diag + Y_off + xh * D[:, None]).reshape(Bsz, L, D_INNER)
            Y = Y * jax.nn.silu(z)
            Y = Y * jax.lax.rsqrt(jnp.mean(Y * Y, axis=-1, keepdims=True) + EPS) * norm_w
            out = Y @ W_out
            return out @ W_lin + b_lin
        key = jax.random.key(seed)
        ks = jax.random.split(key, 12)
        B, L = (8, 2048)

        def gauss(k, shape, scale):
            return jax.random.normal(k, shape, dtype=jnp.float32) * scale
        return {'x': gauss(ks[0], (B, L, D_MODEL), 1.0), 'W_in': gauss(ks[1], (D_MODEL, D_IN_PROJ), D_MODEL ** (-0.5)), 'conv_w': gauss(ks[2], (CONV_DIM, D_CONV), 0.3), 'conv_b': gauss(ks[3], (CONV_DIM,), 0.1), 'dt_bias': jax.random.uniform(ks[4], (NHEADS,), minval=-4.0, maxval=-1.0), 'A_log': jnp.log(jax.random.uniform(ks[5], (NHEADS,), minval=1.0, maxval=16.0)), 'D': jnp.ones((NHEADS,), jnp.float32), 'norm_w': jnp.ones((D_INNER,), jnp.float32), 'W_out': gauss(ks[6], (D_INNER, D_MODEL), D_INNER ** (-0.5)), 'W_lin': gauss(ks[7], (D_MODEL, D_MODEL), D_MODEL ** (-0.5)), 'b_lin': jnp.zeros((D_MODEL,), jnp.float32)}
    _L0_ffn_all = _L0_ffn_setup()
    _L0_ffn_in = {k: v for k, v in _L0_ffn_all.items() if k in ('W_in', 'conv_w', 'conv_b', 'dt_bias', 'A_log', 'D', 'norm_w', 'W_out', 'W_lin', 'b_lin')}
    del _L0_ffn_all

    def _L1_gnn_setup():
        import jax, jax.numpy as jnp
        import numpy as np
        import math
        B, N, IN_DIM, OUT_DIM, H = (8, 512, 128, 128, 8)
        D_K = OUT_DIM // H
        key = jax.random.key(seed)
        ks = jax.random.split(key, 12)
        s_in = 1.0 / math.sqrt(IN_DIM)
        s_out = 1.0 / math.sqrt(OUT_DIM)
        return {'X': jax.random.normal(ks[0], (B, N, IN_DIM), jnp.float32), 'A': jax.random.randint(ks[1], (B, N, N), 0, 2, jnp.int32), 'D': jax.random.uniform(ks[2], (B, N, N), jnp.float32), 'W_q': jax.random.uniform(ks[3], (IN_DIM, OUT_DIM), jnp.float32, -s_in, s_in), 'b_q': jax.random.uniform(ks[4], (OUT_DIM,), jnp.float32, -s_in, s_in), 'W_k': jax.random.uniform(ks[5], (IN_DIM, OUT_DIM), jnp.float32, -s_in, s_in), 'b_k': jax.random.uniform(ks[6], (OUT_DIM,), jnp.float32, -s_in, s_in), 'W_v': jax.random.uniform(ks[7], (IN_DIM, OUT_DIM), jnp.float32, -s_in, s_in), 'b_v': jax.random.uniform(ks[8], (OUT_DIM,), jnp.float32, -s_in, s_in), 'W_o': jax.random.uniform(ks[9], (OUT_DIM, OUT_DIM), jnp.float32, -s_out, s_out), 'b_o': jax.random.uniform(ks[10], (OUT_DIM,), jnp.float32, -s_out, s_out), 'dist_scale': jnp.array(1.0, jnp.float32)}
    _L1_gnn_all = _L1_gnn_setup()
    _L1_gnn_in = {k: v for k, v in _L1_gnn_all.items() if k in ('W_q', 'b_q', 'W_k', 'b_k', 'W_v', 'b_v', 'W_o', 'b_o', 'dist_scale')}
    del _L1_gnn_all

    def _L1_ffn_setup():
        import jax, jax.numpy as jnp
        import numpy as np
        C = 128
        HID = 512
        E = 8
        TEMP = 1.0
        key = jax.random.key(seed)
        ks = jax.random.split(key, 7)
        x = jax.random.normal(ks[0], (8, 8192, C), dtype=jnp.float32)
        W1 = jax.random.normal(ks[1], (C, HID), dtype=jnp.float32) * 0.02
        b1 = jnp.zeros((HID,), dtype=jnp.float32)
        Wg = jax.random.normal(ks[2], (HID, E), dtype=jnp.float32) * 0.02
        bg = jnp.zeros((E,), dtype=jnp.float32)
        Wd = jax.random.normal(ks[3], (E, HID, C), dtype=jnp.float32) * 0.02
        bd = jnp.zeros((E, C), dtype=jnp.float32)
        return {'x': x, 'W1': W1, 'b1': b1, 'Wg': Wg, 'bg': bg, 'Wd': Wd, 'bd': bd}
    _L1_ffn_all = _L1_ffn_setup()
    _L1_ffn_in = {k: v for k, v in _L1_ffn_all.items() if k in ('W1', 'b1', 'Wg', 'bg', 'Wd', 'bd')}
    del _L1_ffn_all

    def _L2_gnn_setup():
        import jax, jax.numpy as jnp
        import numpy as np
        ALPHA = 0.2
        NEG_INF = -9000000000000000.0
        key = jax.random.key(seed)
        k1, k2, k3, k4 = jax.random.split(key, 4)
        B, N, D = (8, 1024, 128)
        h = jax.random.normal(k1, (B, N, D), dtype=jnp.float32)
        adj = jax.random.randint(k2, (B, N, N), 0, 2, dtype=jnp.int32)
        W = jax.random.normal(k3, (D, D), dtype=jnp.float32) * (1.0 / np.sqrt(D))
        a = jax.random.normal(k4, (2 * D, 1), dtype=jnp.float32) * 0.05
        return {'h': h, 'adj': adj, 'W': W, 'a': a}
    _L2_gnn_all = _L2_gnn_setup()
    _L2_gnn_in = {k: v for k, v in _L2_gnn_all.items() if k in ('W', 'a')}
    del _L2_gnn_all

    def _L2_ffn_setup():
        import jax, jax.numpy as jnp
        import numpy as np
        B, A = (2048, 8)
        IN, OUT = (128, 128)
        SH1, SH2 = (128, 128)
        EH1, EH2 = (128, 64)
        E, TOPK = (4, 2)

        def _shared_mlp(x, W1, b1, W2, b2, W3, b3):
            h = jax.nn.relu(x @ W1 + b1)
            h = jax.nn.relu(h @ W2 + b2)
            return h @ W3 + b3

        def _experts_mlp(x, eW1, eb1, eW2, eb2, eW3, eb3):
            h = jax.nn.relu(jnp.einsum('baf,efh->ebah', x, eW1) + eb1[:, None, None, :])
            h = jax.nn.relu(jnp.einsum('ebah,ehg->ebag', h, eW2) + eb2[:, None, None, :])
            o = jnp.einsum('ebag,ego->ebao', h, eW3) + eb3[:, None, None, :]
            return jnp.moveaxis(o, 0, -1)
        key = jax.random.key(seed)
        ks = jax.random.split(key, 16)
        s = 0.05
        return {'x': jax.random.normal(ks[0], (B, A, IN), jnp.float32), 'sW1': jax.random.normal(ks[1], (IN, SH1), jnp.float32) * s, 'sb1': jnp.zeros((SH1,), jnp.float32), 'sW2': jax.random.normal(ks[2], (SH1, SH2), jnp.float32) * s, 'sb2': jnp.zeros((SH2,), jnp.float32), 'sW3': jax.random.normal(ks[3], (SH2, OUT), jnp.float32) * s, 'sb3': jnp.zeros((OUT,), jnp.float32), 'eW1': jax.random.normal(ks[4], (E, IN, EH1), jnp.float32) * s, 'eb1': jnp.zeros((E, EH1), jnp.float32), 'eW2': jax.random.normal(ks[5], (E, EH1, EH2), jnp.float32) * s, 'eb2': jnp.zeros((E, EH2), jnp.float32), 'eW3': jax.random.normal(ks[6], (E, EH2, OUT), jnp.float32) * s, 'eb3': jnp.zeros((E, OUT), jnp.float32), 'gW': jax.random.normal(ks[7], (IN, E), jnp.float32) * s, 'gb': jnp.zeros((E,), jnp.float32)}
    _L2_ffn_all = _L2_ffn_setup()
    _L2_ffn_in = {k: v for k, v in _L2_ffn_all.items() if k in ('sW1', 'sb1', 'sW2', 'sb2', 'sW3', 'sb3', 'eW1', 'eb1', 'eW2', 'eb2', 'eW3', 'eb3', 'gW', 'gb')}
    del _L2_ffn_all

    def _L3_gnn_setup():
        import jax, jax.numpy as jnp
        import numpy as np
        ALPHA = 0.2
        NEG_BIG = -9000000000000000.0
        key = jax.random.key(seed)
        k1, k2, k3, k4 = jax.random.split(key, 4)
        B, N, Fin, Fout = (8, 1024, 128, 128)
        h = jax.random.normal(k1, (B, N, Fin), dtype=jnp.float32)
        adj = jax.random.randint(k2, (B, N, N), 0, 2, dtype=jnp.int32)
        W = jax.random.normal(k3, (Fin, Fout), dtype=jnp.float32) * 0.05
        a = jax.random.normal(k4, (2 * Fout, 1), dtype=jnp.float32) * 0.05
        return {'h': h, 'adj': adj, 'W': W, 'a': a}
    _L3_gnn_all = _L3_gnn_setup()
    _L3_gnn_in = {k: v for k, v in _L3_gnn_all.items() if k in ('W', 'a')}
    del _L3_gnn_all

    def _L3_ffn_setup():
        import jax, jax.numpy as jnp
        import numpy as np
        B, T, C = (64, 192, 128)
        NH, NKV = (4, 2)
        HD = C // NH
        NREP = NH // NKV
        NE, TOPK = (8, 2)
        HID = int(8 / 3 * C)
        EPS_RMS = 1e-06

        def _rope_tables(t_len):
            inv_freq = 1.0 / 10000.0 ** (np.arange(0, HD, 2, dtype=np.float32) / HD)
            t = np.arange(t_len, dtype=np.float32)
            freqs = np.outer(t, inv_freq)
            emb = np.concatenate([freqs, freqs], axis=-1)
            return (jnp.asarray(np.cos(emb)), jnp.asarray(np.sin(emb)))

        def _rotate_half(x):
            h = x.shape[-1] // 2
            return jnp.concatenate([-x[..., h:], x[..., :h]], axis=-1)

        def _rmsnorm(v, w):
            return v * jax.lax.rsqrt(jnp.mean(v * v, axis=-1, keepdims=True) + EPS_RMS) * w
        key = jax.random.key(seed)
        ks = jax.random.split(key, 10)
        s = lambda k, shape: jax.random.normal(k, shape, jnp.float32) * 0.02
        return {'x': jax.random.normal(ks[0], (B, T, C), jnp.float32), 'ln1_w': jnp.ones((C,), jnp.float32), 'ln2_w': jnp.ones((C,), jnp.float32), 'wq': s(ks[1], (NH * HD, C)), 'wk': s(ks[2], (NKV * HD, C)), 'wv': s(ks[3], (NKV * HD, C)), 'wo': s(ks[4], (C, C)), 'router_w': s(ks[5], (NE, C)), 'w1': s(ks[6], (NE, HID, C)), 'w2': s(ks[7], (NE, C, HID)), 'w3': s(ks[8], (NE, HID, C))}
    _L3_ffn_all = _L3_ffn_setup()
    _L3_ffn_in = {k: v for k, v in _L3_ffn_all.items() if k in ('ln1_w', 'ln2_w', 'wq', 'wk', 'wv', 'wo', 'router_w', 'w1', 'w2', 'w3')}
    del _L3_ffn_all
    return {'x': x, 'adj': adj, 'L0_gnn_W': _L0_gnn_in['W'], 'L0_gnn_a': _L0_gnn_in['a'], 'L0_ffn_W_in': _L0_ffn_in['W_in'], 'L0_ffn_conv_w': _L0_ffn_in['conv_w'], 'L0_ffn_conv_b': _L0_ffn_in['conv_b'], 'L0_ffn_dt_bias': _L0_ffn_in['dt_bias'], 'L0_ffn_A_log': _L0_ffn_in['A_log'], 'L0_ffn_D': _L0_ffn_in['D'], 'L0_ffn_norm_w': _L0_ffn_in['norm_w'], 'L0_ffn_W_out': _L0_ffn_in['W_out'], 'L0_ffn_W_lin': _L0_ffn_in['W_lin'], 'L0_ffn_b_lin': _L0_ffn_in['b_lin'], 'L1_gnn_W_q': _L1_gnn_in['W_q'], 'L1_gnn_b_q': _L1_gnn_in['b_q'], 'L1_gnn_W_k': _L1_gnn_in['W_k'], 'L1_gnn_b_k': _L1_gnn_in['b_k'], 'L1_gnn_W_v': _L1_gnn_in['W_v'], 'L1_gnn_b_v': _L1_gnn_in['b_v'], 'L1_gnn_W_o': _L1_gnn_in['W_o'], 'L1_gnn_b_o': _L1_gnn_in['b_o'], 'L1_gnn_dist_scale': _L1_gnn_in['dist_scale'], 'L1_ffn_W1': _L1_ffn_in['W1'], 'L1_ffn_b1': _L1_ffn_in['b1'], 'L1_ffn_Wg': _L1_ffn_in['Wg'], 'L1_ffn_bg': _L1_ffn_in['bg'], 'L1_ffn_Wd': _L1_ffn_in['Wd'], 'L1_ffn_bd': _L1_ffn_in['bd'], 'L2_gnn_W': _L2_gnn_in['W'], 'L2_gnn_a': _L2_gnn_in['a'], 'L2_ffn_sW1': _L2_ffn_in['sW1'], 'L2_ffn_sb1': _L2_ffn_in['sb1'], 'L2_ffn_sW2': _L2_ffn_in['sW2'], 'L2_ffn_sb2': _L2_ffn_in['sb2'], 'L2_ffn_sW3': _L2_ffn_in['sW3'], 'L2_ffn_sb3': _L2_ffn_in['sb3'], 'L2_ffn_eW1': _L2_ffn_in['eW1'], 'L2_ffn_eb1': _L2_ffn_in['eb1'], 'L2_ffn_eW2': _L2_ffn_in['eW2'], 'L2_ffn_eb2': _L2_ffn_in['eb2'], 'L2_ffn_eW3': _L2_ffn_in['eW3'], 'L2_ffn_eb3': _L2_ffn_in['eb3'], 'L2_ffn_gW': _L2_ffn_in['gW'], 'L2_ffn_gb': _L2_ffn_in['gb'], 'L3_gnn_W': _L3_gnn_in['W'], 'L3_gnn_a': _L3_gnn_in['a'], 'L3_ffn_ln1_w': _L3_ffn_in['ln1_w'], 'L3_ffn_ln2_w': _L3_ffn_in['ln2_w'], 'L3_ffn_wq': _L3_ffn_in['wq'], 'L3_ffn_wk': _L3_ffn_in['wk'], 'L3_ffn_wv': _L3_ffn_in['wv'], 'L3_ffn_wo': _L3_ffn_in['wo'], 'L3_ffn_router_w': _L3_ffn_in['router_w'], 'L3_ffn_w1': _L3_ffn_in['w1'], 'L3_ffn_w2': _L3_ffn_in['w2'], 'L3_ffn_w3': _L3_ffn_in['w3']}

def reference(x, adj, L0_gnn_W, L0_gnn_a, L0_ffn_W_in, L0_ffn_conv_w, L0_ffn_conv_b, L0_ffn_dt_bias, L0_ffn_A_log, L0_ffn_D, L0_ffn_norm_w, L0_ffn_W_out, L0_ffn_W_lin, L0_ffn_b_lin, L1_gnn_W_q, L1_gnn_b_q, L1_gnn_W_k, L1_gnn_b_k, L1_gnn_W_v, L1_gnn_b_v, L1_gnn_W_o, L1_gnn_b_o, L1_gnn_dist_scale, L1_ffn_W1, L1_ffn_b1, L1_ffn_Wg, L1_ffn_bg, L1_ffn_Wd, L1_ffn_bd, L2_gnn_W, L2_gnn_a, L2_ffn_sW1, L2_ffn_sb1, L2_ffn_sW2, L2_ffn_sb2, L2_ffn_sW3, L2_ffn_sb3, L2_ffn_eW1, L2_ffn_eb1, L2_ffn_eW2, L2_ffn_eb2, L2_ffn_eW3, L2_ffn_eb3, L2_ffn_gW, L2_ffn_gb, L3_gnn_W, L3_gnn_a, L3_ffn_ln1_w, L3_ffn_ln2_w, L3_ffn_wq, L3_ffn_wk, L3_ffn_wv, L3_ffn_wo, L3_ffn_router_w, L3_ffn_w1, L3_ffn_w2, L3_ffn_w3):
    import jax
    import jax.numpy as jnp

    def _L0_gnn_ref(h, adj, W, a):
        import jax, jax.numpy as jnp
        import numpy as np
        NEG_BIG = -9000000000000000.0
        ALPHA = 0.2
        Fout = W.shape[1]
        wh = jnp.einsum('bni,io->bno', h, W)
        a1 = a[:Fout, 0]
        a2 = a[Fout:, 0]
        s1 = wh @ a1
        s2 = wh @ a2
        e = jax.nn.leaky_relu(s1[:, :, None] + s2[:, None, :], negative_slope=ALPHA)
        e = jnp.where(adj > 0, e, NEG_BIG)
        attention = jax.nn.softmax(e, axis=2)
        h_prime = jnp.einsum('bmn,bno->bmo', attention, wh)
        return h_prime

    def _L0_ffn_ref(x, W_in, conv_w, conv_b, dt_bias, A_log, D, norm_w, W_out, W_lin, b_lin):
        import jax, jax.numpy as jnp
        import numpy as np
        D_MODEL = 128
        D_STATE = 64
        D_CONV = 4
        EXPAND = 2
        HEADDIM = 64
        D_INNER = EXPAND * D_MODEL
        NHEADS = D_INNER // HEADDIM
        CONV_DIM = D_INNER + 2 * D_STATE
        D_IN_PROJ = 2 * D_INNER + 2 * D_STATE + NHEADS
        CHUNK = 128
        EPS = 1e-05

        def segsum(a):
            T = a.shape[-1]
            cs = jnp.cumsum(a, axis=-1)
            ss = cs[..., :, None] - cs[..., None, :]
            mask = jnp.tril(jnp.ones((T, T), dtype=bool))
            return jnp.where(mask, ss, -jnp.inf)

        def mamba2_block(x, W_in, conv_w, conv_b, dt_bias, A_log, D, norm_w, W_out, W_lin, b_lin):
            Bsz, L, _ = x.shape
            zxbcdt = x @ W_in
            z, xBC, dt = jnp.split(zxbcdt, [D_INNER, D_INNER + CONV_DIM], axis=-1)
            xp = jnp.pad(xBC, ((0, 0), (D_CONV - 1, 0), (0, 0)))
            conv = conv_b + sum((xp[:, k:k + L, :] * conv_w[:, k] for k in range(D_CONV)))
            xBC = jax.nn.silu(conv)
            xh, Bmat, Cmat = jnp.split(xBC, [D_INNER, D_INNER + D_STATE], axis=-1)
            dt = jax.nn.softplus(dt + dt_bias)
            A = -jnp.exp(A_log)
            nc = L // CHUNK
            xh = xh.reshape(Bsz, nc, CHUNK, NHEADS, HEADDIM)
            Bc = Bmat.reshape(Bsz, nc, CHUNK, D_STATE)
            Cc = Cmat.reshape(Bsz, nc, CHUNK, D_STATE)
            dtc = dt.reshape(Bsz, nc, CHUNK, NHEADS)
            dA = jnp.einsum('bclh,h->bhcl', dtc, A)
            A_cum = jnp.cumsum(dA, axis=-1)
            Lmat = jnp.exp(segsum(dA))
            xdt = xh * dtc[..., None]
            Y_diag = jnp.einsum('bcln,bcsn,bhcls,bcshp->bclhp', Cc, Bc, Lmat, xdt)
            decay_states = jnp.exp(A_cum[..., -1:] - A_cum)
            states = jnp.einsum('bcln,bhcl,bclhp->bchpn', Bc, decay_states, xdt)
            chunk_decay = jnp.exp(A_cum[..., -1])

            def step(h, inp):
                s, d = inp
                return (h * d[..., None, None] + s, h)
            _, prevs = jax.lax.scan(step, jnp.zeros_like(states[:, 0]), (jnp.moveaxis(states, 1, 0), jnp.moveaxis(chunk_decay, 2, 0)))
            prevs = jnp.moveaxis(prevs, 0, 1)
            Y_off = jnp.einsum('bcln,bchpn,bhcl->bclhp', Cc, prevs, jnp.exp(A_cum))
            Y = (Y_diag + Y_off + xh * D[:, None]).reshape(Bsz, L, D_INNER)
            Y = Y * jax.nn.silu(z)
            Y = Y * jax.lax.rsqrt(jnp.mean(Y * Y, axis=-1, keepdims=True) + EPS) * norm_w
            out = Y @ W_out
            return out @ W_lin + b_lin
        return mamba2_block(x, W_in, conv_w, conv_b, dt_bias, A_log, D, norm_w, W_out, W_lin, b_lin)

    def _L1_gnn_ref(X, A, D, W_q, b_q, W_k, b_k, W_v, b_v, W_o, b_o, dist_scale):
        import jax, jax.numpy as jnp
        import numpy as np
        import math
        B, N, IN_DIM, OUT_DIM, H = (8, 512, 128, 128, 8)
        D_K = OUT_DIM // H
        b, n, _ = X.shape
        Q = (X @ W_q + b_q).reshape(b, n, H, D_K).transpose(0, 2, 1, 3)
        K = (X @ W_k + b_k).reshape(b, n, H, D_K).transpose(0, 2, 1, 3)
        V = (X @ W_v + b_v).reshape(b, n, H, D_K).transpose(0, 2, 1, 3)
        scores = jnp.einsum('bhqd,bhkd->bhqk', Q, K) / jnp.sqrt(jnp.float32(D_K))
        scores = scores - dist_scale * D[:, None, :, :]
        scores = jnp.where(A[:, None, :, :] <= 0, jnp.float32(-1000000000.0), scores)
        attn = jax.nn.softmax(scores, axis=-1)
        out = jnp.einsum('bhqk,bhkd->bhqd', attn, V)
        out = out.transpose(0, 2, 1, 3).reshape(b, n, H * D_K)
        return out @ W_o + b_o

    def _L1_ffn_ref(x, W1, b1, Wg, bg, Wd, bd):
        import jax, jax.numpy as jnp
        import numpy as np
        C = 128
        HID = 512
        E = 8
        TEMP = 1.0
        orig_shape = x.shape
        xf = x.reshape(-1, orig_shape[-1])
        H = jax.nn.gelu(xf @ W1 + b1, approximate=False)
        probs = jax.nn.softmax((H @ Wg + bg) / TEMP, axis=-1)
        assign = jnp.argmax(probs, axis=-1)
        out = jnp.zeros_like(xf)
        for e in range(Wd.shape[0]):
            y = H @ Wd[e] + bd[e]
            sel = (assign == e)[:, None]
            out = out + jnp.where(sel, probs[:, e:e + 1] * y, 0.0)
        return out.reshape(orig_shape)

    def _L2_gnn_ref(h, adj, W, a):
        import jax, jax.numpy as jnp
        import numpy as np
        ALPHA = 0.2
        NEG_INF = -9000000000000000.0
        Wh = jnp.einsum('bnd,od->bno', h, W)
        D = Wh.shape[-1]
        a1, a2 = (a[:D, 0], a[D:, 0])
        s1 = Wh @ a1
        s2 = Wh @ a2
        e = jax.nn.leaky_relu(s1[:, :, None] + s2[:, None, :], negative_slope=ALPHA)
        e = jnp.where(adj > 0, e, NEG_INF)
        attention = jax.nn.softmax(e, axis=-1)
        h_prime = jnp.einsum('bij,bjd->bid', attention, Wh)
        return h_prime

    def _L2_ffn_ref(x, sW1, sb1, sW2, sb2, sW3, sb3, eW1, eb1, eW2, eb2, eW3, eb3, gW, gb):
        import jax, jax.numpy as jnp
        import numpy as np
        B, A = (2048, 8)
        IN, OUT = (128, 128)
        SH1, SH2 = (128, 128)
        EH1, EH2 = (128, 64)
        E, TOPK = (4, 2)

        def _shared_mlp(x, W1, b1, W2, b2, W3, b3):
            h = jax.nn.relu(x @ W1 + b1)
            h = jax.nn.relu(h @ W2 + b2)
            return h @ W3 + b3

        def _experts_mlp(x, eW1, eb1, eW2, eb2, eW3, eb3):
            h = jax.nn.relu(jnp.einsum('baf,efh->ebah', x, eW1) + eb1[:, None, None, :])
            h = jax.nn.relu(jnp.einsum('ebah,ehg->ebag', h, eW2) + eb2[:, None, None, :])
            o = jnp.einsum('ebag,ego->ebao', h, eW3) + eb3[:, None, None, :]
            return jnp.moveaxis(o, 0, -1)
        all_out = _experts_mlp(x, eW1, eb1, eW2, eb2, eW3, eb3)
        shared = _shared_mlp(x, sW1, sb1, sW2, sb2, sW3, sb3)
        gates = jax.nn.softmax(x @ gW + gb, axis=-1)
        topv, topi = jax.lax.top_k(gates, TOPK)
        topw = jax.nn.softmax(topv, axis=-1)
        sel = jnp.take_along_axis(all_out, topi[:, :, None, :], axis=-1)
        gated = jnp.sum(sel * topw[:, :, None, :], axis=-1)
        return shared + gated

    def _L3_gnn_ref(h, adj, W, a):
        import jax, jax.numpy as jnp
        import numpy as np
        ALPHA = 0.2
        NEG_BIG = -9000000000000000.0
        Wh = jnp.einsum('bni,io->bno', h, W)
        Fout = W.shape[1]
        a1 = a[:Fout, 0]
        a2 = a[Fout:, 0]
        s1 = Wh @ a1
        s2 = Wh @ a2
        e = s1[:, :, None] + s2[:, None, :]
        e = jnp.where(e > 0, e, ALPHA * e)
        e = jnp.where(adj > 0, e, NEG_BIG)
        attention = jax.nn.softmax(e, axis=-1)
        h_prime = jnp.einsum('bij,bjo->bio', attention, Wh)
        return h_prime

    def _L3_ffn_ref(x, ln1_w, ln2_w, wq, wk, wv, wo, router_w, w1, w2, w3):
        import jax, jax.numpy as jnp
        import numpy as np
        B, T, C = (64, 192, 128)
        NH, NKV = (4, 2)
        HD = C // NH
        NREP = NH // NKV
        NE, TOPK = (8, 2)
        HID = int(8 / 3 * C)
        EPS_RMS = 1e-06

        def _rope_tables(t_len):
            inv_freq = 1.0 / 10000.0 ** (np.arange(0, HD, 2, dtype=np.float32) / HD)
            t = np.arange(t_len, dtype=np.float32)
            freqs = np.outer(t, inv_freq)
            emb = np.concatenate([freqs, freqs], axis=-1)
            return (jnp.asarray(np.cos(emb)), jnp.asarray(np.sin(emb)))

        def _rotate_half(x):
            h = x.shape[-1] // 2
            return jnp.concatenate([-x[..., h:], x[..., :h]], axis=-1)

        def _rmsnorm(v, w):
            return v * jax.lax.rsqrt(jnp.mean(v * v, axis=-1, keepdims=True) + EPS_RMS) * w
        Bx, Tx, Cx = x.shape
        h = _rmsnorm(x, ln1_w)
        q = (h @ wq.T).reshape(Bx, Tx, NH, HD).transpose(0, 2, 1, 3)
        k = (h @ wk.T).reshape(Bx, Tx, NKV, HD).transpose(0, 2, 1, 3)
        v = (h @ wv.T).reshape(Bx, Tx, NKV, HD).transpose(0, 2, 1, 3)
        cos, sin = _rope_tables(Tx)
        cos, sin = (cos[None, None], sin[None, None])
        q = q * cos + _rotate_half(q) * sin
        k = k * cos + _rotate_half(k) * sin
        k = jnp.repeat(k, NREP, axis=1)
        v = jnp.repeat(v, NREP, axis=1)
        scores = jnp.einsum('bhtd,bhsd->bhts', q, k) / jnp.sqrt(jnp.float32(HD))
        causal = jnp.tril(jnp.ones((Tx, Tx), dtype=bool))
        scores = jnp.where(causal[None, None], scores, jnp.float32(-1e+30))
        att = jax.nn.softmax(scores, axis=-1)
        y = jnp.einsum('bhts,bhsd->bhtd', att, v).transpose(0, 2, 1, 3).reshape(Bx, Tx, Cx)
        x = x + y @ wo.T
        flat = _rmsnorm(x, ln2_w).reshape(-1, Cx)
        probs = jax.nn.softmax(flat @ router_w.T, axis=-1)
        tp, ti = jax.lax.top_k(probs, TOPK)
        tp = tp / (jnp.sum(tp, axis=-1, keepdims=True) + 1e-09)
        weights = jnp.sum(tp[..., None] * jax.nn.one_hot(ti, NE, dtype=flat.dtype), axis=1)
        out = jnp.zeros_like(flat)
        for e in range(NE):
            hh = jax.nn.silu(flat @ w1[e].T) * (flat @ w3[e].T)
            out = out + weights[:, e:e + 1] * (hh @ w2[e].T)
        return x + out.reshape(Bx, Tx, Cx)
    x = x + _L0_gnn_ref(_layernorm(x, axis=-1), adj, L0_gnn_W, L0_gnn_a)
    x = x + _L0_ffn_ref(_layernorm(x, axis=-1), L0_ffn_W_in, L0_ffn_conv_w, L0_ffn_conv_b, L0_ffn_dt_bias, L0_ffn_A_log, L0_ffn_D, L0_ffn_norm_w, L0_ffn_W_out, L0_ffn_W_lin, L0_ffn_b_lin)
    x = x + _L1_gnn_ref(_layernorm(x, axis=-1), adj, adj, L1_gnn_W_q, L1_gnn_b_q, L1_gnn_W_k, L1_gnn_b_k, L1_gnn_W_v, L1_gnn_b_v, L1_gnn_W_o, L1_gnn_b_o, L1_gnn_dist_scale)
    x = x + _L1_ffn_ref(_layernorm(x, axis=-1), L1_ffn_W1, L1_ffn_b1, L1_ffn_Wg, L1_ffn_bg, L1_ffn_Wd, L1_ffn_bd)
    x = x + _L2_gnn_ref(_layernorm(x, axis=-1), adj, L2_gnn_W, L2_gnn_a)
    x = x + _L2_ffn_ref(_layernorm(x, axis=-1), L2_ffn_sW1, L2_ffn_sb1, L2_ffn_sW2, L2_ffn_sb2, L2_ffn_sW3, L2_ffn_sb3, L2_ffn_eW1, L2_ffn_eb1, L2_ffn_eW2, L2_ffn_eb2, L2_ffn_eW3, L2_ffn_eb3, L2_ffn_gW, L2_ffn_gb)
    x = x + _L3_gnn_ref(_layernorm(x, axis=-1), adj, L3_gnn_W, L3_gnn_a)
    x = x + _L3_ffn_ref(_layernorm(x, axis=-1), L3_ffn_ln1_w, L3_ffn_ln2_w, L3_ffn_wq, L3_ffn_wk, L3_ffn_wv, L3_ffn_wo, L3_ffn_router_w, L3_ffn_w1, L3_ffn_w2, L3_ffn_w3)
    return x

_drawn_inputs = setup_inputs


def setup_inputs(seed=0):
    import zlib

    import numpy as np

    out = dict(_drawn_inputs(seed))
    spreads = {'L0_ffn_D': (1.0, 0.2),
     'L0_ffn_norm_w': (1.0, 0.2),
     'L0_ffn_b_lin': (0.0, 0.1),
     'L1_ffn_b1': (0.0, 0.8),
     'L1_ffn_bg': (0.0, 0.661),
     'L1_ffn_bd': (0.0, 0.774),
     'L2_ffn_sb1': (0.0, 0.8),
     'L2_ffn_sb2': (0.0, 0.277),
     'L2_ffn_sb3': (0.0, 0.1),
     'L2_ffn_eb1': (0.0, 0.8),
     'L2_ffn_eb2': (0.0, 0.776),
     'L2_ffn_eb3': (0.0, 0.1),
     'L2_ffn_gb': (0.0, 0.489),
     'L3_ffn_ln1_w': (1.0, 0.6),
     'L3_ffn_ln2_w': (1.0, 0.6)}
    factors = {'L0_ffn_A_log': 7.204,
     'L1_gnn_W_q': 3.177,
     'L1_gnn_b_q': 8.0,
     'L1_gnn_W_k': 3.184,
     'L1_gnn_b_k': 8.0,
     'L1_ffn_W1': 6.408,
     'L1_ffn_Wg': 6.155,
     'L1_ffn_Wd': 8.0,
     'L2_ffn_eW1': 3.205,
     'L2_ffn_eW2': 2.711,
     'L3_gnn_a': 2.975,
     'L3_ffn_wq': 8.0,
     'L3_ffn_wk': 8.0,
     'L3_ffn_wv': 6.771,
     'L3_ffn_wo': 6.973,
     'L3_ffn_router_w': 8.0,
     'L3_ffn_w1': 8.0,
     'L3_ffn_w2': 8.0,
     'L3_ffn_w3': 8.0}
    for name, (base, spread) in spreads.items():
        noise = np.random.default_rng([zlib.crc32(name.encode()), seed]).standard_normal(out[name].shape)
        drawn = base * np.exp(spread * noise) if base else spread * noise
        out[name] = jnp.asarray(drawn.astype(out[name].dtype))
    for name, factor in factors.items():
        out[name] = (out[name] * factor).astype(out[name].dtype)
    return out
```

```python
from contextlib import ExitStack

import numpy as np
import concourse.bass as bass
from concourse import mybir
from concourse.alu_op_type import AluOpType as ALU

ACT = mybir.ActivationFunctionType
AX = mybir.AxisListType
F32 = mybir.dt.float32
BF16 = mybir.dt.bfloat16
I32 = mybir.dt.int32

N = 128
C = 128
GRAPHS = 4
NG = 2
W = GRAPHS * N
NEG = -float(2 ** 60)
PHASES = 9

HEADS1, DK1 = 8, 16
E1, HID1 = 8, 512
E2, EH2 = 4, 64
NH3, HD3 = 4, 32
E3, HID3 = 8, 341
CHUNKS3 = [(0, 128), (128, 128), (256, HID3 - 256)]
H0, P0, S0 = 4, 64, 64
EPS_LN, EPS_RMS0, EPS_RMS3 = 1e-5, 1e-5, 1e-6
SCALE3 = float(np.float32(1.0) / np.sqrt(np.float32(HD3)))


def columns(sizes):
    at, out = 0, {}
    for name, n in sizes:
        out[name] = (at, at + n)
        at += n
    return out, at


SMALL = [("ident", 128), ("upto", 128), ("after", 128), ("future", 128), ("past", 128), ("cos", 128),
         ("sin", 128), ("rank8", 8), ("rank4", 4), ("even", 1), ("odd", 1), ("minus_half", 8), ("eps", 3 * GRAPHS), ("scale3", 16)]
for _l in range(3):
    SMALL += [(f"gat{_l}_w", 128), (f"gat{_l}_wt", 128), (f"gat{_l}_a", 2)]
SMALL += [("in_xbc", 384), ("in_z", 256), ("in_dt", 4), ("conv_w", 12), ("conv_b", 3), ("dt_bias", 4),
          ("a_log", 4), ("d_chan", 2), ("norm_w", 2), ("out_t", 256), ("lin", 128), ("b_lin", 128)]
SMALL += [("q1", 128), ("k1", 128), ("v1", 128), ("o1", 128), ("bq1", 1), ("bk1", 1), ("bv1", 1),
          ("bo1", 128), ("dist", 1)]
SMALL += [("up1", HID1), ("b_up1", 4), ("gate1", 4 * E1), ("b_gate1", E1), ("b_down1", W)]
SMALL += [("s1", 128), ("s2", 128), ("s3", 128), ("sb1", 1), ("sb2", 1), ("e1", E2 * 128), ("eb1", E2),
          ("e2", E2 * EH2), ("eb2", E2), ("e3", E2 * 128), ("eb3", W), ("sb3", W), ("gate2", E2), ("b_gate2", E2)]
SMALL += [("ln1", 1), ("ln2", 1), ("q3", 128), ("q3r", 128), ("k3", 128), ("k3r", 128), ("v3", 64), ("o3", 128),
          ("router3", E3)]
AT, SMALL_COLS = columns(SMALL)
BIG3, BIG_COLS = columns([("w1", E3 * HID3), ("w3", E3 * HID3), ("w2", E3 * 3 * C)])

SIGNALS = """loaded_small loaded_x loaded_adj loaded_down1 loaded_big3 stored x_new
const_bf const_mask const_rows const_score_psum const_score const_exp const_a const_folds const_mix_psum const_mix
const_bias
ln_stats ln_moments ln_var ln_rstd xn_ready xnt_psum xnt_ready
gat_proj gat_score gat_wh gat_leak gat_max gat_exp gat_pt gat_ptc gat_inv gat_agg
ssm_conv ssm_tap ssm_dtx ssm_dta ssm_dte ssm_dtl ssm_dt ssm_da ssm_tri ssm_taps ssm_tanh ssm_silu ssm_z ssm_tz ssm_gz
ssm_xt ssm_xdt ssm_seg ssm_decay ssm_m ssm_y ssm_yg ssm_sq ssm_ms ssm_rstd ssm_yt ssm_ytc ssm_o ssm_bias
mha_adj0 mha_adj1 mha_bias mha_qkv mha_q mha_k mha_score mha_t mha_exp mha_pt mha_pta mha_ptc mha_inv mha_av mha_o
mha_ot mha_otc mha_out
one_h one_act one_logit one_sub one_exp one_gate one_gt one_gtc one_bd one_xb one_y one_gated one_sum
two_logit two_sub two_exp two_sub2 two_exp2 two_gate two_gt two_gtc two_h1 two_h1c two_h2 two_h2c two_sh two_xs
two_y two_gated two_sum
at_rms at_rope at_ropem at_qk at_v at_vc at_score at_max at_nmax at_exp at_pt at_pta at_ptc at_inv at_av at_y
at_yt at_ytc at_o at_x1 at_xadd at_sq at_ms at_rstd at_f at_ft at_ftc at_store at_logit at_sub at_sexp at_gate
big_w big_up big_silu big_hh big_y big_x""".split()


def program(nc, x_in, adj_in, small_in, down1_in, big3_in, out):
    B = x_in.shape[0]
    GROUPS = B // GRAPHS
    ITER = GROUPS // NG
    x_dram = x_in.rearrange("b n c -> n b c")
    adj_dram = adj_in.rearrange("b n c -> n b c")
    out_dram = out.rearrange("b n c -> n b c")

    ctx = ExitStack()
    with ctx:
        def sb(name, shape, dt=F32):
            return ctx.enter_context(nc.sbuf_tensor(name, shape, dt))

        sem = {name: ctx.enter_context(nc.semaphore(name)) for name in SIGNALS}

        x = sb("x", [N, B, C])
        small = sb("small", [128, SMALL_COLS])
        big = sb("big", [128, BIG_COLS])
        late = sb("late", [128, B * C])
        mask = late[:, 0:B * N // 2].bitcast(BF16).rearrange("p (b n) -> p b n", b=B)
        adj = big[:, 0:B * N].bitcast(I32)
        down1 = big[:, 0:4 * E1 * C].rearrange("p (j n) -> p j n", j=4)
        A = [sb(f"A{g}", [128, 4 * W]) for g in range(NG)]
        Bb = [sb(f"B{g}", [128, 4 * W]) for g in range(NG)]
        Cc = [sb(f"C{g}", [128, 2 * W]) for g in range(NG)]
        xn = [sb(f"xn{g}", [128, GRAPHS, C]) for g in range(NG)]
        xnt = [sb(f"xnt{g}", [128, W]) for g in range(NG)]
        PS = [[ctx.enter_context(nc.psum_tensor(f"ps{g}{k}", [128, W], F32)) for k in range(4)] for g in range(NG)]
        stats = sb("stats", [128, NG, GRAPHS, 6])
        moments = sb("moments", [128, NG, GRAPHS, 2])
        vare = sb("vare", [128, NG, GRAPHS])
        rstd = sb("rstd", [128, NG, GRAPHS])
        row = sb("row", [128, NG, 16])
        tot = sb("tot", [128, NG, 16])
        inv = sb("inv", [128, NG, 16])
        ident_bf = sb("ident_bf", [128, 128], BF16)
        future_bf = sb("future_bf", [128, 128], BF16)
        past_bf = sb("past_bf", [128, 128], BF16)
        score_w = sb("score_w", [128, 3, 2, 128])
        a_rep = sb("a_rep", [128, 6, 128])
        gsm = [sb(f"gsm{g}", [128, 14, 32]) for g in range(NG)]
        neg_a = sb("neg_a", [128, H0])
        diag_d = sb("diag_d", [128, 2, 128])
        mix = sb("mix", [128, 2, 128])
        q_fold = sb("q_fold", [128, 4])
        bv_rep = sb("bv_rep", [128, 128])
        bias_out1 = sb("bias_out1", [128, 128])
        neg_dist = sb("neg_dist", [128, 1])
        neg_row = sb("neg_row", [128, NG, 16])
        rms = sb("rms", [128, NG, 4, GRAPHS])
        nothing = sb("nothing", [128, 2 * NG])
        weights3 = sb("weights3", [128, B * E3])

        def s(name):
            a, b = AT[name]
            return small[:, a:b]

        def upto(k, i, g, steps=1, step=0):
            return i * (NG * steps) + (k * GROUPS * steps + step * NG + g + 1)

        def x_before(k, i, g):
            return i * NG + (k * GROUPS + g + 1)

        def x_phase_done(k):
            return k * GROUPS + NG

        def wait_apart(eng, name, value):
            eng.wait_ge(sem["loaded_small"], 16)
            eng.wait_ge(sem[name], value)

        block = ctx.enter_context(nc.Block())
        dve_ = nc.vector
        act_ = nc.scalar
        pe_ = nc.tensor
        pool_ = nc.gpsimd

        def fill(tensor, i, g):
            return tensor[:, bass.ds(i * W // N * NG + g * GRAPHS, GRAPHS), :]

        def ln_stats(dve, k, i, g):
            dve.wait_ge(sem["x_new"], x_before(k, i, g))
            for e in range(GRAPHS):
                ins = dve_.bn_stats(stats[:, g, e, :], xg(i, g, e))
            ins.then_inc(sem["ln_stats"], 1)

        def xg(i, g, e):
            return x[:, i * (NG * GRAPHS) + (g * GRAPHS + e), :]

        def xgroup(i, g):
            return x[:, bass.ds(i * (NG * GRAPHS) + g * GRAPHS, GRAPHS), :]

        def maskgroup(i, g):
            return mask[:, bass.ds(i * (NG * GRAPHS) + g * GRAPHS, GRAPHS), :]

        def ln_moments(dve, k, i, g):
            wait_apart(dve, "ln_stats", upto(k, i, g))
            for e in range(GRAPHS):
                ins = dve_.bn_aggr(moments[:, g, e, :], stats[:, g, e, :])
            ins.then_inc(sem["ln_moments"], 1)

        def ln_rstd(pool, k, i, g):
            pool.wait_ge(sem["ln_moments"], upto(k, i, g))
            pool_.tensor_tensor(vare[:, g, :], moments[:, g, :, 1], s("eps")[:, 0:GRAPHS], ALU.add)\
                .then_inc(sem["ln_var"], 1)
            pool.wait_ge(sem["ln_var"], upto(k, i, g))
            pool_.tensor_tensor(rstd[:, g, :], vare[:, g, :], s("minus_half")[:, 0:GRAPHS], ALU.pow)\
                .then_inc(sem["ln_rstd"], 1)

        def ln_apply(dve, k, i, g):
            dve.wait_ge(sem["ln_rstd"], upto(k, i, g))
            for e in range(GRAPHS):
                ins = dve_.tensor_scalar(xn[g][:, e, :], xg(i, g, e), moments[:, g, e, 0:1], rstd[:, g, e:e + 1],
                                         ALU.subtract, ALU.mult)
            ins.then_inc(sem["xn_ready"], 1)

        def xn_transpose(pe, k, i, g):
            pe.wait_ge(sem["xn_ready"], upto(k, i, g))
            for e in range(GRAPHS):
                ins = pe_.transpose(PS[g][0][:, e * N:(e + 1) * N], xn[g][:, e, :], s("ident"))
            ins.then_inc(sem["xnt_psum"], 1)

        def xnt_copy(act, k, i, g):
            act.wait_ge(sem["xnt_psum"], upto(k, i, g))
            act_.activation(xnt[g][:, :], PS[g][0][:, :], ACT.Copy).then_inc(sem["xnt_ready"], 1)

        def each(eng, steps, i):
            for step in steps:
                for g in range(NG):
                    step(eng, i, g)

        def gat_pe(pe, k, l):
            pe.wait_ge(sem["x_new"], x_phase_done(k))

            def project(pe, i, g):
                pe.wait_ge(sem["xnt_ready"], upto(k, i, g))
                for e in range(GRAPHS):
                    ins = pe_.matmul(PS[g][1][:, e * N:(e + 1) * N], xnt[g][:, e * N:(e + 1) * N], s(f"gat{l}_w"),
                                     start=True, stop=True)
                ins.then_inc(sem["gat_proj"], 1)

            def scores(pe, i, g):
                pe_.matmul(PS[g][2][:, :], score_w[:, l, 1, :], xnt[g][:, :], start=True, stop=False)
                for e in range(GRAPHS):
                    pe_.matmul(PS[g][2][:, e * N:(e + 1) * N], xnt[g][:, e * N:(e + 1) * N], score_w[:, l, 0, :],
                               start=False, stop=False)
                pe_.matmul(PS[g][2][:, :], ident_bf[:, :], maskgroup(i, g), start=False, stop=True)\
                    .then_inc(sem["gat_score"], 1)

            def transpose(pe, i, g):
                pe.wait_ge(sem["gat_exp"], upto(l, i, g))
                for e in range(GRAPHS):
                    ins = pe_.transpose(PS[g][0][:, e * N:(e + 1) * N], A[g][:, e * N:(e + 1) * N], s("ident"))
                ins.then_inc(sem["gat_pt"], 1)

            def aggregate(pe, i, g):
                pe.wait_ge(sem["gat_ptc"], upto(l, i, g))
                pe.wait_ge(sem["gat_wh"], upto(l, i, g))
                for e in range(GRAPHS):
                    ins = pe_.matmul(PS[g][3][:, e * N:(e + 1) * N], Bb[g][:, e * N:(e + 1) * N],
                                     Cc[g][:, e * N:(e + 1) * N], start=True, stop=True)
                ins.then_inc(sem["gat_agg"], 1)

            with pe.Fori(0, ITER) as i:
                each(pe, [lambda pe, i, g: xn_transpose(pe, k, i, g), project, scores, transpose, aggregate], i)

        def gat_act(act, k, l):
            act.wait_ge(sem["x_new"], x_phase_done(k))

            def leak(act, i, g):
                act.wait_ge(sem["gat_score"], upto(l, i, g))
                act_.activation(Cc[g][:, W:2 * W], PS[g][2][:, :], ACT.Relu, scale=-0.8).then_inc(sem["gat_leak"], 1)

            def copy_wh(act, i, g):
                act.wait_ge(sem["gat_proj"], upto(l, i, g))
                act_.activation(Cc[g][:, 0:W], PS[g][1][:, :], ACT.Copy).then_inc(sem["gat_wh"], 1)

            def exps(act, i, g):
                act.wait_ge(sem["gat_max"], upto(l, i, g))
                for e in range(GRAPHS):
                    ins = act_.activation(A[g][:, e * N:(e + 1) * N], Bb[g][:, e * N:(e + 1) * N], ACT.Exp,
                                          bias=row[:, g, e:e + 1], scale=-1.0, accum_out=tot[:, g, e:e + 1])
                ins.then_inc(sem["gat_exp"], 1)

            with act.Fori(0, ITER) as i:
                each(act, [lambda act, i, g: xnt_copy(act, k, i, g), leak, copy_wh, exps], i)

        def gat_dve(dve, k, l):
            dve.wait_ge(sem["x_new"], x_phase_done(k))

            def leaky_max(dve, i, g):
                dve.wait_ge(sem["gat_leak"], upto(l, i, g))
                dve_.memset(nothing[:, g:g + 1], 0.0)
                for e in range(GRAPHS):
                    ins = dve_.tensor_tensor_reduce(
                        out=Bb[g][:, e * N:(e + 1) * N], in0=PS[g][2][:, e * N:(e + 1) * N],
                        in1=Cc[g][:, W + e * N:W + (e + 1) * N], scale=-1.0, scalar=3.0e38, op0=ALU.add, op1=ALU.min,
                        accum_out=row[:, g, e:e + 1])
                ins.then_inc(sem["gat_max"], 1)

            def copy_pt(dve, i, g):
                dve.wait_ge(sem["gat_pt"], upto(l, i, g))
                dve_.tensor_copy(Bb[g][:, 0:W], PS[g][0][:, :]).then_inc(sem["gat_ptc"], 1)
                dve_.reciprocal(inv[:, g, 0:GRAPHS], tot[:, g, 0:GRAPHS]).then_inc(sem["gat_inv"], 1)

            def update(dve, i, g):
                dve.wait_ge(sem["gat_agg"], upto(l, i, g))
                dve.wait_ge(sem["gat_inv"], upto(l, i, g))
                for e in range(GRAPHS):
                    ins = dve_.scalar_tensor_tensor(out=xg(i, g, e), in0=PS[g][3][:, e * N:(e + 1) * N],
                                                    scalar=inv[:, g, e:e + 1], in1=xg(i, g, e),
                                                    op0=ALU.mult, op1=ALU.add)
                ins.then_inc(sem["x_new"], 1)

            with dve.Fori(0, ITER) as i:
                each(dve, [lambda d, i, g: ln_stats(d, k, i, g), lambda d, i, g: ln_moments(d, k, i, g),
                           lambda d, i, g: ln_apply(d, k, i, g), leaky_max, copy_pt, update], i)

        def ln_pool(pool, k):
            pool.wait_ge(sem["x_new"], x_phase_done(k))
            with pool.Fori(0, ITER) as i:
                for g in range(NG):
                    ln_rstd(pool, k, i, g)

        PH_SSM = 1
        tri_d = [big[:, g * 4096:g * 4096 + 2048] for g in range(NG)]
        gz = [big[:, g * 4096 + 2048:g * 4096 + 3072] for g in range(NG)]
        xdt = [big[:, g * 4096 + 3072:g * 4096 + 4096] for g in range(NG)]
        BH = GRAPHS * H0

        def ssm_pe(pe):
            pe.wait_ge(sem["x_new"], x_phase_done(PH_SSM))

            def conv_in(pe, i, g):
                pe.wait_ge(sem["xnt_ready"], upto(PH_SSM, i, g))
                for j in range(3):
                    pe_.matmul(PS[g][j][:, :], s("in_xbc")[:, j * 128:(j + 1) * 128], xnt[g][:, :], start=True, stop=True)
                for e in range(GRAPHS):
                    ins = pe_.matmul(PS[g][3][:, e * H0:(e + 1) * H0], xnt[g][:, e * N:(e + 1) * N], s("in_dt"),
                                     start=True, stop=True)
                ins.then_inc(sem["ssm_conv"], 1)

            def z_in(pe, i, g):
                pe.wait_ge(sem["ssm_taps"], upto(0, i, g, 3, 2))
                for e in range(GRAPHS):
                    ins = pe_.matmul(PS[g][e // 2][:, e % 2 * 256:e % 2 * 256 + 256], xnt[g][:, e * N:(e + 1) * N],
                                     s("in_z"), start=True, stop=True)
                ins.then_inc(sem["ssm_z"], 1)

            def x_transpose(pe, i, g):
                pe.wait_ge(sem["ssm_silu"], upto(0, i, g))
                pe.wait_ge(sem["ssm_gz"], upto(0, i, g))
                for e in range(GRAPHS):
                    for j in range(2):
                        pe_.transpose(PS[g][e // 2][:, e % 2 * 256 + j * 128:e % 2 * 256 + (j + 1) * 128],
                                      A[g][:, j * W + e * N:j * W + (e + 1) * N], s("ident"))
                for e in range(GRAPHS):
                    ins = pe_.matmul(PS[g][2][:, e * N:(e + 1) * N], Cc[g][0:S0, e * N:(e + 1) * N],
                                     Cc[g][0:S0, W + e * N:W + (e + 1) * N], start=True, stop=True)
                ins.then_inc(sem["ssm_xt"], 1)

            def seg(e):
                bank = (3, 0, 1, 3)[e]

                def step(pe, i, g):
                    if e == 0:
                        pe.wait_ge(sem["ssm_tri"], upto(0, i, g))
                    elif e == 3:
                        pe.wait_ge(sem["ssm_decay"], upto(0, i, g, 4, 0))
                    else:
                        pe.wait_ge(sem["ssm_xdt"], upto(0, i, g))
                    for h in range(H0):
                        pe_.matmul(PS[g][bank][:, h * N:(h + 1) * N],
                                   tri_d[g][:, (e * H0 + h) * N:(e * H0 + h + 1) * N], s("upto"),
                                   start=h == 0, stop=False)
                    pe_.matmul(PS[g][bank][:, :].rearrange("p (h n) -> p h n", h=H0), ident_bf[:, :],
                               past_bf[:, :].unsqueeze(1).to_broadcast([128, H0, N]), start=False, stop=True)\
                        .then_inc(sem["ssm_seg"], 1)
                return step

            def y(pe, i, g):
                pe.wait_ge(sem["ssm_m"], upto(0, i, g, 4, 3))
                for e in range(GRAPHS):
                    o = e % 2 * 256
                    for j in range(2):
                        pe_.matmul(PS[g][e // 2][:, o + j * 128:o + (j + 1) * 128], A[g][:, j * W + e * N:j * W + (e + 1) * N],
                                   diag_d[:, j, :], start=j == 0, stop=False)
                    for h in range(H0):
                        ins = pe_.matmul(PS[g][e // 2][:, o + h * P0:o + (h + 1) * P0],
                                         Bb[g][:, e * W + h * N:e * W + (h + 1) * N],
                                         xdt[g][:, e * 256 + h * P0:e * 256 + (h + 1) * P0], start=False, stop=h == H0 - 1)
                ins.then_inc(sem["ssm_y"], 1)

            def y_transpose(pe, i, g):
                pe.wait_ge(sem["ssm_yg"], upto(0, i, g))
                for e in range(GRAPHS):
                    for j in range(2):
                        ins = pe_.transpose(PS[g][2 + j][:, e * N:(e + 1) * N],
                                            Cc[g][:, e * 256 + j * 128:e * 256 + (j + 1) * 128], s("ident"))
                ins.then_inc(sem["ssm_yt"], 1)

            def mix_out(pe, i, g):
                pe.wait_ge(sem["ssm_ytc"], upto(0, i, g))
                for e in range(GRAPHS):
                    for j in range(2):
                        ins = pe_.matmul(PS[g][0][:, e * N:(e + 1) * N], Bb[g][:, j * W + e * N:j * W + (e + 1) * N],
                                         mix[:, j, :], start=j == 0, stop=j == 1)
                ins.then_inc(sem["ssm_o"], 1)

            with pe.Fori(0, ITER) as i:
                each(pe, [lambda pe, i, g: xn_transpose(pe, PH_SSM, i, g), conv_in, z_in, x_transpose,
                          seg(0), seg(1), seg(2), seg(3), y, y_transpose, mix_out], i)

        def ssm_act(act):
            act.wait_ge(sem["x_new"], x_phase_done(PH_SSM))

            def tap(act, i, g):
                act.wait_ge(sem["ssm_conv"], upto(0, i, g))
                for j in range(3):
                    ins = act_.activation(A[g][:, j * W:(j + 1) * W], PS[g][j][:, :], ACT.Identity,
                                          bias=s("conv_b")[:, j:j + 1], scale=s("conv_w")[:, j * 4 + 3:j * 4 + 4])
                ins.then_inc(sem["ssm_tap"], 1)

            def dt_exp(act, i, g):
                act.wait_ge(sem["ssm_dta"], upto(0, i, g))
                act_.activation(gsm[g][:, 2, 0:BH], gsm[g][:, 1, 0:BH], ACT.Exp).then_inc(sem["ssm_dte"], 1)

            def dt_ln(act, i, g):
                act.wait_ge(sem["ssm_dte"], upto(0, i, g))
                act_.activation(gsm[g][:, 3, 0:BH], gsm[g][:, 2, 0:BH], ACT.Ln, bias=1.0).then_inc(sem["ssm_dtl"], 1)

            def tanh_xbc(act, i, g):
                act.wait_ge(sem["ssm_taps"], upto(0, i, g, 3, 2))
                act_.activation(Bb[g][:, 0:3 * W], A[g][:, 0:3 * W], ACT.Tanh).then_inc(sem["ssm_tanh"], 1)

            def tanh_z(act, i, g):
                act.wait_ge(sem["ssm_z"], upto(0, i, g))
                for b in range(2):
                    ins = act_.activation(gz[g][:, b * W:(b + 1) * W], PS[g][b][:, :], ACT.Tanh)
                ins.then_inc(sem["ssm_tz"], 1)

            def decay(e):
                bank = (3, 0, 1, 3)[e]

                def step(act, i, g):
                    act.wait_ge(sem["ssm_seg"], i * (4 * NG) + (e * NG + g + 1))
                    if e == 0:
                        act.wait_ge(sem["ssm_silu"], upto(0, i, g))
                    act_.activation(Bb[g][:, e * W:(e + 1) * W], PS[g][bank][:, :], ACT.Exp).then_inc(sem["ssm_decay"], 1)
                return step

            def square(act, i, g):
                act.wait_ge(sem["ssm_yg"], upto(0, i, g))
                for e in range(GRAPHS):
                    ins = act_.activation(A[g][:, e * 256:(e + 1) * 256], Cc[g][:, e * 256:(e + 1) * 256], ACT.Square,
                                          scale=1.0 / 16, accum_out=tot[:, g, e:e + 1])
                ins.then_inc(sem["ssm_sq"], 1)

            def copy_yt(act, i, g):
                act.wait_ge(sem["ssm_yt"], upto(0, i, g))
                for j in range(2):
                    ins = act_.activation(Bb[g][:, j * W:(j + 1) * W], PS[g][2 + j][:, :], ACT.Copy)
                ins.then_inc(sem["ssm_ytc"], 1)

            with act.Fori(0, ITER) as i:
                each(act, [lambda act, i, g: xnt_copy(act, PH_SSM, i, g), tap, dt_exp, dt_ln, tanh_xbc, tanh_z,
                           decay(0), decay(1), decay(2), decay(3), square, copy_yt], i)

        def ssm_dve(dve):
            dve.wait_ge(sem["x_new"], x_phase_done(PH_SSM))

            def dt_x(dve, i, g):
                dve.wait_ge(sem["ssm_conv"], upto(0, i, g))
                dve_.tensor_tensor(gsm[g][:, 0, 0:BH].rearrange("p (e h) -> p e h", h=H0),
                                   PS[g][3][:, 0:BH].rearrange("p (e h) -> p e h", h=H0),
                                   s("dt_bias").unsqueeze(1).to_broadcast([128, GRAPHS, H0]), ALU.add)\
                    .then_inc(sem["ssm_dtx"], 1)

            def dt_abs(dve, i, g):
                dve.wait_ge(sem["ssm_dtx"], upto(0, i, g))
                dve_.scalar_tensor_tensor(out=gsm[g][:, 1, 0:BH], in0=gsm[g][:, 0, 0:BH], scalar=-1.0,
                                          in1=gsm[g][:, 0, 0:BH], op0=ALU.mult, op1=ALU.min)\
                    .then_inc(sem["ssm_dta"], 1)

            def dt_sum(dve, i, g):
                dve.wait_ge(sem["ssm_dtl"], upto(0, i, g))
                dve_.scalar_tensor_tensor(out=gsm[g][:, 4, 0:BH], in0=gsm[g][:, 0, 0:BH], scalar=0.0,
                                          in1=gsm[g][:, 3, 0:BH], op0=ALU.max, op1=ALU.add).then_inc(sem["ssm_dt"], 1)

            def da(dve, i, g):
                dve.wait_ge(sem["ssm_dt"], upto(0, i, g))
                dve_.tensor_tensor(gsm[g][:, 5, 0:BH].rearrange("p (e h) -> p e h", h=H0),
                                   gsm[g][:, 4, 0:BH].rearrange("p (e h) -> p e h", h=H0),
                                   neg_a[:, :].unsqueeze(1).to_broadcast([128, GRAPHS, H0]), ALU.mult)\
                    .then_inc(sem["ssm_da"], 1)

            def shifted(n):
                def step(dve, i, g):
                    if n == 1:
                        dve.wait_ge(sem["ssm_tap"], upto(0, i, g))
                    else:
                        dve.wait_ge(sem["ssm_taps"], i * (3 * NG) + ((n - 2) * NG + g + 1))
                    for j in range(3):
                        acc = A[g][:, j * W:(j + 1) * W].rearrange("p (e n) -> p e n", n=N)[:, :, n:N]
                        ins = dve_.scalar_tensor_tensor(
                            out=acc, in0=PS[g][j][:, :].rearrange("p (e n) -> p e n", n=N)[:, :, 0:N - n],
                            scalar=s("conv_w")[:, j * 4 + 3 - n:j * 4 + 4 - n], in1=acc, op0=ALU.mult, op1=ALU.add)
                    ins.then_inc(sem["ssm_taps"], 1)
                return step

            def silu(dve, i, g):
                dve.wait_ge(sem["ssm_tanh"], upto(0, i, g))
                dve_.scalar_tensor_tensor(out=A[g][:, 0:2 * W], in0=Bb[g][:, 0:2 * W], scalar=1.0, in1=A[g][:, 0:2 * W],
                                          op0=ALU.add, op1=ALU.mult)
                for j in range(2):
                    r = slice(j * S0, (j + 1) * S0)
                    ins = dve_.scalar_tensor_tensor(out=Cc[g][0:S0, j * W:(j + 1) * W], in0=Bb[g][r, 2 * W:3 * W], scalar=1.0,
                                                    in1=A[g][r, 2 * W:3 * W], op0=ALU.add, op1=ALU.mult)
                ins.then_inc(sem["ssm_silu"], 1)

            def gate_z(dve, i, g):
                dve.wait_ge(sem["ssm_tz"], upto(0, i, g))
                for b in range(2):
                    ins = dve_.scalar_tensor_tensor(out=gz[g][:, b * W:(b + 1) * W], in0=gz[g][:, b * W:(b + 1) * W],
                                                    scalar=1.0, in1=PS[g][b][:, :], op0=ALU.add, op1=ALU.mult)
                ins.then_inc(sem["ssm_gz"], 1)

            def x_dt(dve, i, g):
                dve.wait_ge(sem["ssm_xt"], upto(0, i, g))
                for b in range(2):
                    ins = dve_.tensor_tensor(
                        xdt[g][:, b * W:(b + 1) * W].rearrange("p (h c) -> p h c", c=P0),
                        PS[g][b][:, :].rearrange("p (h c) -> p h c", c=P0),
                        gsm[g][:, 4, b * 8:b * 8 + 8].unsqueeze(2).to_broadcast([128, 8, P0]), ALU.mult)
                ins.then_inc(sem["ssm_xdt"], 1)

            def m(e):
                def step(dve, i, g):
                    dve.wait_ge(sem["ssm_decay"], i * (4 * NG) + (e * NG + g + 1))
                    b = Bb[g][:, e * W:(e + 1) * W].rearrange("p (h n) -> p h n", h=H0)
                    dve_.tensor_tensor(b, b, PS[g][2][:, e * N:(e + 1) * N].unsqueeze(1).to_broadcast([128, H0, N]), ALU.mult)\
                        .then_inc(sem["ssm_m"], 1)
                return step

            def y_gate(dve, i, g):
                dve.wait_ge(sem["ssm_y"], upto(0, i, g))
                for b in range(2):
                    ins = dve_.tensor_tensor(Cc[g][:, b * W:(b + 1) * W], PS[g][b][:, :], gz[g][:, b * W:(b + 1) * W], ALU.mult)
                ins.then_inc(sem["ssm_yg"], 1)

            def update(dve, i, g):
                dve.wait_ge(sem["ssm_o"], upto(0, i, g))
                dve.wait_ge(sem["ssm_rstd"], upto(0, i, g))
                dve.wait_ge(sem["ssm_bias"], upto(0, i, g))
                for e in range(GRAPHS):
                    ins = dve_.scalar_tensor_tensor(out=xg(i, g, e), in0=PS[g][0][:, e * N:(e + 1) * N],
                                                    scalar=inv[:, g, e:e + 1], in1=xg(i, g, e),
                                                    op0=ALU.mult, op1=ALU.add)
                ins.then_inc(sem["x_new"], 1)

            with dve.Fori(0, ITER) as i:
                each(dve, [lambda d, i, g: ln_stats(d, PH_SSM, i, g), lambda d, i, g: ln_moments(d, PH_SSM, i, g),
                           lambda d, i, g: ln_apply(d, PH_SSM, i, g), dt_x, dt_abs, shifted(1), dt_sum, da, shifted(2),
                           shifted(3), silu, gate_z, x_dt, m(0), m(1), m(2), m(3), y_gate, update], i)

        def ssm_pool(pool):
            pool.wait_ge(sem["x_new"], x_phase_done(PH_SSM))

            def bias(pool, i, g):
                pool.wait_ge(sem["xn_ready"], upto(PH_SSM, i, g))
                pool_.tensor_tensor(xgroup(i, g), xgroup(i, g),
                                    s("b_lin").unsqueeze(1).to_broadcast([128, GRAPHS, C]), ALU.add)\
                    .then_inc(sem["ssm_bias"], 1)

            def tri(pool, i, g):
                pool.wait_ge(sem["ssm_da"], upto(0, i, g))
                for e in range(GRAPHS):
                    ins = pool_.tensor_tensor(
                        tri_d[g][:, e * W:(e + 1) * W].rearrange("p (h n) -> p h n", h=H0),
                        s("after").unsqueeze(1).to_broadcast([128, H0, N]),
                        gsm[g][:, 5, e * H0:(e + 1) * H0].unsqueeze(2).to_broadcast([128, H0, N]), ALU.mult)
                ins.then_inc(sem["ssm_tri"], 1)

            def rms_y(pool, i, g):
                pool.wait_ge(sem["ssm_sq"], upto(0, i, g))
                pool_.tensor_tensor(vare[:, g, :], tot[:, g, 0:GRAPHS], s("eps")[:, 0:GRAPHS], ALU.add)\
                    .then_inc(sem["ssm_ms"], 1)
                pool.wait_ge(sem["ssm_ms"], upto(0, i, g))
                pool_.tensor_tensor(inv[:, g, 0:GRAPHS], vare[:, g, :], s("minus_half")[:, 0:GRAPHS], ALU.pow)\
                    .then_inc(sem["ssm_rstd"], 1)

            with pool.Fori(0, ITER) as i:
                each(pool, [lambda p, i, g: ln_rstd(p, PH_SSM, i, g), bias, tri, rms_y], i)

        PH_MHA = 2
        adj_g = [Cc[g][:, W:2 * W].bitcast(I32) for g in range(NG)]
        bias1 = [Cc[g][:, W:2 * W] for g in range(NG)]
        q_odd = [big[:, 4096 + g * 1024:4096 + g * 1024 + 512] for g in range(NG)]
        o_cat = [big[:, 4096 + g * 1024 + 512:4096 + (g + 1) * 1024] for g in range(NG)]
        SLOTS = [(j, e, p) for j in range(4) for e in range(2) for p in range(2)]

        def slot(t, n):
            return t[:, n * N:(n + 1) * N]

        def mha_sp(sp):
            with sp.Fori(0, ITER) as i:
                for g in range(NG):
                    sp.wait_ge(sem["x_new"], x_before(PH_MHA, i, g))
                    sp.dma_start(adj_g[g].rearrange("p (e n) -> p e n", n=N),
                                 adj_dram[:, bass.ds(i * (NG * GRAPHS) + g * GRAPHS, GRAPHS), :])\
                        .then_inc(sem[f"mha_adj{g}"], 16)

        def mha_pe(pe):
            pe.wait_ge(sem["x_new"], x_phase_done(PH_MHA))

            def qkv(pe, i, g):
                pe.wait_ge(sem["xnt_ready"], upto(PH_MHA, i, g))
                pe_.matmul(PS[g][1][:, :], s("q1"), xnt[g][:, :], start=True, stop=True)
                pe_.matmul(PS[g][2][:, :], s("k1"), xnt[g][:, :], start=True, stop=True)
                for e in range(GRAPHS):
                    ins = pe_.matmul(slot(PS[g][3], e), slot(xnt[g], e), s("v1"), start=True, stop=True)
                ins.then_inc(sem["mha_qkv"], 1)

            def score(hf):
                def step(pe, i, g):
                    if hf == 0:
                        pe.wait_ge(sem["mha_q"], upto(0, i, g))
                        pe.wait_ge(sem["mha_k"], upto(0, i, g))
                    else:
                        pe.wait_ge(sem["mha_o"], i * (2 * NG) + (g + 1))
                    for e in range(2):
                        for p in range(2):
                            for j in range(4):
                                q = (xn[g][:, :, :].rearrange("p e n -> p (e n)"), q_odd[g])[p]
                                r = slice(32 * j, 32 * j + 32)
                                ins = pe_.matmul(slot(PS[g][j], e * 2 + p), slot(q[r, :], 2 * hf + e),
                                                 slot(xnt[g][r, :], 2 * hf + e), start=True, stop=True)
                    ins.then_inc(sem["mha_score"], 1)
                return step

            def transpose(hf):
                def step(pe, i, g):
                    pe.wait_ge(sem["mha_exp"], i * (2 * NG) + (hf * NG + g + 1))
                    for n, (j, e, p) in enumerate(SLOTS):
                        ins = pe_.transpose(slot(PS[g][j], e * 2 + p), slot(A[g], n), s("ident"))
                    ins.then_inc(sem["mha_pt"], 1)
                return step

            def attend(hf):
                def step(pe, i, g):
                    pe.wait_ge(sem["mha_pta"], i * (2 * NG) + (hf * NG + g + 1))
                    pe.wait_ge(sem["mha_ptc"], i * (2 * NG) + (hf * NG + g + 1))
                    for n, (j, e, p) in enumerate(SLOTS):
                        h = 2 * j + p
                        ins = pe_.matmul(PS[g][0][:, e * N + h * DK1:e * N + (h + 1) * DK1], slot(Bb[g], n),
                                         Cc[g][:, (2 * hf + e) * N + h * DK1:(2 * hf + e) * N + (h + 1) * DK1],
                                         start=True, stop=True)
                    ins.then_inc(sem["mha_av"], 1)
                return step

            def o_transpose(pe, i, g):
                pe.wait_ge(sem["mha_o"], i * (2 * NG) + (NG + g + 1))
                for e in range(GRAPHS):
                    ins = pe_.transpose(slot(PS[g][1], e), slot(o_cat[g], e), s("ident"))
                ins.then_inc(sem["mha_ot"], 1)

            def out_proj(pe, i, g):
                pe.wait_ge(sem["mha_otc"], upto(0, i, g))
                pe_.matmul(PS[g][2][:, :].rearrange("p (e n) -> p e n", n=N), s("ident"),
                           bias_out1[:, :].unsqueeze(1).to_broadcast([128, GRAPHS, C]), start=True, stop=False)
                for e in range(GRAPHS):
                    ins = pe_.matmul(slot(PS[g][2], e), slot(A[g], e), s("o1"), start=False, stop=e == GRAPHS - 1)
                ins.then_inc(sem["mha_out"], 1)

            with pe.Fori(0, ITER) as i:
                each(pe, [lambda pe, i, g: xn_transpose(pe, PH_MHA, i, g), qkv, score(0), transpose(0), attend(0),
                          score(1), transpose(1), attend(1), o_transpose, out_proj], i)

        def mha_act(act):
            act.wait_ge(sem["x_new"], x_phase_done(PH_MHA))

            def q_out(act, i, g):
                act.wait_ge(sem["mha_qkv"], upto(0, i, g))
                act_.activation(xn[g][:, :, :].rearrange("p e n -> p (e n)"), PS[g][1][:, :], ACT.Identity,
                                bias=q_fold[:, 1:2], scale=q_fold[:, 0:1])
                act_.activation(q_odd[g], PS[g][1][:, :], ACT.Identity, bias=q_fold[:, 3:4], scale=q_fold[:, 2:3])
                act_.activation(Cc[g][:, 0:W], PS[g][3][:, :], ACT.Copy).then_inc(sem["mha_q"], 1)

            def exps(hf):
                def step(act, i, g):
                    act.wait_ge(sem["mha_t"], i * (2 * NG) + (hf * NG + g + 1))
                    for n in range(16):
                        ins = act_.activation(slot(A[g], n), slot(A[g], n), ACT.Exp, bias=row[:, g, n:n + 1], scale=-1.0,
                                              accum_out=tot[:, g, n:n + 1])
                    ins.then_inc(sem["mha_exp"], 1)
                return step

            def copy_pt(hf):
                def step(act, i, g):
                    act.wait_ge(sem["mha_pt"], i * (2 * NG) + (hf * NG + g + 1))
                    for j in range(2):
                        ins = act_.activation(Bb[g][:, j * W:(j + 1) * W], PS[g][j][:, :], ACT.Copy)
                    ins.then_inc(sem["mha_pta"], 1)
                return step

            def copy_ot(act, i, g):
                act.wait_ge(sem["mha_ot"], upto(0, i, g))
                act_.activation(A[g][:, 0:W], PS[g][1][:, :], ACT.Copy).then_inc(sem["mha_otc"], 1)

            with act.Fori(0, ITER) as i:
                each(act, [lambda act, i, g: xnt_copy(act, PH_MHA, i, g), q_out, exps(0), copy_pt(0),
                           exps(1), copy_pt(1), copy_ot], i)

        def mha_dve(dve):
            dve.wait_ge(sem["x_new"], x_phase_done(PH_MHA))

            def bias(dve, i, g):
                dve.wait_ge(sem[f"mha_adj{g}"], i * 16 + 16)
                dve_.scalar_tensor_tensor(out=bias1[g].rearrange("p (e n) -> p e n", n=N),
                                          in0=adj_g[g].rearrange("p (e n) -> p e n", n=N),
                                          scalar=neg_dist[:, 0:1], in1=maskgroup(i, g), op0=ALU.mult, op1=ALU.add)\
                    .then_inc(sem["mha_bias"], 1)

            def k_out(dve, i, g):
                dve.wait_ge(sem["mha_qkv"], upto(0, i, g))
                dve_.tensor_scalar(xnt[g][:, :], PS[g][2][:, :], s("bk1"), None, ALU.add).then_inc(sem["mha_k"], 1)

            def masked_max(hf):
                def step(dve, i, g):
                    if hf == 0:
                        dve.wait_ge(sem["mha_bias"], upto(0, i, g))
                    dve.wait_ge(sem["mha_score"], i * (2 * NG) + (hf * NG + g + 1))
                    dve_.memset(nothing[:, hf * NG + g:hf * NG + g + 1], 0.0)
                    for n, (j, e, p) in enumerate(SLOTS):
                        ins = dve_.tensor_tensor_reduce(
                            out=slot(A[g], n), in0=slot(PS[g][j], e * 2 + p), in1=slot(bias1[g], 2 * hf + e), scale=-1.0,
                            scalar=3.0e38, op0=ALU.add, op1=ALU.min, accum_out=row[:, g, n:n + 1])
                    ins.then_inc(sem["mha_t"], 1)
                return step

            def copy_pt(hf):
                def step(dve, i, g):
                    dve.wait_ge(sem["mha_pt"], i * (2 * NG) + (hf * NG + g + 1))
                    for j in range(2, 4):
                        ins = dve_.tensor_copy(Bb[g][:, j * W:(j + 1) * W], PS[g][j][:, :])
                    ins.then_inc(sem["mha_ptc"], 1)
                    dve_.reciprocal(inv[:, g, :], tot[:, g, :]).then_inc(sem["mha_inv"], 1)
                return step

            def normalise(hf):
                def step(dve, i, g):
                    dve.wait_ge(sem["mha_av"], i * (2 * NG) + (hf * NG + g + 1))
                    dve.wait_ge(sem["mha_inv"], i * (2 * NG) + (hf * NG + g + 1))
                    for e in range(2):
                        r = inv[:, g, :].rearrange("p (j e k) -> p j e k", j=4, e=2)[:, :, e, :]
                        ins = dve_.tensor_tensor(
                            slot(o_cat[g], 2 * hf + e).rearrange("p (j k d) -> p j k d", j=4, k=2),
                            slot(PS[g][0], e).rearrange("p (j k d) -> p j k d", j=4, k=2),
                            r.unsqueeze(3).to_broadcast([128, 4, 2, DK1]), ALU.mult)
                    ins.then_inc(sem["mha_o"], 1)
                return step

            def update(dve, i, g):
                dve.wait_ge(sem["mha_out"], upto(0, i, g))
                dve_.tensor_tensor(xgroup(i, g), PS[g][2][:, :].rearrange("p (e n) -> p e n", n=N), xgroup(i, g), ALU.add)\
                    .then_inc(sem["x_new"], 1)

            with dve.Fori(0, ITER) as i:
                each(dve, [lambda d, i, g: ln_stats(d, PH_MHA, i, g), lambda d, i, g: ln_moments(d, PH_MHA, i, g),
                           lambda d, i, g: ln_apply(d, PH_MHA, i, g), bias, k_out, masked_max(0), copy_pt(0), normalise(0),
                           masked_max(1), copy_pt(1), normalise(1), update], i)

        def v3(a, e):
            return a.rearrange("p (g e) -> p g e", e=e)

        def per_graph(a, e):
            return a.unsqueeze(2).to_broadcast([128, GRAPHS, e])

        def gate_chain(dve, name, ops):
            stages = []
            for n, (op, also) in enumerate(ops):
                def step(dve, i, g, n=n, op=op, also=also):
                    if n:
                        dve.wait_ge(sem[name], i * (NG * len(ops)) + ((n - 1) * NG + g + 1))
                    for other, k in also:
                        dve.wait_ge(sem[other], upto(k, i, g))
                    op(i, g).then_inc(sem[name], 1)
                stages.append(step)
            return stages

        def gate_at(count, i, g, n):
            return i * (NG * count) + (n * NG + g + 1)

        def softmax_ops(logits, bias, e):
            z = slice(0, GRAPHS * e)
            ops = []
            if bias is not None:
                ops.append(lambda i, g: dve_.tensor_tensor(v3(gsm[g][:, 0, z], e), v3(logits(g), e),
                                                           s(bias).unsqueeze(1).to_broadcast([128, GRAPHS, e]), ALU.add))
            else:
                ops.append(lambda i, g: dve_.tensor_copy(gsm[g][:, 0, z], logits(g)))
            ops.append(lambda i, g: dve_.tensor_reduce(gsm[g][:, 1, 0:GRAPHS], v3(gsm[g][:, 0, z], e), AX.X, ALU.max))
            ops.append(lambda i, g: dve_.tensor_tensor(v3(gsm[g][:, 2, z], e), v3(gsm[g][:, 0, z], e),
                                                       per_graph(gsm[g][:, 1, 0:GRAPHS], e), ALU.subtract))
            return ops

        def first_of_max_ops(src, top, eq, cand, best, sel, rank, e):
            z = slice(0, GRAPHS * e)
            return [
                lambda i, g: dve_.tensor_reduce(gsm[g][:, top, 0:GRAPHS], v3(gsm[g][:, src, z], e), AX.X, ALU.max),
                lambda i, g: dve_.tensor_tensor(v3(gsm[g][:, eq, z], e), v3(gsm[g][:, src, z], e),
                                                per_graph(gsm[g][:, top, 0:GRAPHS], e), ALU.is_equal),
                lambda i, g: dve_.tensor_tensor(v3(gsm[g][:, cand, z], e), v3(gsm[g][:, eq, z], e),
                                                s(rank).unsqueeze(1).to_broadcast([128, GRAPHS, e]), ALU.mult),
                lambda i, g: dve_.tensor_reduce(gsm[g][:, best, 0:GRAPHS], v3(gsm[g][:, cand, z], e), AX.X, ALU.max),
                lambda i, g: dve_.tensor_tensor(v3(gsm[g][:, sel, z], e), v3(gsm[g][:, cand, z], e),
                                                per_graph(gsm[g][:, best, 0:GRAPHS], e), ALU.is_equal),
            ]

        def probability_ops(e):
            z = slice(0, GRAPHS * e)
            return [
                lambda i, g: dve_.tensor_reduce(gsm[g][:, 5, 0:GRAPHS], v3(gsm[g][:, 3, z], e), AX.X, ALU.add),
                lambda i, g: dve_.reciprocal(gsm[g][:, 6, 0:GRAPHS], gsm[g][:, 5, 0:GRAPHS]),
                lambda i, g: dve_.tensor_tensor(v3(gsm[g][:, 4, z], e), v3(gsm[g][:, 3, z], e),
                                                per_graph(gsm[g][:, 6, 0:GRAPHS], e), ALU.mult),
            ]

        def rest_op(e):
            z = slice(0, GRAPHS * e)
            return [lambda i, g: dve_.scalar_tensor_tensor(out=gsm[g][:, 7, z], in0=gsm[g][:, 8, z], scalar=-2.0,
                                                           in1=gsm[g][:, 4, z], op0=ALU.mult, op1=ALU.add)]

        PH_ONE = 3
        GE1 = GRAPHS * E1
        one_ops = [[op, []] for op in softmax_ops(lambda g: PS[g][0][:, 0:GE1], "b_gate1", E1)]
        one_ops[0][1] = [("one_logit", 0)]
        ONE_SUB = len(one_ops) - 1
        one_ops += [[op, []] for op in first_of_max_ops(0, 7, 8, 9, 10, 11, "rank8", E1)]
        one_ops += [[op, []] for op in probability_ops(E1)[0:2]]
        one_ops[-2][1] = [("one_exp", 0)]
        one_ops += [[lambda i, g: dve_.tensor_tensor(v3(gsm[g][:, 12, 0:GE1], E1), v3(gsm[g][:, 11, 0:GE1], E1),
                                                     per_graph(gsm[g][:, 6, 0:GRAPHS], E1), ALU.mult), []]]
        ONE_N = len(one_ops)

        def one_pe(pe):
            pe.wait_ge(sem["x_new"], x_phase_done(PH_ONE))
            pe.wait_ge(sem["loaded_down1"], 16)

            def up(pe, i, g):
                pe.wait_ge(sem["xnt_ready"], upto(PH_ONE, i, g))
                for j in range(4):
                    ins = pe_.matmul(PS[g][j][:, :], s("up1")[:, j * 128:(j + 1) * 128], xnt[g][:, :], start=True, stop=True)
                ins.then_inc(sem["one_h"], 1)

            def logit(pe, i, g):
                pe.wait_ge(sem["one_act"], upto(0, i, g))
                for e in range(GRAPHS):
                    for j in range(4):
                        ins = pe_.matmul(PS[g][0][:, e * E1:(e + 1) * E1], A[g][:, j * W + e * N:j * W + (e + 1) * N],
                                         s("gate1")[:, j * E1:(j + 1) * E1], start=j == 0, stop=j == 3)
                ins.then_inc(sem["one_logit"], 1)

            def gate_t(pe, i, g):
                pe.wait_ge(sem["one_gate"], gate_at(ONE_N, i, g, ONE_N - 1))
                pe_.transpose(PS[g][1][0:GE1, 0:N], gsm[g][:, 12, 0:GE1], s("ident")).then_inc(sem["one_gt"], 1)

            def down_bias(pe, i, g):
                pe.wait_ge(sem["one_gtc"], upto(0, i, g))
                pe_.matmul(PS[g][0][:, :], Cc[g][0:GE1, 0:N], s("b_down1")[0:GE1, :], start=True, stop=True)\
                    .then_inc(sem["one_bd"], 1)

            def down(e):
                def step(pe, i, g):
                    if e == 1:
                        pe.wait_ge(sem["one_xb"], upto(0, i, g))
                    if e >= 2:
                        pe.wait_ge(sem["one_gated"], i * (4 * NG) + ((e - 2) * NG + g + 1))
                    for b in range(2):
                        for j in range(4):
                            ins = pe_.matmul(PS[g][(2, 0)[e % 2] + b][:, :], A[g][:, j * W + e * N:j * W + (e + 1) * N],
                                             down1[:, j, b * W:(b + 1) * W], start=j == 0, stop=j == 3)
                    ins.then_inc(sem["one_y"], 1)
                return step

            with pe.Fori(0, ITER) as i:
                each(pe, [lambda pe, i, g: xn_transpose(pe, PH_ONE, i, g), up, logit, down(0), gate_t, down_bias,
                          down(1), down(2), down(3)], i)

        def one_act(act):
            act.wait_ge(sem["x_new"], x_phase_done(PH_ONE))

            def gelu(act, i, g):
                act.wait_ge(sem["one_h"], upto(0, i, g))
                for j in range(4):
                    ins = act_.activation(A[g][:, j * W:(j + 1) * W], PS[g][j][:, :], ACT.Gelu, bias=s("b_up1")[:, j:j + 1])
                ins.then_inc(sem["one_act"], 1)

            def gate_exp(act, i, g):
                act.wait_ge(sem["one_gate"], gate_at(ONE_N, i, g, ONE_SUB))
                act_.activation(gsm[g][:, 3, 0:GE1], gsm[g][:, 2, 0:GE1], ACT.Exp).then_inc(sem["one_exp"], 1)

            def copy_gt(act, i, g):
                act.wait_ge(sem["one_gt"], upto(0, i, g))
                act_.activation(Cc[g][0:GE1, 0:N], PS[g][1][0:GE1, 0:N], ACT.Copy).then_inc(sem["one_gtc"], 1)

            with act.Fori(0, ITER) as i:
                each(act, [lambda act, i, g: xnt_copy(act, PH_ONE, i, g), gelu, gate_exp, copy_gt], i)

        def gated(dve, y_name, done_name, g, e, i, banks, gate, buf, free):
            if free:
                dve.wait_ge(sem[free[0]], free[1])
            dve.wait_ge(sem[y_name], i * (4 * NG) + (e * NG + g + 1))
            for b, bank in enumerate(banks):
                ins = dve_.tensor_tensor(buf[:, b * W:(b + 1) * W].rearrange("p (x n) -> p x n", n=N),
                                         PS[g][bank][:, :].rearrange("p (x n) -> p x n", n=N),
                                         gate[:, b * 4:b * 4 + 4].unsqueeze(2).to_broadcast([128, 4, N]), ALU.mult)
            ins.then_inc(sem[done_name], 1)

        def one_dve(dve):
            dve.wait_ge(sem["x_new"], x_phase_done(PH_ONE))

            def add_bias(dve, i, g):
                dve.wait_ge(sem["one_bd"], upto(0, i, g))
                dve_.tensor_tensor(xgroup(i, g), PS[g][0][:, :].rearrange("p (e n) -> p e n", n=N), xgroup(i, g), ALU.add)\
                    .then_inc(sem["one_xb"], 1)

            def gate_y(e):
                def step(dve, i, g):
                    free = ("one_sum", i * (16 * NG) + (((e - 2) * NG + g) * 4 + 4)) if e >= 2 else None
                    gated(dve, "one_y", "one_gated", g, e, i, ((2, 3), (0, 1))[e % 2],
                          gsm[g][:, 12, e * E1:(e + 1) * E1], Bb[g][:, e % 2 * 1024:e % 2 * 1024 + 1024], free)
                return step

            with dve.Fori(0, ITER) as i:
                each(dve, [lambda d, i, g: ln_stats(d, PH_ONE, i, g), lambda d, i, g: ln_moments(d, PH_ONE, i, g),
                           lambda d, i, g: ln_apply(d, PH_ONE, i, g)] + gate_chain(dve, "one_gate", one_ops)
                     + [add_bias, gate_y(0), gate_y(1), gate_y(2), gate_y(3)], i)

        def one_pool(pool):
            pool.wait_ge(sem["x_new"], x_phase_done(PH_ONE))

            def add_up(e):
                def step(pool, i, g):
                    at = i * (16 * NG) + (e * NG + g) * 4
                    t = Bb[g][:, e % 2 * 1024:e % 2 * 1024 + 1024]
                    if e == 0:
                        pool.wait_ge(sem["one_xb"], upto(0, i, g))
                    pool.wait_ge(sem["one_gated"], i * (4 * NG) + (e * NG + g + 1))
                    for n, half in enumerate((512, 256, 128)):
                        pool_.tensor_tensor(t[:, 0:half], t[:, 0:half], t[:, half:2 * half], ALU.add)\
                            .then_inc(sem["one_sum"], 1)
                        pool.wait_ge(sem["one_sum"], at + (n + 1))
                    ins = pool_.tensor_tensor(xg(i, g, e), xg(i, g, e), t[:, 0:C], ALU.add)
                    ins.then_inc(sem["one_sum"], 1)
                    if e == GRAPHS - 1:
                        pool.wait_ge(sem["one_sum"], at + 4)
                        pool.sem_inc(sem["x_new"], 1)
                return step

            with pool.Fori(0, ITER) as i:
                each(pool, [lambda p, i, g: ln_rstd(p, PH_ONE, i, g), add_up(0), add_up(1), add_up(2), add_up(3)], i)

        PH_TWO = 5
        GE2 = GRAPHS * E2
        two_ops = [[op, []] for op in softmax_ops(lambda g: PS[g][0][:, 0:GE2], "b_gate2", E2)]
        two_ops[0][1] = [("two_logit", 0)]
        TWO_SUB = len(two_ops) - 1
        two_ops += [[op, []] for op in probability_ops(E2)]
        two_ops[TWO_SUB + 1][1] = [("two_exp", 0)]
        two_ops += [[op, []] for op in first_of_max_ops(4, 9, 10, 11, 12, 8, "rank4", E2) + rest_op(E2)
                    + first_of_max_ops(7, 13, 10, 11, 12, 2, "rank4", E2)]
        two_ops += [[lambda i, g: dve_.tensor_tensor(gsm[g][:, 5, 0:4], gsm[g][:, 13, 0:4], gsm[g][:, 9, 0:4], ALU.subtract), []]]
        TWO_SUB2 = len(two_ops) - 1
        two_ops += [
            [lambda i, g: dve_.tensor_scalar(gsm[g][:, 10, 0:4], gsm[g][:, 6, 0:4], 1.0, None, ALU.add), [("two_exp2", 0)]],
            [lambda i, g: dve_.reciprocal(gsm[g][:, 11, 0:4], gsm[g][:, 10, 0:4]), []],
            [lambda i, g: dve_.tensor_tensor(gsm[g][:, 12, 0:4], gsm[g][:, 11, 0:4], gsm[g][:, 6, 0:4], ALU.mult), []],
            [lambda i, g: dve_.tensor_tensor(v3(gsm[g][:, 0, 0:GE2], E2), v3(gsm[g][:, 8, 0:GE2], E2),
                                             per_graph(gsm[g][:, 11, 0:4], E2), ALU.mult), []],
            [lambda i, g: dve_.tensor_tensor(v3(gsm[g][:, 1, 0:GE2], E2), v3(gsm[g][:, 2, 0:GE2], E2),
                                             per_graph(gsm[g][:, 12, 0:4], E2), ALU.mult), []],
            [lambda i, g: dve_.tensor_tensor(gsm[g][:, 3, 0:GE2], gsm[g][:, 0, 0:GE2], gsm[g][:, 1, 0:GE2], ALU.add), []],
        ]
        TWO_N = len(two_ops)
        NETS = range(1 + E2)

        def h1_bank(q):
            return 1 + 2 * (q % 2)

        def net_at(i, g, q):
            return i * (5 * NG) + (q * NG + g + 1)

        def two_pe(pe):
            pe.wait_ge(sem["x_new"], x_phase_done(PH_TWO))

            def logit(pe, i, g):
                pe.wait_ge(sem["xnt_ready"], upto(PH_TWO, i, g))
                for e in range(GRAPHS):
                    ins = pe_.matmul(PS[g][0][:, e * E2:(e + 1) * E2], slot(xnt[g], e), s("gate2"), start=True, stop=True)
                ins.then_inc(sem["two_logit"], 1)

            def hidden1(q):
                def step(pe, i, g):
                    if q >= 2:
                        pe.wait_ge(sem["two_h1c"], net_at(i, g, q - 2))
                    w = s("s1") if q == 0 else s("e1")[:, (q - 1) * 128:q * 128]
                    pe_.matmul(PS[g][h1_bank(q)][:, :], w, xnt[g][:, :], start=True, stop=True).then_inc(sem["two_h1"], 1)
                return step

            def hidden2(q):
                def step(pe, i, g):
                    pe.wait_ge(sem["two_h1c"], net_at(i, g, q))
                    if q:
                        pe.wait_ge(sem["two_h2c"], net_at(i, g, q - 1))
                    w = s("s2") if q == 0 else s("e2")[:, (q - 1) * EH2:q * EH2]
                    m = 128 if q == 0 else EH2
                    pe_.matmul(PS[g][2][0:m, :], w, A[g][:, q % 2 * W:(q % 2 + 1) * W], start=True, stop=True)\
                        .then_inc(sem["two_h2"], 1)
                return step

            def gate_t(pe, i, g):
                pe.wait_ge(sem["two_gate"], gate_at(TWO_N, i, g, TWO_N - 1))
                pe_.transpose(PS[g][0][0:GE2, 0:N], gsm[g][:, 3, 0:GE2], s("ident")).then_inc(sem["two_gt"], 1)

            def shared_out(pe, i, g):
                pe.wait_ge(sem["two_gtc"], upto(0, i, g))
                pe.wait_ge(sem["two_h2c"], net_at(i, g, 0))
                pe_.matmul(PS[g][0][:, :], Cc[g][0:GE2, W:W + N], s("eb3")[0:GE2, :], start=True, stop=False)
                for e in range(GRAPHS):
                    ins = pe_.matmul(slot(PS[g][0], e), Cc[g][:, e * N:(e + 1) * N], s("s3"), start=False, stop=e == GRAPHS - 1)
                ins.then_inc(sem["two_sh"], 1)

            def expert_out(e):
                bank = (1, 2, 3, 1)[e]

                def step(pe, i, g):
                    if e == 0:
                        pe.wait_ge(sem["two_h2c"], net_at(i, g, E2))
                    if e == 3:
                        pe.wait_ge(sem["two_gated"], i * (4 * NG) + (g + 1))
                    for q in range(E2):
                        ins = pe_.matmul(slot(PS[g][bank], q), Bb[g][0:EH2, q * W + e * N:q * W + (e + 1) * N],
                                         s("e3")[0:EH2, q * 128:(q + 1) * 128], start=True, stop=True)
                    ins.then_inc(sem["two_y"], 1)
                return step

            with pe.Fori(0, ITER) as i:
                each(pe, [lambda pe, i, g: xn_transpose(pe, PH_TWO, i, g), logit, hidden1(0), hidden1(1), hidden2(0),
                          hidden1(2), hidden2(1), hidden1(3), hidden2(2), hidden1(4), hidden2(3), hidden2(4),
                          gate_t, shared_out, expert_out(0), expert_out(1), expert_out(2), expert_out(3)], i)

        def two_act(act):
            act.wait_ge(sem["x_new"], x_phase_done(PH_TWO))

            def relu1(q):
                def step(act, i, g):
                    act.wait_ge(sem["two_h1"], net_at(i, g, q))
                    if q >= 2:
                        act.wait_ge(sem["two_h2"], net_at(i, g, q - 2))
                    b = s("sb1") if q == 0 else s("eb1")[:, q - 1:q]
                    act_.activation(A[g][:, q % 2 * W:(q % 2 + 1) * W], PS[g][h1_bank(q)][:, :], ACT.Relu, bias=b)\
                        .then_inc(sem["two_h1c"], 1)
                return step

            def gate_exp(act, i, g):
                act.wait_ge(sem["two_gate"], gate_at(TWO_N, i, g, TWO_SUB))
                act_.activation(gsm[g][:, 3, 0:GE2], gsm[g][:, 2, 0:GE2], ACT.Exp).then_inc(sem["two_exp"], 1)

            def gate_exp2(act, i, g):
                act.wait_ge(sem["two_gate"], gate_at(TWO_N, i, g, TWO_SUB2))
                act_.activation(gsm[g][:, 6, 0:4], gsm[g][:, 5, 0:4], ACT.Exp).then_inc(sem["two_exp2"], 1)

            def copy_gt(act, i, g):
                act.wait_ge(sem["two_gt"], upto(0, i, g))
                act_.activation(Cc[g][0:GE2, W:W + N], PS[g][0][0:GE2, 0:N], ACT.Copy).then_inc(sem["two_gtc"], 1)

            with act.Fori(0, ITER) as i:
                each(act, [lambda act, i, g: xnt_copy(act, PH_TWO, i, g), relu1(0), relu1(1), gate_exp, relu1(2), relu1(3),
                           relu1(4), gate_exp2, copy_gt], i)

        def two_dve(dve):
            dve.wait_ge(sem["x_new"], x_phase_done(PH_TWO))

            def relu2(q):
                def step(dve, i, g):
                    dve.wait_ge(sem["two_h2"], net_at(i, g, q))
                    m = 128 if q == 0 else EH2
                    b = s("sb2") if q == 0 else s("eb2")[0:m, q - 1:q]
                    o = Cc[g][:, 0:W] if q == 0 else Bb[g][0:m, (q - 1) * W:q * W]
                    dve_.tensor_scalar(o, PS[g][2][0:m, :], b, 0.0, ALU.add, ALU.max).then_inc(sem["two_h2c"], 1)
                return step

            def add_shared(dve, i, g):
                dve.wait_ge(sem["two_sh"], upto(0, i, g))
                dve_.tensor_tensor(xgroup(i, g), PS[g][0][:, :].rearrange("p (e n) -> p e n", n=N), xgroup(i, g), ALU.add)\
                    .then_inc(sem["two_xs"], 1)

            def gate_y(e):
                def step(dve, i, g):
                    gated(dve, "two_y", "two_gated", g, e, i, ((1, 2, 3, 1)[e],), gsm[g][:, 3, e * E2:(e + 1) * E2],
                          A[g][:, e * W:(e + 1) * W], None)
                return step

            chain = gate_chain(dve, "two_gate", two_ops)
            steps = [lambda d, i, g: ln_stats(d, PH_TWO, i, g), lambda d, i, g: ln_moments(d, PH_TWO, i, g),
                     lambda d, i, g: ln_apply(d, PH_TWO, i, g)] + chain[0:TWO_SUB + 1] + [relu2(0)]
            rest = chain[TWO_SUB + 1:]
            for q in range(1, 5):
                n = len(rest) // 4
                steps += rest[(q - 1) * n:q * n if q < 4 else TWO_SUB2 - TWO_SUB] if False else []
                steps += [relu2(q)] if q < 4 else []
            steps += rest[0:TWO_SUB2 - TWO_SUB] + [relu2(4)] + rest[TWO_SUB2 - TWO_SUB:]
            steps += [add_shared, gate_y(0), gate_y(1), gate_y(2), gate_y(3)]
            with dve.Fori(0, ITER) as i:
                each(dve, steps, i)

        def two_pool(pool):
            pool.wait_ge(sem["x_new"], x_phase_done(PH_TWO))

            def add_up(e):
                def step(pool, i, g):
                    at = i * (12 * NG) + (e * NG + g) * 3
                    t = A[g][:, e * W:(e + 1) * W]
                    if e == 0:
                        pool.wait_ge(sem["two_xs"], upto(0, i, g))
                    pool.wait_ge(sem["two_gated"], i * (4 * NG) + (e * NG + g + 1))
                    for n, half in enumerate((256, 128)):
                        pool_.tensor_tensor(t[:, 0:half], t[:, 0:half], t[:, half:2 * half], ALU.add)\
                            .then_inc(sem["two_sum"], 1)
                        pool.wait_ge(sem["two_sum"], at + (n + 1))
                    pool_.tensor_tensor(xg(i, g, e), xg(i, g, e), t[:, 0:C], ALU.add).then_inc(sem["two_sum"], 1)
                    if e == GRAPHS - 1:
                        pool.wait_ge(sem["two_sum"], at + 3)
                        pool.sem_inc(sem["x_new"], 1)
                return step

            with pool.Fori(0, ITER) as i:
                each(pool, [lambda p, i, g: ln_rstd(p, PH_TWO, i, g), add_up(0), add_up(1), add_up(2), add_up(3)], i)

        PH_AT = 7
        GE3 = GRAPHS * E3
        at_ops = [[op, []] for op in softmax_ops(lambda g: PS[g][0][:, 0:GE3], None, E3)]
        at_ops[0][1] = [("at_logit", 0)]
        AT_SUB = len(at_ops) - 1
        at_ops += [[op, []] for op in probability_ops(E3)]
        at_ops[AT_SUB + 1][1] = [("at_sexp", 0)]
        at_ops += [[op, []] for op in first_of_max_ops(4, 9, 10, 11, 12, 8, "rank8", E3) + rest_op(E3)
                   + first_of_max_ops(7, 13, 10, 11, 12, 2, "rank8", E3)]
        at_ops += [
            [lambda i, g: dve_.scalar_tensor_tensor(out=gsm[g][:, 5, 0:4], in0=gsm[g][:, 9, 0:4], scalar=1e-9,
                                                    in1=gsm[g][:, 13, 0:4], op0=ALU.add, op1=ALU.add), []],
            [lambda i, g: dve_.reciprocal(gsm[g][:, 6, 0:4], gsm[g][:, 5, 0:4]), []],
            [lambda i, g: dve_.tensor_tensor(gsm[g][:, 0, 0:GE3], gsm[g][:, 8, 0:GE3], gsm[g][:, 2, 0:GE3], ALU.add), []],
            [lambda i, g: dve_.tensor_tensor(gsm[g][:, 1, 0:GE3], gsm[g][:, 0, 0:GE3], gsm[g][:, 4, 0:GE3], ALU.mult), []],
            [lambda i, g: dve_.tensor_tensor(v3(weights3[:, bass.ds(i * (NG * GE3) + g * GE3, GE3)], E3),
                                             v3(gsm[g][:, 1, 0:GE3], E3), per_graph(gsm[g][:, 6, 0:4], E3), ALU.mult),
             [("at_xadd", 0), ("at_store", 0)]],
        ]
        AT_N = len(at_ops)

        def at_pe(pe):
            pe.wait_ge(sem["x_new"], x_phase_done(PH_AT))

            def rope_in(pe, i, g):
                pe.wait_ge(sem["xnt_ready"], upto(PH_AT, i, g))
                for b, w in enumerate(("q3", "q3r", "k3", "k3r")):
                    ins = pe_.matmul(PS[g][b][:, :], s(w), xnt[g][:, :], start=True, stop=True)
                ins.then_inc(sem["at_rope"], 1)

            def v_in(pe, i, g):
                pe.wait_ge(sem["at_ropem"], upto(0, i, g))
                for e in range(GRAPHS):
                    ins = pe_.matmul(PS[g][0][:, e * 64:(e + 1) * 64], slot(xnt[g], e), s("v3"), start=True, stop=True)
                ins.then_inc(sem["at_v"], 1)

            def score(pe, i, g):
                pe.wait_ge(sem["at_qk"], upto(0, i, g))
                pe.wait_ge(sem["at_vc"], upto(0, i, g))
                for h in range(NH3):
                    pe_.matmul(PS[g][h][:, :].rearrange("p (e n) -> p e n", n=N), ident_bf[:, :],
                               future_bf[:, :].unsqueeze(1).to_broadcast([128, GRAPHS, N]), start=True, stop=False)
                for e in range(GRAPHS):
                    for h in range(NH3):
                        r = slice(32 * h, 32 * h + 32)
                        ins = pe_.matmul(slot(PS[g][h], e), Bb[g][r, e * N:(e + 1) * N], Bb[g][r, W + e * N:W + (e + 1) * N],
                                         start=False, stop=e == GRAPHS - 1)
                ins.then_inc(sem["at_score"], 1)

            def transpose(pe, i, g):
                pe.wait_ge(sem["at_exp"], upto(0, i, g))
                for h in range(NH3):
                    for e in range(GRAPHS):
                        ins = pe_.transpose(slot(PS[g][h], e), slot(A[g], h * 4 + e), s("ident"))
                ins.then_inc(sem["at_pt"], 1)

            def attend(pe, i, g):
                pe.wait_ge(sem["at_pta"], upto(0, i, g))
                pe.wait_ge(sem["at_ptc"], upto(0, i, g))
                for h in range(NH3):
                    for e in range(GRAPHS):
                        ins = pe_.matmul(PS[g][0][:, e * N + h * HD3:e * N + (h + 1) * HD3], slot(Bb[g], h * 4 + e),
                                         Cc[g][:, W + e * 64 + h // 2 * HD3:W + e * 64 + (h // 2 + 1) * HD3],
                                         start=True, stop=True)
                ins.then_inc(sem["at_av"], 1)

            def y_transpose(pe, i, g):
                pe.wait_ge(sem["at_y"], upto(0, i, g))
                for e in range(GRAPHS):
                    ins = pe_.transpose(slot(PS[g][1], e), xn[g][:, e, :], s("ident"))
                ins.then_inc(sem["at_yt"], 1)

            def out_proj(pe, i, g):
                pe.wait_ge(sem["at_ytc"], upto(0, i, g))
                for e in range(GRAPHS):
                    ins = pe_.matmul(slot(PS[g][2], e), slot(xnt[g], e), s("o3"), start=True, stop=True)
                ins.then_inc(sem["at_o"], 1)

            def f_transpose(pe, i, g):
                pe.wait_ge(sem["at_f"], upto(0, i, g))
                for e in range(GRAPHS):
                    ins = pe_.transpose(slot(PS[g][3], e), slot(A[g], e), s("ident"))
                ins.then_inc(sem["at_ft"], 1)

            def router(pe, i, g):
                pe.wait_ge(sem["at_ftc"], upto(0, i, g))
                for e in range(GRAPHS):
                    ins = pe_.matmul(PS[g][0][:, e * E3:(e + 1) * E3], slot(xnt[g], e), s("router3"), start=True, stop=True)
                ins.then_inc(sem["at_logit"], 1)

            with pe.Fori(0, ITER) as i:
                each(pe, [lambda pe, i, g: xn_transpose(pe, PH_AT, i, g), rope_in, v_in, score, transpose, attend,
                          y_transpose, out_proj, f_transpose, router], i)

        def at_act(act):
            act.wait_ge(sem["x_new"], x_phase_done(PH_AT))

            def copy_v(act, i, g):
                act.wait_ge(sem["at_v"], upto(0, i, g))
                act_.activation(Cc[g][:, W:W + 256], PS[g][0][:, 0:256], ACT.Copy).then_inc(sem["at_vc"], 1)

            def exps(act, i, g):
                act.wait_ge(sem["at_nmax"], upto(0, i, g))
                for h in range(NH3):
                    for e in range(GRAPHS):
                        n = h * 4 + e
                        ins = act_.activation(slot(A[g], n), slot(PS[g][h], e), ACT.Exp, bias=neg_row[:, g, n:n + 1],
                                              scale=SCALE3, accum_out=tot[:, g, n:n + 1])
                ins.then_inc(sem["at_exp"], 1)

            def copy_pt(act, i, g):
                act.wait_ge(sem["at_pt"], upto(0, i, g))
                for h in range(2):
                    ins = act_.activation(Bb[g][:, h * W:(h + 1) * W], PS[g][h][:, :], ACT.Copy)
                ins.then_inc(sem["at_pta"], 1)

            def copy_yt(act, i, g):
                act.wait_ge(sem["at_yt"], upto(0, i, g))
                act_.activation(xnt[g][:, :], PS[g][1][:, :], ACT.Copy).then_inc(sem["at_ytc"], 1)

            def square(act, i, g):
                act.wait_ge(sem["at_x1"], upto(0, i, g))
                for e in range(GRAPHS):
                    ins = act_.activation(slot(Bb[g], e), xn[g][:, e, :], ACT.Square, accum_out=tot[:, g, e:e + 1])
                ins.then_inc(sem["at_sq"], 1)

            def copy_ft(act, i, g):
                act.wait_ge(sem["at_ft"], upto(0, i, g))
                act_.activation(xnt[g][:, :], PS[g][3][:, :], ACT.Copy).then_inc(sem["at_ftc"], 1)

            def gate_exp(act, i, g):
                act.wait_ge(sem["at_gate"], gate_at(AT_N, i, g, AT_SUB))
                act_.activation(gsm[g][:, 3, 0:GE3], gsm[g][:, 2, 0:GE3], ACT.Exp).then_inc(sem["at_sexp"], 1)

            with act.Fori(0, ITER) as i:
                each(act, [lambda act, i, g: xnt_copy(act, PH_AT, i, g), copy_v, exps, copy_pt, copy_yt, square, copy_ft,
                           gate_exp], i)

        def at_dve(dve):
            dve.wait_ge(sem["x_new"], x_phase_done(PH_AT))

            def norms(dve, i, g):
                dve.wait_ge(sem["at_rms"], i * (NG * 5) + (g + 1) * 5)
                for e in range(GRAPHS):
                    dve_.tensor_scalar(slot(Cc[g], e), xg(i, g, e), moments[:, g, e, 0:1], rstd[:, g, e:e + 1],
                                       ALU.subtract, ALU.mult)
                    ins = dve_.tensor_scalar(xn[g][:, e, :], xg(i, g, e), moments[:, g, e, 0:1], rms[:, g, 3, e:e + 1],
                                             ALU.subtract, ALU.mult)
                ins.then_inc(sem["xn_ready"], 1)

            def rope(dve, i, g):
                dve.wait_ge(sem["at_rope"], upto(0, i, g))
                for b in range(4):
                    table = s("cos") if b % 2 == 0 else s("sin")
                    ins = dve_.tensor_tensor(A[g][:, b * W:(b + 1) * W].rearrange("p (e n) -> p e n", n=N),
                                             PS[g][b][:, :].rearrange("p (e n) -> p e n", n=N),
                                             table.unsqueeze(1).to_broadcast([128, GRAPHS, N]), ALU.mult)
                ins.then_inc(sem["at_ropem"], 1)

            def row_max(dve, i, g):
                dve.wait_ge(sem["at_score"], upto(0, i, g))
                for h in range(NH3):
                    ins = dve_.tensor_reduce(row[:, g, h * 4:h * 4 + 4], PS[g][h][:, :].rearrange("p (e n) -> p e n", n=N),
                                             AX.X, ALU.max)
                ins.then_inc(sem["at_max"], 1)

            def copy_pt(dve, i, g):
                dve.wait_ge(sem["at_pt"], upto(0, i, g))
                for h in range(2, 4):
                    ins = dve_.tensor_copy(Bb[g][:, h * W:(h + 1) * W], PS[g][h][:, :])
                ins.then_inc(sem["at_ptc"], 1)
                dve_.reciprocal(inv[:, g, :], tot[:, g, :]).then_inc(sem["at_inv"], 1)

            def normalise(dve, i, g):
                dve.wait_ge(sem["at_av"], upto(0, i, g))
                dve.wait_ge(sem["at_inv"], upto(0, i, g))
                dve_.tensor_tensor(xn[g][:, :, :].rearrange("p e (h d) -> p e h d", h=NH3),
                                   PS[g][0][:, :].rearrange("p (e h d) -> p e h d", e=GRAPHS, h=NH3),
                                   inv[:, g, :].rearrange("p (h e) -> p e h", h=NH3).unsqueeze(3)
                                   .to_broadcast([128, GRAPHS, NH3, HD3]), ALU.mult).then_inc(sem["at_y"], 1)

            def x1(dve, i, g):
                dve.wait_ge(sem["at_o"], upto(0, i, g))
                dve_.tensor_tensor(xn[g][:, :, :].rearrange("p e n -> p (e n)"), PS[g][2][:, :], Cc[g][:, 0:W], ALU.add)\
                    .then_inc(sem["at_x1"], 1)

            def f(dve, i, g):
                dve.wait_ge(sem["at_rstd"], upto(0, i, g))
                for e in range(GRAPHS):
                    ins = dve_.tensor_scalar(slot(A[g], e), xn[g][:, e, :], rstd[:, g, e:e + 1], float(C) ** 0.5,
                                             ALU.mult, ALU.mult)
                ins.then_inc(sem["at_f"], 1)

            def finish(dve, i, g):
                dve.wait_ge(sem["at_gate"], gate_at(AT_N, i, g, AT_N - 1))
                dve.sem_inc(sem["x_new"], 1)

            with dve.Fori(0, ITER) as i:
                each(dve, [lambda d, i, g: ln_stats(d, PH_AT, i, g), lambda d, i, g: ln_moments(d, PH_AT, i, g), norms,
                           rope, row_max, copy_pt, normalise, x1, f] + gate_chain(dve, "at_gate", at_ops) + [finish], i)

        def at_pool(pool):
            pool.wait_ge(sem["x_new"], x_phase_done(PH_AT))

            def rms_of_ln(pool, i, g):
                at = i * (NG * 5) + g * 5
                pool.wait_ge(sem["ln_rstd"], upto(PH_AT, i, g))
                pool_.tensor_tensor(rms[:, g, 0, :], rstd[:, g, :], rstd[:, g, :], ALU.mult).then_inc(sem["at_rms"], 1)
                pool.wait_ge(sem["at_rms"], at + 1)
                pool_.tensor_tensor(rms[:, g, 1, :], rms[:, g, 0, :], moments[:, g, :, 1], ALU.mult).then_inc(sem["at_rms"], 1)
                pool.wait_ge(sem["at_rms"], at + 2)
                pool_.tensor_tensor(rms[:, g, 2, :], rms[:, g, 1, :], s("eps")[:, GRAPHS:2 * GRAPHS], ALU.add).then_inc(sem["at_rms"], 1)
                pool.wait_ge(sem["at_rms"], at + 3)
                pool_.tensor_tensor(rms[:, g, 0, :], rms[:, g, 2, :], s("minus_half")[:, 0:GRAPHS], ALU.pow)\
                    .then_inc(sem["at_rms"], 1)
                pool.wait_ge(sem["at_rms"], at + 4)
                pool_.tensor_tensor(rms[:, g, 3, :], rms[:, g, 0, :], rstd[:, g, :], ALU.mult).then_inc(sem["at_rms"], 1)

            def add_rope(pool, i, g):
                pool.wait_ge(sem["at_ropem"], upto(0, i, g))
                for b in range(2):
                    ins = pool_.tensor_tensor(Bb[g][:, b * W:(b + 1) * W], A[g][:, 2 * b * W:(2 * b + 1) * W],
                                              A[g][:, (2 * b + 1) * W:(2 * b + 2) * W], ALU.add)
                ins.then_inc(sem["at_qk"], 1)

            def neg_max(pool, i, g):
                pool.wait_ge(sem["at_max"], upto(0, i, g))
                pool_.tensor_tensor(neg_row[:, g, :], row[:, g, :], s("scale3"), ALU.mult).then_inc(sem["at_nmax"], 1)

            def add_x(pool, i, g):
                pool.wait_ge(sem["at_x1"], upto(0, i, g))
                pool_.tensor_tensor(xgroup(i, g), xgroup(i, g), xn[g][:, :, :], ALU.add).then_inc(sem["at_xadd"], 1)

            def rms_x1(pool, i, g):
                pool.wait_ge(sem["at_sq"], upto(0, i, g))
                pool_.tensor_tensor(vare[:, g, :], tot[:, g, 0:GRAPHS], s("eps")[:, 2 * GRAPHS:3 * GRAPHS], ALU.add)\
                    .then_inc(sem["at_ms"], 1)
                pool.wait_ge(sem["at_ms"], upto(0, i, g))
                pool_.tensor_tensor(rstd[:, g, :], vare[:, g, :], s("minus_half")[:, 0:GRAPHS], ALU.pow)\
                    .then_inc(sem["at_rstd"], 1)

            def store_f(pool, i, g):
                pool.wait_ge(sem["at_ftc"], upto(0, i, g))
                pool_.tensor_copy(late[:, bass.ds(i * (NG * W) + g * W, W)], xnt[g][:, :]).then_inc(sem["at_store"], 1)

            with pool.Fori(0, ITER) as i:
                each(pool, [lambda p, i, g: ln_rstd(p, PH_AT, i, g), rms_of_ln, add_rope, neg_max, rms_x1, add_x, store_f], i)

        PH_BIG = 8
        NC3 = len(CHUNKS3)

        def big_at(i, g, n, count):
            return i * (NG * count) + (n * NG + g + 1)

        def w3(name, e, c0, c):
            a = BIG3[name][0] + e * HID3
            return big[:, a + c0:a + c0 + c]

        def hh(g, e, c):
            return (A, Bb)[e % 2][g][:, c * W:(c + 1) * W]

        def big_pe(pe):
            pe.wait_ge(sem["x_new"], x_phase_done(PH_BIG))
            pe.wait_ge(sem["loaded_big3"], 16)

            def up(e, c):
                u = e * NC3 + c
                c0, m = CHUNKS3[c]

                def step(pe, i, g):
                    if u == 0:
                        pe.wait_ge(sem["x_new"], x_before(PH_BIG, i, g))
                    else:
                        pe.wait_ge(sem["big_hh"], big_at(i, g, u - 1, E3 * NC3))
                    rhs = late[:, bass.ds(i * (NG * W) + g * W, W)]
                    pe_.matmul(PS[g][0][0:m, :], w3("w1", e, c0, m), rhs, start=True, stop=True)
                    pe_.matmul(PS[g][1][0:m, :], w3("w3", e, c0, m), rhs, start=True, stop=True).then_inc(sem["big_up"], 1)
                return step

            def down(e):
                def step(pe, i, g):
                    pe.wait_ge(sem["big_hh"], big_at(i, g, e * NC3 + NC3 - 1, E3 * NC3))
                    if e >= 2:
                        pe.wait_ge(sem["big_x"], big_at(i, g, e - 2, E3))
                    a = BIG3["w2"][0]
                    for q in range(GRAPHS):
                        for c, (c0, m) in enumerate(CHUNKS3):
                            ins = pe_.matmul(slot(PS[g][2 + e % 2], q), hh(g, e, c)[0:m, q * N:(q + 1) * N],
                                             big[0:m, a + (e * 3 + c) * C:a + (e * 3 + c + 1) * C],
                                             start=c == 0, stop=c == NC3 - 1)
                    ins.then_inc(sem["big_y"], 1)
                return step

            steps = []
            for e in range(E3):
                steps.append(up(e, 0))
                if e:
                    steps.append(down(e - 1))
                steps += [up(e, c) for c in range(1, NC3)]
            steps.append(down(E3 - 1))
            with pe.Fori(0, ITER) as i:
                each(pe, steps, i)

        def big_act(act):
            act.wait_ge(sem["x_new"], x_phase_done(PH_BIG))

            def silu(e, c):
                u = e * NC3 + c
                m = CHUNKS3[c][1]

                def step(act, i, g):
                    act.wait_ge(sem["big_up"], big_at(i, g, u, E3 * NC3))
                    act_.activation(Cc[g][0:m, u % 2 * W:(u % 2 + 1) * W], PS[g][0][0:m, :], ACT.Silu)\
                        .then_inc(sem["big_silu"], 1)
                return step

            with act.Fori(0, ITER) as i:
                each(act, [silu(e, c) for e in range(E3) for c in range(NC3)], i)

        def big_dve(dve):
            dve.wait_ge(sem["x_new"], x_phase_done(PH_BIG))

            def weights(dve, i, g):
                dve.wait_ge(sem["x_new"], x_before(PH_BIG, i, g))
                dve_.tensor_copy(gsm[g][:, 0, 0:GE3], weights3[:, bass.ds(i * (NG * GE3) + g * GE3, GE3)])\
                    .then_inc(sem["big_w"], 1)

            def multiply(e, c):
                u = e * NC3 + c
                m = CHUNKS3[c][1]

                def step(dve, i, g):
                    if c == 0 and e >= 2:
                        dve.wait_ge(sem["big_y"], big_at(i, g, e - 2, E3))
                    dve.wait_ge(sem["big_silu"], big_at(i, g, u, E3 * NC3))
                    dve_.tensor_tensor(hh(g, e, c)[0:m, :], PS[g][1][0:m, :], Cc[g][0:m, u % 2 * W:(u % 2 + 1) * W],
                                       ALU.mult).then_inc(sem["big_hh"], 1)
                return step

            def add(e):
                def step(dve, i, g):
                    if e == 0:
                        dve.wait_ge(sem["big_w"], upto(0, i, g))
                    else:
                        dve.wait_ge(sem["big_x"], big_at(i, g, e - 1, E3))
                    dve.wait_ge(sem["big_y"], big_at(i, g, e, E3))
                    for q in range(GRAPHS):
                        ins = dve_.scalar_tensor_tensor(out=xg(i, g, q), in0=slot(PS[g][2 + e % 2], q),
                                                        scalar=gsm[g][:, 0, q * E3 + e:q * E3 + e + 1], in1=xg(i, g, q),
                                                        op0=ALU.mult, op1=ALU.add)
                    ins.then_inc(sem["big_x"], 1)
                return step

            def finish(dve, i, g):
                dve.wait_ge(sem["big_x"], big_at(i, g, E3 - 1, E3))
                dve.sem_inc(sem["x_new"], 1)

            steps = [weights]
            for e in range(E3):
                steps += [multiply(e, 0)]
                if e:
                    steps += [add(e - 1)]
                steps += [multiply(e, c) for c in range(1, NC3)]
            steps += [add(E3 - 1), finish]
            with dve.Fori(0, ITER) as i:
                each(dve, steps, i)

        @block.sync
        def _(sp):
            sp.dma_start(small[:, :], small_in).then_inc(sem["loaded_small"], 16)
            for h in range(2):
                c = B // 2
                sp.dma_start(x[:, h * c:(h + 1) * c, :], x_dram[:, h * c:(h + 1) * c, :]).then_inc(sem["loaded_x"], 16)
            if PHASES > 2:
                sp.wait_ge(sem["x_new"], x_phase_done(PH_MHA))
                sp.dma_start(big[:, 0:4 * E1 * C], down1_in).then_inc(sem["loaded_down1"], 16)
                mha_sp(sp)
            if PHASES > 4:
                sp.wait_ge(sem["x_new"], x_phase_done(4))
                sp.dma_start(big[:, :], big3_in).then_inc(sem["loaded_big3"], 16)
            sp.wait_ge(sem["x_new"], x_phase_done(PHASES))
            sp.dma_start(out_dram, x[:, :, :]).then_inc(sem["stored"], 16)
            sp.wait_ge(sem["stored"], 16)

        @block.gpsimd
        def _(pool):
            for _ in range(NG):
                pool.sem_inc(sem["x_new"], 1)
            pool.wait_ge(sem["loaded_small"], 16)
            run = [lambda: ln_pool(pool, 0), lambda: ssm_pool(pool), lambda: ln_pool(pool, 2), lambda: one_pool(pool),
                   lambda: ln_pool(pool, 4), lambda: two_pool(pool), lambda: ln_pool(pool, 6), lambda: at_pool(pool),
                   lambda: None]
            for phase in run[0:PHASES]:
                phase()

        @block.scalar
        def _(act):
            act.dma_start(adj.rearrange("p (b n) -> p b n", b=B), adj_dram).then_inc(sem["loaded_adj"], 16)
            act.wait_ge(sem["loaded_small"], 16)
            act_.activation(neg_a[:, :], s("a_log"), ACT.Exp).then_inc(sem["const_exp"], 1)
            run = [lambda: gat_act(act, 0, 0), lambda: ssm_act(act), lambda: mha_act(act), lambda: one_act(act),
                   lambda: gat_act(act, 4, 1), lambda: two_act(act), lambda: gat_act(act, 6, 2), lambda: at_act(act),
                   lambda: big_act(act)]
            for phase in run[0:PHASES]:
                phase()

        @block.vector
        def _(dve):
            dve.wait_ge(sem["loaded_small"], 16)
            dve_.tensor_copy(ident_bf[:, :], s("ident"))
            dve_.tensor_copy(future_bf[:, :], s("future"))
            dve_.tensor_copy(past_bf[:, :], s("past")).then_inc(sem["const_bf"], 1)
            for l in range(3):
                for j in range(2):
                    dve_.tensor_copy(a_rep[:, 2 * l + j, :], s(f"gat{l}_a")[:, j:j + 1].to_broadcast([128, 128]))
            dve_.tensor_copy(bv_rep[:, :], s("bv1").to_broadcast([128, 128])).then_inc(sem["const_rows"], 1)
            for name in ("in_z", "conv_w", "conv_b"):
                dve_.tensor_scalar(s(name), s(name), 0.5, None, ALU.mult)
            for name in ("q3", "q3r", "k3", "k3r", "v3"):
                dve_.tensor_scalar(s(name), s(name), s("ln1"), None, ALU.mult)
            dve_.tensor_scalar(s("router3"), s("router3"), s("ln2"), None, ALU.mult)
            dve_.tensor_scalar(neg_dist[:, :], s("dist"), -1.0, None, ALU.mult)
            for n, name in enumerate(("even", "odd")):
                dve_.tensor_scalar(q_fold[:, 2 * n:2 * n + 1], s(name), 0.25, None, ALU.mult)
                dve_.tensor_scalar(q_fold[:, 2 * n + 1:2 * n + 2], s("bq1"), s(name), 0.25, ALU.mult, ALU.mult)
            for j in range(2):
                dve_.tensor_scalar(diag_d[:, j, :], s("ident"), s("d_chan")[:, j:j + 1], None, ALU.mult)
            dve_.tensor_tensor(s("eb3"), s("eb3"), s("sb3"), ALU.add).then_inc(sem["const_folds"], 1)
            dve.wait_ge(sem["const_exp"], 1)
            dve_.tensor_scalar(neg_a[:, :], neg_a[:, :], -1.0, None, ALU.mult).then_inc(sem["const_a"], 1)
            dve.wait_ge(sem["const_score_psum"], 1)
            for l in range(3):
                dve_.tensor_copy(score_w[:, l, :, :], PS[0][l][:, 0:256].rearrange("p (j n) -> p j n", j=2))
            for j in range(2):
                dve_.tensor_scalar(mix[:, j, :], PS[1][j][:, 0:128], s("norm_w")[:, j:j + 1], None, ALU.mult)
            dve_.tensor_tensor(bias_out1[:, :], PS[1][2][:, 0:128], s("bo1"), ALU.add).then_inc(sem["const_score"], 1)
            dve.wait_ge(sem["loaded_adj"], 16)
            dve_.tensor_scalar(late[:, 0:B * N // 2].bitcast(BF16), adj, 0.0, NEG, ALU.is_le, ALU.mult)\
                .then_inc(sem["const_mask"], 1)
            dve.wait_ge(sem["const_folds"], 1)
            dve.wait_ge(sem["const_a"], 1)
            dve.wait_ge(sem["const_score"], 1)
            dve.wait_ge(sem["loaded_x"], 32)
            if PHASES > 8:
                pass
            run = [lambda: gat_dve(dve, 0, 0), lambda: ssm_dve(dve), lambda: mha_dve(dve), lambda: one_dve(dve),
                   lambda: gat_dve(dve, 4, 1), lambda: two_dve(dve), lambda: gat_dve(dve, 6, 2), lambda: at_dve(dve),
                   lambda: big_dve(dve)]
            for n, phase in enumerate(run[0:PHASES]):
                phase()
                if n == 5:
                    dve.wait_ge(sem["loaded_big3"], 16)
                    a, b = BIG3["w1"][0], BIG3["w3"][1]
                    dve_.tensor_scalar(big[:, a:b], big[:, a:b], s("ln2"), None, ALU.mult).then_inc(sem["const_bias"], 1)

        @block.tensor
        def _(pe):
            pe.wait_ge(sem["const_rows"], 1)
            for l in range(3):
                for j in range(2):
                    pe_.matmul(PS[0][l][:, j * 128:(j + 1) * 128], s(f"gat{l}_wt"), a_rep[:, 2 * l + j, :],
                               start=True, stop=True)
            for j in range(2):
                pe_.matmul(PS[1][j][:, 0:128], s("out_t")[:, j * 128:(j + 1) * 128], s("lin"), start=True, stop=True)
            pe_.matmul(PS[1][2][:, 0:128], bv_rep[:, :], s("o1"), start=True, stop=True)\
                .then_inc(sem["const_score_psum"], 1)
            pe.wait_ge(sem["const_score"], 1)
            pe.wait_ge(sem["const_folds"], 1)
            pe.wait_ge(sem["const_mask"], 1)
            run = [lambda: gat_pe(pe, 0, 0), lambda: ssm_pe(pe), lambda: mha_pe(pe), lambda: one_pe(pe),
                   lambda: gat_pe(pe, 4, 1), lambda: two_pe(pe), lambda: gat_pe(pe, 6, 2), lambda: at_pe(pe),
                   lambda: big_pe(pe)]
            for phase in run[0:PHASES]:
                phase()


def kernel(**inputs):
    import concourse.bacc as bacc
    from concourse.bass_utils import run_bass_kernel_spmd

    v = {k: np.asarray(a) for k, a in inputs.items()}
    f = np.float32
    tri = np.arange(128)
    HD = HD3
    inv_freq = 1.0 / 10000.0 ** (np.arange(0, HD, 2, dtype=np.float32) / HD)
    freqs = np.outer(np.arange(N, dtype=np.float32), inv_freq)
    emb = np.concatenate([freqs, freqs], axis=-1)
    sign = np.where(np.arange(HD) < HD // 2, -1.0, 1.0).astype(f)
    half = np.concatenate([np.arange(HD // 2, HD), np.arange(HD // 2)])
    rot = np.concatenate([h * HD + half for h in range(NH3)])

    def rows(a, n=128):
        return np.tile(a.reshape(1, -1), (n, 1))

    def pad(a):
        return np.concatenate([a, np.zeros((128 - a.shape[0], a.shape[1]), a.dtype)]) if a.shape[0] < 128 else a

    def blocks(a):
        e = a.shape[0]
        out = np.zeros((GRAPHS * e, GRAPHS * 128), a.dtype)
        for g in range(GRAPHS):
            out[g * e:(g + 1) * e, g * 128:(g + 1) * 128] = a
        return out

    w_in = v["L0_ffn_W_in"]
    k3 = v["L3_ffn_wk"].reshape(2, HD, C)[[0, 0, 1, 1]].reshape(128, C)
    parts = {
        "ident": np.eye(128, dtype=f), "upto": (tri[:, None] <= tri[None]).astype(f),
        "after": (tri[:, None] > tri[None]).astype(f),
        "future": np.where(tri[None] > tri[:, None], f(NEG), f(0)), "past": np.where(tri[:, None] > tri[None], f(NEG), f(0)),
        "cos": np.tile(np.cos(emb).T, (NH3, 1)), "sin": np.tile((np.sin(emb) * sign).T, (NH3, 1)),
        "rank8": rows(np.arange(8, 0, -1).astype(f)), "rank4": rows(np.arange(4, 0, -1).astype(f)),
        "even": (tri // DK1 % 2 == 0).astype(f)[:, None], "odd": (tri // DK1 % 2 == 1).astype(f)[:, None],
        "minus_half": np.full((128, 8), -0.5, f),
        "eps": rows(np.repeat(np.array([EPS_LN, EPS_RMS3, C * EPS_RMS3], f), GRAPHS)),
        "scale3": np.full((128, 16), -SCALE3, f),
        "in_xbc": w_in[:, 256:640], "in_z": w_in[:, 0:256], "in_dt": w_in[:, 640:644],
        "conv_w": v["L0_ffn_conv_w"].reshape(3, 128, 4).transpose(1, 0, 2).reshape(128, 12),
        "conv_b": v["L0_ffn_conv_b"].reshape(3, 128).T, "dt_bias": rows(v["L0_ffn_dt_bias"]),
        "a_log": rows(v["L0_ffn_A_log"]), "d_chan": np.repeat(v["L0_ffn_D"], P0).reshape(2, 128).T,
        "norm_w": v["L0_ffn_norm_w"].reshape(2, 128).T, "out_t": v["L0_ffn_W_out"].T, "lin": v["L0_ffn_W_lin"],
        "b_lin": rows(v["L0_ffn_b_lin"]),
        "q1": v["L1_gnn_W_q"], "k1": v["L1_gnn_W_k"], "v1": v["L1_gnn_W_v"], "o1": v["L1_gnn_W_o"],
        "bq1": v["L1_gnn_b_q"][:, None], "bk1": v["L1_gnn_b_k"][:, None], "bv1": v["L1_gnn_b_v"][:, None],
        "bo1": rows(v["L1_gnn_b_o"]), "dist": rows(v["L1_gnn_dist_scale"].reshape(1)),
        "up1": v["L1_ffn_W1"], "b_up1": v["L1_ffn_b1"].reshape(4, 128).T,
        "gate1": v["L1_ffn_Wg"].reshape(4, 128, E1).transpose(1, 0, 2).reshape(128, 4 * E1),
        "b_gate1": rows(v["L1_ffn_bg"]), "b_down1": pad(blocks(v["L1_ffn_bd"])),
        "s1": v["L2_ffn_sW1"], "s2": v["L2_ffn_sW2"], "s3": v["L2_ffn_sW3"], "sb1": v["L2_ffn_sb1"][:, None],
        "sb2": v["L2_ffn_sb2"][:, None], "e1": v["L2_ffn_eW1"].transpose(1, 0, 2).reshape(128, E2 * 128),
        "eb1": v["L2_ffn_eb1"].T, "e2": v["L2_ffn_eW2"].transpose(1, 0, 2).reshape(128, E2 * EH2),
        "eb2": pad(v["L2_ffn_eb2"].T), "e3": pad(v["L2_ffn_eW3"].transpose(1, 0, 2).reshape(EH2, E2 * 128)),
        "eb3": pad(blocks(v["L2_ffn_eb3"])), "sb3": pad(blocks(rows(v["L2_ffn_sb3"], E2))),
        "gate2": v["L2_ffn_gW"], "b_gate2": rows(v["L2_ffn_gb"]),
        "ln1": v["L3_ffn_ln1_w"][:, None], "ln2": v["L3_ffn_ln2_w"][:, None],
        "q3": v["L3_ffn_wq"].T, "q3r": v["L3_ffn_wq"][rot].T, "k3": k3.T, "k3r": k3[rot].T,
        "v3": v["L3_ffn_wv"].T, "o3": v["L3_ffn_wo"].T, "router3": v["L3_ffn_router_w"].T,
    }
    for l, n in enumerate(("L0", "L2", "L3")):
        w, a = v[f"{n}_gnn_W"], v[f"{n}_gnn_a"]
        w = w.T if n == "L2" else w
        parts[f"gat{l}_w"], parts[f"gat{l}_wt"] = w, w.T
        parts[f"gat{l}_a"] = a.reshape(2, 128).T
    small = np.concatenate([parts[name] for name, _ in SMALL], axis=1)
    down1 = v["L1_ffn_Wd"].reshape(E1, 4, 128, C).transpose(2, 1, 0, 3).reshape(128, 4 * E1 * C)
    w2 = v["L3_ffn_w2"].transpose(0, 2, 1)
    w2 = np.concatenate([w2, np.zeros((E3, 384 - HID3, C), f)], axis=1).reshape(E3, 3, 128, C)
    big3 = np.concatenate([v["L3_ffn_w1"].transpose(2, 0, 1).reshape(C, E3 * HID3),
                           v["L3_ffn_w3"].transpose(2, 0, 1).reshape(C, E3 * HID3),
                           w2.transpose(2, 0, 1, 3).reshape(128, E3 * 3 * C)], axis=1)

    arrays = {"x_dram": v["x"], "adj_dram": v["adj"], "small_dram": small, "down1_dram": down1, "big3_dram": big3}
    arrays = {n: np.ascontiguousarray(a) for n, a in arrays.items()}
    nc = bacc.Bacc("TRN2", target_bir_lowering=False, num_devices=1)
    args = [nc.dram_tensor(n, a.shape, mybir.dt.from_np(a.dtype), kind="ExternalInput").ap() for n, a in arrays.items()]
    args.append(nc.dram_tensor("out_dram", v["x"].shape, F32, kind="ExternalOutput").ap())
    program(nc, *args)
    r = run_bass_kernel_spmd(nc, [arrays], core_ids=[0])
    return r.results[0]["out_dram"]
```

```python
from contextlib import ExitStack

import numpy as np
import concourse.bass as bass
from concourse import mybir
from concourse.alu_op_type import AluOpType as ALU

ACT = mybir.ActivationFunctionType
AX = mybir.AxisListType
F32 = mybir.dt.float32
BF16 = mybir.dt.bfloat16
F32R = mybir.dt.float32r
I32 = mybir.dt.int32

N = 128
C = 128
GRAPHS = 4
NG = 2
W = GRAPHS * N
NEG = -float(2 ** 60)
PHASES = 9

HEADS1, DK1 = 8, 16
E1, HID1 = 8, 512
E2, EH2 = 4, 64
NH3, HD3 = 4, 32
E3, HID3 = 8, 341
CHUNK3 = -(-HID3 // 3)
CHUNKS3 = [(c, min(CHUNK3, HID3 - c)) for c in range(0, HID3, CHUNK3)]
H0, P0, S0 = 4, 64, 64
EPS_LN, EPS_RMS0, EPS_RMS3 = 1e-5, 1e-5, 1e-6
SCALE3 = float(np.float32(1.0) / np.sqrt(np.float32(HD3)))


def columns(sizes):
    at, out = 0, {}
    for name, n in sizes:
        out[name] = (at, at + n)
        at += n
    return out, at


SMALL = [("ident", 128), ("upto", 128), ("after", 128), ("future", 128), ("past", 128), ("cos", 128),
         ("sin", 128), ("rank8", 8), ("rank4", 4), ("even", 1), ("odd", 1), ("minus_half", 8), ("eps", 3 * GRAPHS), ("scale3", 16)]
for _l in range(3):
    SMALL += [(f"gat{_l}_w", 128), (f"gat{_l}_wt", 128), (f"gat{_l}_a", 2)]
SMALL += [("in_xbc", 384), ("in_z", 256), ("in_dt", 4), ("conv_w", 12), ("conv_b", 3), ("dt_bias", 4),
          ("a_log", 4), ("d_chan", 2), ("norm_w", 2), ("out_t", 256), ("lin", 128), ("b_lin", 128)]
SMALL += [("q1", 128), ("k1", 128), ("v1", 128), ("o1", 128), ("bq1", 1), ("bk1", 1), ("bv1", 1),
          ("bo1", 128), ("dist", 1)]
SMALL += [("up1", HID1), ("b_up1", 4), ("gate1", 4 * E1), ("b_gate1", E1), ("b_down1", W)]
SMALL += [("s1", 128), ("s2", 128), ("s3", 128), ("sb1", 1), ("sb2", 1), ("e1", E2 * 128), ("eb1", E2),
          ("e2", E2 * EH2), ("eb2", E2), ("e3", E2 * 128), ("eb3", W), ("sb3", W), ("gate2", E2), ("b_gate2", E2)]
SMALL += [("ln1", 1), ("ln2", 1), ("q3", 128), ("q3r", 128), ("k3", 128), ("k3r", 128), ("v3", 64), ("o3", 128),
          ("router3", E3)]
AT, SMALL_COLS = columns(SMALL)
BIG3, BIG_COLS = columns([("w1", E3 * HID3), ("w3", E3 * HID3), ("w2", E3 * 3 * C)])

SIGNALS = """loaded_small x_new ln_stats ln_moments ln_var ln_rstd xn_ready xnt_psum xnt_ready gat_proj gat_score gat_exp
gat_pt gat_ptc gat_wh gat_agg gat_leak gat_max gat_inv ssm_conv ssm_z ssm_silu ssm_gz ssm_xt ssm_tri ssm_xdt
ssm_y ssm_yg ssm_yt ssm_ytc ssm_o ssm_tap ssm_dta ssm_dte ssm_dtl ssm_tanh ssm_tz ssm_sq ssm_dtx ssm_dt ssm_da
ssm_rstd ssm_bias ssm_ms mha_qkv mha_q mha_k mha_ot mha_otc mha_out mha_bias loaded_down1 one_h one_act
gate_logit gate_gt gate_gtc one_bd one_xb gate_exp two_sh two_exp2 two_xs at_rope at_ropem at_v at_qk at_vc
at_pta at_av at_y at_yt at_ytc at_o at_f at_ft at_ftc at_nmax at_x1 at_sq at_rstd at_xadd at_ms at_store
loaded_big3 one_w one_high one_low big_fhigh big_flow big_whigh big_wlow big_hh big_up big_x big_y big_silu big_w loaded_x stored loaded_adj const_exp const_bf const_rows
const_folds const_a const_score_psum const_score const_mask const_bias""".split()
TURNS = """ssm_taps ssm_decay ssm_seg ssm_m mha_adj mha_o mha_score mha_exp mha_pt mha_pta mha_ptc mha_av mha_t mha_inv
gate_step expert_gated expert_y expert_sum two_h1c two_h1 two_h2c two_h2 at_rms""".split()


def program(nc, x_in, adj_in, small_in, down1_in, big3_in, out):
    B = x_in.shape[0]
    GROUPS = B // GRAPHS
    ITER = GROUPS // NG
    x_dram = x_in.rearrange("b n c -> n b c")
    adj_dram = adj_in.rearrange("b n c -> n b c")
    out_dram = out.rearrange("b n c -> n b c")

    ctx = ExitStack()
    with ctx:
        address = {}

        def sb(name, shape, dt=F32):
            address[name] = -(-nc.sbuf_base // 32) * 32
            return ctx.enter_context(nc.sbuf_tensor(name, shape, dt))

        def rounded(name, shape):
            return nc.alloc_sbuf_tensor_at(name + "_rounded", shape, F32R, offset=address[name]).ap()

        sem = {name: ctx.enter_context(nc.semaphore(name)) for name in SIGNALS}
        turns = {name: [ctx.enter_context(nc.semaphore(f"{name}_{g}")) for g in range(NG)] for name in TURNS}

        x = sb("x", [N, B, C])
        small = sb("small", [128, SMALL_COLS])
        big = sb("big", [128, BIG_COLS])
        late = sb("late", [128, B * C])
        mask = late[:, 0:B * N // 2].bitcast(BF16).rearrange("p (b n) -> p b n", b=B)
        adj = big[:, 0:B * N].bitcast(I32)
        down1 = big[:, 0:4 * E1 * C]
        A = [sb(f"A{g}", [128, 4 * W]) for g in range(NG)]
        Bb = [sb(f"B{g}", [128, 4 * W]) for g in range(NG)]
        Cc = [sb(f"C{g}", [128, 2 * W]) for g in range(NG)]
        xn = [sb(f"xn{g}", [128, GRAPHS, C]) for g in range(NG)]
        xnt = [sb(f"xnt{g}", [128, W]) for g in range(NG)]
        PS = [[ctx.enter_context(nc.psum_tensor(f"ps{g}{k}", [128, W], F32)) for k in range(4)] for g in range(NG)]
        big_r = rounded("big", [128, BIG_COLS])
        down1_low, down1_high = big_r[:, 0:4 * E1 * C], big_r[:, 4 * E1 * C:8 * E1 * C]
        A_r = [rounded(f"A{g}", [128, 4 * W]) for g in range(NG)]
        B_r = [rounded(f"B{g}", [128, 4 * W]) for g in range(NG)]
        C_r = [rounded(f"C{g}", [128, 2 * W]) for g in range(NG)]
        xn_r = [rounded(f"xn{g}", [128, W]) for g in range(NG)]
        stats = sb("stats", [128, NG, GRAPHS, 6])
        moments = sb("moments", [128, NG, GRAPHS, 2])
        vare = sb("vare", [128, NG, GRAPHS])
        rstd = sb("rstd", [128, NG, GRAPHS])
        row = sb("row", [128, NG, 16])
        tot = sb("tot", [128, NG, 16])
        inv = sb("inv", [128, NG, 16])
        ident_bf = sb("ident_bf", [128, 128], BF16)
        future_bf = sb("future_bf", [128, 128], BF16)
        past_bf = sb("past_bf", [128, 128], BF16)
        score_w = sb("score_w", [128, 3, 2, 128])
        a_rep = sb("a_rep", [128, 6, 128])
        gsm = [sb(f"gsm{g}", [128, 14, 32]) for g in range(NG)]
        neg_a = sb("neg_a", [128, H0])
        diag_d = sb("diag_d", [128, 2, 128])
        mix = sb("mix", [128, 2, 128])
        q_fold = sb("q_fold", [128, 4])
        bv_rep = sb("bv_rep", [128, 128])
        bias_out1 = sb("bias_out1", [128, 128])
        neg_dist = sb("neg_dist", [128, 1])
        neg_row = sb("neg_row", [128, NG, 16])
        rms = sb("rms", [128, NG, 4, GRAPHS])
        odd_and_o = sb("odd_and_o", [128, NG, 2, W])
        odd_and_o_r = rounded("odd_and_o", [128, NG * 2 * W])
        nothing = sb("nothing", [128, 2 * NG])
        weights3 = sb("weights3", [128, B * E3])

        def s(name):
            a, b = AT[name]
            return small[:, a:b]

        def lin(i, n, c):
            register, ahead = i
            return ahead * n + c if register is None else register * n + (ahead * n + c)

        def turn(name, g):
            return turns[name][g]

        def step_at(i, steps, step, before=0):
            return lin(i, steps, before + step + 1)

        def upto(k, i, g):
            return lin(i, NG, k * GROUPS + g + 1)

        def x_before(k, i, g):
            return lin(i, NG, k * GROUPS + g + 1)

        def first(i):
            return i[0] is None and i[1] == 0

        def x_phase_done(k):
            return k * GROUPS + NG

        block = ctx.enter_context(nc.Block())
        dve_ = nc.vector
        act_ = nc.scalar
        pe_ = nc.tensor
        pool_ = nc.gpsimd

        def ln_stats(dve, k, i, g):
            if first(i) or k == 7:
                dve.wait_ge(sem["x_new"], x_before(k, i, g))
            else:
                dve.wait_ge(sem["ln_moments"], lin(i, NG, k * GROUPS + g + 1 - NG))
            for e in range(GRAPHS):
                ins = dve_.bn_stats(stats[:, g, e, :], xg(i, g, e))
            ins.then_inc(sem["ln_stats"], 1)

        def xg(i, g, e):
            return x[:, lin(i, NG * GRAPHS, g * GRAPHS + e), :]

        def xgroup(i, g):
            return x[:, bass.ds(lin(i, NG * GRAPHS, g * GRAPHS), GRAPHS), :]

        def maskgroup(i, g):
            return mask[:, bass.ds(lin(i, NG * GRAPHS, g * GRAPHS), GRAPHS), :]

        def ln_moments(dve, k, i, g):
            dve.wait_ge(sem["ln_stats"], upto(k, i, g))
            dve_.memset(nothing[:, g:g + 1], 0.0)
            for e in range(GRAPHS):
                ins = dve_.bn_aggr(moments[:, g, e, :], stats[:, g, e, :])
            ins.then_inc(sem["ln_moments"], 1)

        def ln_rstd(pool, k, i, g):
            pool.wait_ge(sem["ln_moments"], upto(k, i, g))
            pool_.tensor_tensor(vare[:, g, :], moments[:, g, :, 1], s("eps")[:, 0:GRAPHS], ALU.add)\
                .then_inc(sem["ln_var"], 1)
            pool.wait_ge(sem["ln_var"], upto(k, i, g))
            pool_.tensor_tensor(rstd[:, g, :], vare[:, g, :], s("minus_half")[:, 0:GRAPHS], ALU.pow)\
                .then_inc(sem["ln_rstd"], 1)

        def ln_apply(dve, k, i, g):
            if not first(i):
                if k == 2:
                    dve.wait_ge(turn("mha_score", g), lin(i, 2, 0))
                elif k == 3:
                    dve.wait_ge(turn("expert_y", g), lin(i, 4, 0))
                else:
                    dve.wait_ge(sem["xnt_psum"], lin(i, NG, k * GROUPS + g + 1 - NG))
            dve.wait_ge(sem["ln_rstd"], upto(k, i, g))
            for e in range(GRAPHS):
                ins = dve_.tensor_scalar(xn[g][:, e, :], xg(i, g, e), moments[:, g, e, 0:1], rstd[:, g, e:e + 1],
                                         ALU.subtract, ALU.mult)
            ins.then_inc(sem["xn_ready"], 1)

        def xn_transpose(pe, k, i, g):
            before = g + 1 - NG
            if k in (1, 7) or first(i):
                pe.wait_ge(sem["x_new"], x_before(k, i, g))
            elif k == 3:
                pe.wait_ge(turn("expert_gated", g), lin(i, 4, 0))
            elif k == 2:
                pe.wait_ge(turn("mha_o", g), lin(i, 2, 0))
            elif k == 5:
                pe.wait_ge(sem["two_xs"], lin(i, NG, before))
            else:
                pe.wait_ge(sem["gat_ptc"], lin(i, NG, {0: 0, 4: 1, 6: 2}[k] * GROUPS + before))
            pe.wait_ge(sem["xn_ready"], upto(k, i, g))
            for e in range(GRAPHS):
                ins = pe_.transpose(PS[g][0][:, e * N:(e + 1) * N], xn[g][:, e, :], s("ident"))
            ins.then_inc(sem["xnt_psum"], 1)

        def all_free(pe, k, i, g):
            pe.wait_ge(sem["x_new"], x_before(k, i, g))

        def xnt_copy(act, k, i, g):
            act.wait_ge(sem["xnt_psum"], upto(k, i, g))
            act_.activation(xnt[g][:, :], PS[g][0][:, :], ACT.Copy).then_inc(sem["xnt_ready"], 1)

        def each(eng, steps, i):
            for step in steps:
                for g in range(NG):
                    step(eng, i, g)

        def gat_pe(k, l):
            def project(pe, i, g):
                all_free(pe, k, i, g)
                pe.wait_ge(sem["xnt_ready"], upto(k, i, g))
                for e in range(GRAPHS):
                    ins = pe_.matmul(PS[g][1][:, e * N:(e + 1) * N], xnt[g][:, e * N:(e + 1) * N], s(f"gat{l}_w"),
                                     start=True, stop=True)
                ins.then_inc(sem["gat_proj"], 1)

            def scores(pe, i, g):
                pe_.matmul(PS[g][2][:, :], score_w[:, l, 1, :], xnt[g][:, :], start=True, stop=False)
                for e in range(GRAPHS):
                    pe_.matmul(PS[g][2][:, e * N:(e + 1) * N], xnt[g][:, e * N:(e + 1) * N], score_w[:, l, 0, :],
                               start=False, stop=False)
                pe_.matmul(PS[g][2][:, :], ident_bf[:, :], maskgroup(i, g), start=False, stop=True)\
                    .then_inc(sem["gat_score"], 1)

            def transpose(pe, i, g):
                pe.wait_ge(sem["gat_exp"], upto(l, i, g))
                for e in range(GRAPHS):
                    ins = pe_.transpose(PS[g][0][:, e * N:(e + 1) * N], A[g][:, e * N:(e + 1) * N], s("ident"))
                ins.then_inc(sem["gat_pt"], 1)

            def aggregate(pe, i, g):
                pe.wait_ge(sem["gat_ptc"], upto(l, i, g))
                pe.wait_ge(sem["gat_wh"], upto(l, i, g))
                for e in range(GRAPHS):
                    ins = pe_.matmul(PS[g][3][:, e * N:(e + 1) * N], Bb[g][:, e * N:(e + 1) * N],
                                     Cc[g][:, e * N:(e + 1) * N], start=True, stop=True)
                ins.then_inc(sem["gat_agg"], 1)

            return [lambda pe, i, g: xn_transpose(pe, k, i, g), project, scores, transpose, aggregate]

        def gat_act(k, l):
            def leak(act, i, g):
                act.wait_ge(sem["gat_score"], upto(l, i, g))
                act_.activation(Cc[g][:, W:2 * W], PS[g][2][:, :], ACT.Relu, scale=-0.8).then_inc(sem["gat_leak"], 1)

            def copy_wh(act, i, g):
                act.wait_ge(sem["gat_proj"], upto(l, i, g))
                act_.activation(Cc[g][:, 0:W], PS[g][1][:, :], ACT.Copy).then_inc(sem["gat_wh"], 1)

            def exps(act, i, g):
                act.wait_ge(sem["gat_max"], upto(l, i, g))
                for e in range(GRAPHS):
                    ins = act_.activation(A[g][:, e * N:(e + 1) * N], Bb[g][:, e * N:(e + 1) * N], ACT.Exp,
                                          bias=row[:, g, e:e + 1], scale=-1.0, accum_out=tot[:, g, e:e + 1])
                ins.then_inc(sem["gat_exp"], 1)

            return [lambda act, i, g: xnt_copy(act, k, i, g), leak, copy_wh, exps]

        def gat_dve(k, l):
            def leaky_max(dve, i, g):
                dve.wait_ge(sem["gat_leak"], upto(l, i, g))
                dve_.memset(nothing[:, g:g + 1], 0.0)
                for e in range(GRAPHS):
                    ins = dve_.tensor_tensor_reduce(
                        out=Bb[g][:, e * N:(e + 1) * N], in0=PS[g][2][:, e * N:(e + 1) * N],
                        in1=Cc[g][:, W + e * N:W + (e + 1) * N], scale=-1.0, scalar=3.0e38, op0=ALU.add, op1=ALU.min,
                        accum_out=row[:, g, e:e + 1])
                ins.then_inc(sem["gat_max"], 1)

            def copy_pt(dve, i, g):
                dve.wait_ge(sem["gat_pt"], upto(l, i, g))
                dve_.tensor_copy(Bb[g][:, 0:W], PS[g][0][:, :]).then_inc(sem["gat_ptc"], 1)
                dve_.reciprocal(inv[:, g, 0:GRAPHS], tot[:, g, 0:GRAPHS]).then_inc(sem["gat_inv"], 1)

            def update(dve, i, g):
                dve.wait_ge(sem["gat_agg"], upto(l, i, g))
                dve.wait_ge(sem["gat_inv"], upto(l, i, g))
                for e in range(GRAPHS):
                    ins = dve_.scalar_tensor_tensor(out=xg(i, g, e), in0=PS[g][3][:, e * N:(e + 1) * N],
                                                    scalar=inv[:, g, e:e + 1], in1=xg(i, g, e),
                                                    op0=ALU.mult, op1=ALU.add)
                ins.then_inc(sem["x_new"], 1)

            return [lambda d, i, g: ln_stats(d, k, i, g), lambda d, i, g: ln_moments(d, k, i, g),
                           lambda d, i, g: ln_apply(d, k, i, g), leaky_max, copy_pt, update]

        def ln_pool(k):
            return [lambda pool, i, g: ln_rstd(pool, k, i, g)]

        PH_SSM = 1
        tri_d = [big[:, g * 4096:g * 4096 + 2048] for g in range(NG)]
        gz = [big[:, g * 4096 + 2048:g * 4096 + 3072] for g in range(NG)]
        xdt = [big[:, g * 4096 + 3072:g * 4096 + 4096] for g in range(NG)]
        BH = GRAPHS * H0

        def ssm_pe():
            def conv_in(pe, i, g):
                pe.wait_ge(sem["xnt_ready"], upto(PH_SSM, i, g))
                for j in range(3):
                    pe_.matmul(PS[g][j][:, :], s("in_xbc")[:, j * 128:(j + 1) * 128], xnt[g][:, :], start=True, stop=True)
                for e in range(GRAPHS):
                    ins = pe_.matmul(PS[g][3][:, e * H0:(e + 1) * H0], xnt[g][:, e * N:(e + 1) * N], s("in_dt"),
                                     start=True, stop=True)
                ins.then_inc(sem["ssm_conv"], 1)

            def z_in(pe, i, g):
                pe.wait_ge(turn("ssm_taps", g), step_at(i, 3, 2))
                for e in range(GRAPHS):
                    ins = pe_.matmul(PS[g][e // 2][:, e % 2 * 256:e % 2 * 256 + 256], xnt[g][:, e * N:(e + 1) * N],
                                     s("in_z"), start=True, stop=True)
                ins.then_inc(sem["ssm_z"], 1)

            def x_transpose(pe, i, g):
                pe.wait_ge(sem["ssm_silu"], upto(0, i, g))
                pe.wait_ge(sem["ssm_gz"], upto(0, i, g))
                for e in range(GRAPHS):
                    for j in range(2):
                        pe_.transpose(PS[g][e // 2][:, e % 2 * 256 + j * 128:e % 2 * 256 + (j + 1) * 128],
                                      A[g][:, j * W + e * N:j * W + (e + 1) * N], s("ident"))
                for e in range(GRAPHS):
                    ins = pe_.matmul(PS[g][2][:, e * N:(e + 1) * N], Cc[g][0:S0, e * N:(e + 1) * N],
                                     Cc[g][0:S0, W + e * N:W + (e + 1) * N], start=True, stop=True)
                ins.then_inc(sem["ssm_xt"], 1)

            def seg(e):
                bank = (3, 0, 1, 3)[e]

                def step(pe, i, g):
                    if e == 0:
                        pe.wait_ge(sem["ssm_tri"], upto(0, i, g))
                    elif e == 3:
                        pe.wait_ge(turn("ssm_decay", g), step_at(i, 4, 0))
                    else:
                        pe.wait_ge(sem["ssm_xdt"], upto(0, i, g))
                    for h in range(H0):
                        pe_.matmul(PS[g][bank][:, h * N:(h + 1) * N],
                                   tri_d[g][:, (e * H0 + h) * N:(e * H0 + h + 1) * N], s("upto"),
                                   start=h == 0, stop=False)
                    pe_.matmul(PS[g][bank][:, :].rearrange("p (h n) -> p h n", h=H0), ident_bf[:, :],
                               past_bf[:, :].unsqueeze(1).to_broadcast([128, H0, N]), start=False, stop=True)\
                        .then_inc(turn("ssm_seg", g), 1)
                return step

            def y(pe, i, g):
                pe.wait_ge(turn("ssm_m", g), step_at(i, 4, 3))
                for e in range(GRAPHS):
                    o = e % 2 * 256
                    for j in range(2):
                        pe_.matmul(PS[g][e // 2][:, o + j * 128:o + (j + 1) * 128], A[g][:, j * W + e * N:j * W + (e + 1) * N],
                                   diag_d[:, j, :], start=j == 0, stop=False)
                    for h in range(H0):
                        ins = pe_.matmul(PS[g][e // 2][:, o + h * P0:o + (h + 1) * P0],
                                         Bb[g][:, e * W + h * N:e * W + (h + 1) * N],
                                         xdt[g][:, e * 256 + h * P0:e * 256 + (h + 1) * P0], start=False, stop=h == H0 - 1)
                ins.then_inc(sem["ssm_y"], 1)

            def y_transpose(pe, i, g):
                pe.wait_ge(sem["ssm_yg"], upto(0, i, g))
                for e in range(GRAPHS):
                    for j in range(2):
                        ins = pe_.transpose(PS[g][2 + j][:, e * N:(e + 1) * N],
                                            Cc[g][:, e * 256 + j * 128:e * 256 + (j + 1) * 128], s("ident"))
                ins.then_inc(sem["ssm_yt"], 1)

            def mix_out(pe, i, g):
                pe.wait_ge(sem["ssm_ytc"], upto(0, i, g))
                for e in range(GRAPHS):
                    for j in range(2):
                        ins = pe_.matmul(PS[g][0][:, e * N:(e + 1) * N], Bb[g][:, j * W + e * N:j * W + (e + 1) * N],
                                         mix[:, j, :], start=j == 0, stop=j == 1)
                ins.then_inc(sem["ssm_o"], 1)

            return [lambda pe, i, g: xn_transpose(pe, PH_SSM, i, g), conv_in, z_in, x_transpose,
                          seg(0), seg(1), seg(2), seg(3), y, y_transpose, mix_out]

        def ssm_act():
            def tap(act, i, g):
                act.wait_ge(sem["ssm_conv"], upto(0, i, g))
                for j in range(3):
                    ins = act_.activation(A[g][:, j * W:(j + 1) * W], PS[g][j][:, :], ACT.Identity,
                                          bias=s("conv_b")[:, j:j + 1], scale=s("conv_w")[:, j * 4 + 3:j * 4 + 4])
                ins.then_inc(sem["ssm_tap"], 1)

            def dt_exp(act, i, g):
                act.wait_ge(sem["ssm_dta"], upto(0, i, g))
                act_.activation(gsm[g][:, 2, 0:BH], gsm[g][:, 1, 0:BH], ACT.Exp).then_inc(sem["ssm_dte"], 1)

            def dt_ln(act, i, g):
                act.wait_ge(sem["ssm_dte"], upto(0, i, g))
                act_.activation(gsm[g][:, 3, 0:BH], gsm[g][:, 2, 0:BH], ACT.Ln, bias=1.0).then_inc(sem["ssm_dtl"], 1)

            def tanh_xbc(act, i, g):
                act.wait_ge(turn("ssm_taps", g), step_at(i, 3, 2))
                act_.activation(Bb[g][:, 0:3 * W], A[g][:, 0:3 * W], ACT.Tanh).then_inc(sem["ssm_tanh"], 1)

            def tanh_z(act, i, g):
                act.wait_ge(sem["ssm_z"], upto(0, i, g))
                for b in range(2):
                    ins = act_.activation(gz[g][:, b * W:(b + 1) * W], PS[g][b][:, :], ACT.Tanh)
                ins.then_inc(sem["ssm_tz"], 1)

            def decay(e):
                bank = (3, 0, 1, 3)[e]

                def step(act, i, g):
                    act.wait_ge(turn("ssm_seg", g), step_at(i, 4, e))
                    if e == 0:
                        act.wait_ge(sem["ssm_silu"], upto(0, i, g))
                    act_.activation(Bb[g][:, e * W:(e + 1) * W], PS[g][bank][:, :], ACT.Exp).then_inc(turn("ssm_decay", g), 1)
                return step

            def square(act, i, g):
                act.wait_ge(sem["ssm_yg"], upto(0, i, g))
                for e in range(GRAPHS):
                    ins = act_.activation(A[g][:, e * 256:(e + 1) * 256], Cc[g][:, e * 256:(e + 1) * 256], ACT.Square,
                                          scale=1.0 / 16, accum_out=tot[:, g, e:e + 1])
                ins.then_inc(sem["ssm_sq"], 1)

            def copy_yt(act, i, g):
                act.wait_ge(sem["ssm_yt"], upto(0, i, g))
                for j in range(2):
                    ins = act_.activation(Bb[g][:, j * W:(j + 1) * W], PS[g][2 + j][:, :], ACT.Copy)
                ins.then_inc(sem["ssm_ytc"], 1)

            return [lambda act, i, g: xnt_copy(act, PH_SSM, i, g), tap, dt_exp, dt_ln, tanh_xbc, tanh_z,
                           decay(0), decay(1), decay(2), decay(3), square, copy_yt]

        def ssm_dve():
            def dt_x(dve, i, g):
                dve.wait_ge(sem["ssm_conv"], upto(0, i, g))
                dve_.tensor_tensor(gsm[g][:, 0, 0:BH].rearrange("p (e h) -> p e h", h=H0),
                                   PS[g][3][:, 0:BH].rearrange("p (e h) -> p e h", h=H0),
                                   s("dt_bias").unsqueeze(1).to_broadcast([128, GRAPHS, H0]), ALU.add)\
                    .then_inc(sem["ssm_dtx"], 1)

            def dt_abs(dve, i, g):
                dve.wait_ge(sem["ssm_dtx"], upto(0, i, g))
                dve_.scalar_tensor_tensor(out=gsm[g][:, 1, 0:BH], in0=gsm[g][:, 0, 0:BH], scalar=-1.0,
                                          in1=gsm[g][:, 0, 0:BH], op0=ALU.mult, op1=ALU.min)\
                    .then_inc(sem["ssm_dta"], 1)

            def dt_sum(dve, i, g):
                dve.wait_ge(sem["ssm_dtl"], upto(0, i, g))
                dve_.scalar_tensor_tensor(out=gsm[g][:, 4, 0:BH], in0=gsm[g][:, 0, 0:BH], scalar=0.0,
                                          in1=gsm[g][:, 3, 0:BH], op0=ALU.max, op1=ALU.add).then_inc(sem["ssm_dt"], 1)

            def da(dve, i, g):
                dve.wait_ge(sem["ssm_dt"], upto(0, i, g))
                dve_.tensor_tensor(gsm[g][:, 5, 0:BH].rearrange("p (e h) -> p e h", h=H0),
                                   gsm[g][:, 4, 0:BH].rearrange("p (e h) -> p e h", h=H0),
                                   neg_a[:, :].unsqueeze(1).to_broadcast([128, GRAPHS, H0]), ALU.mult)\
                    .then_inc(sem["ssm_da"], 1)

            def shifted(n):
                def step(dve, i, g):
                    if n == 1:
                        dve.wait_ge(sem["ssm_tap"], upto(0, i, g))
                    else:
                        dve.wait_ge(turn("ssm_taps", g), step_at(i, 3, n - 2))
                    for j in range(3):
                        acc = A[g][:, j * W:(j + 1) * W].rearrange("p (e n) -> p e n", n=N)[:, :, n:N]
                        ins = dve_.scalar_tensor_tensor(
                            out=acc, in0=PS[g][j][:, :].rearrange("p (e n) -> p e n", n=N)[:, :, 0:N - n],
                            scalar=s("conv_w")[:, j * 4 + 3 - n:j * 4 + 4 - n], in1=acc, op0=ALU.mult, op1=ALU.add)
                    ins.then_inc(turn("ssm_taps", g), 1)
                return step

            def silu(dve, i, g):
                dve.wait_ge(sem["ssm_tanh"], upto(0, i, g))
                dve_.scalar_tensor_tensor(out=A[g][:, 0:2 * W], in0=Bb[g][:, 0:2 * W], scalar=1.0, in1=A[g][:, 0:2 * W],
                                          op0=ALU.add, op1=ALU.mult)
                for j in range(2):
                    r = slice(j * S0, (j + 1) * S0)
                    ins = dve_.scalar_tensor_tensor(out=Cc[g][0:S0, j * W:(j + 1) * W], in0=Bb[g][r, 2 * W:3 * W], scalar=1.0,
                                                    in1=A[g][r, 2 * W:3 * W], op0=ALU.add, op1=ALU.mult)
                ins.then_inc(sem["ssm_silu"], 1)

            def gate_z(dve, i, g):
                dve.wait_ge(sem["ssm_tz"], upto(0, i, g))
                for b in range(2):
                    ins = dve_.scalar_tensor_tensor(out=gz[g][:, b * W:(b + 1) * W], in0=gz[g][:, b * W:(b + 1) * W],
                                                    scalar=1.0, in1=PS[g][b][:, :], op0=ALU.add, op1=ALU.mult)
                ins.then_inc(sem["ssm_gz"], 1)

            def x_dt(dve, i, g):
                dve.wait_ge(sem["ssm_xt"], upto(0, i, g))
                for b in range(2):
                    ins = dve_.tensor_tensor(
                        xdt[g][:, b * W:(b + 1) * W].rearrange("p (h c) -> p h c", c=P0),
                        PS[g][b][:, :].rearrange("p (h c) -> p h c", c=P0),
                        gsm[g][:, 4, b * 8:b * 8 + 8].unsqueeze(2).to_broadcast([128, 8, P0]), ALU.mult)
                ins.then_inc(sem["ssm_xdt"], 1)

            def m(e):
                def step(dve, i, g):
                    dve.wait_ge(turn("ssm_decay", g), step_at(i, 4, e))
                    b = Bb[g][:, e * W:(e + 1) * W].rearrange("p (h n) -> p h n", h=H0)
                    dve_.tensor_tensor(b, b, PS[g][2][:, e * N:(e + 1) * N].unsqueeze(1).to_broadcast([128, H0, N]), ALU.mult)\
                        .then_inc(turn("ssm_m", g), 1)
                return step

            def y_gate(dve, i, g):
                dve.wait_ge(sem["ssm_y"], upto(0, i, g))
                for b in range(2):
                    ins = dve_.tensor_tensor(Cc[g][:, b * W:(b + 1) * W], PS[g][b][:, :], gz[g][:, b * W:(b + 1) * W], ALU.mult)
                ins.then_inc(sem["ssm_yg"], 1)

            def update(dve, i, g):
                dve.wait_ge(sem["ssm_o"], upto(0, i, g))
                dve.wait_ge(sem["ssm_rstd"], upto(0, i, g))
                dve.wait_ge(sem["ssm_bias"], upto(0, i, g))
                for e in range(GRAPHS):
                    ins = dve_.scalar_tensor_tensor(out=xg(i, g, e), in0=PS[g][0][:, e * N:(e + 1) * N],
                                                    scalar=inv[:, g, e:e + 1], in1=xg(i, g, e),
                                                    op0=ALU.mult, op1=ALU.add)
                ins.then_inc(sem["x_new"], 1)

            return [lambda d, i, g: ln_stats(d, PH_SSM, i, g), lambda d, i, g: ln_moments(d, PH_SSM, i, g),
                           lambda d, i, g: ln_apply(d, PH_SSM, i, g), dt_x, dt_abs, shifted(1), dt_sum, da, shifted(2),
                           shifted(3), silu, gate_z, x_dt, m(0), m(1), m(2), m(3), y_gate, update]

        def ssm_pool():
            def bias(pool, i, g):
                pool.wait_ge(sem["xn_ready"], upto(PH_SSM, i, g))
                pool_.tensor_tensor(xgroup(i, g), xgroup(i, g),
                                    s("b_lin").unsqueeze(1).to_broadcast([128, GRAPHS, C]), ALU.add)\
                    .then_inc(sem["ssm_bias"], 1)

            def tri(pool, i, g):
                pool.wait_ge(sem["ssm_da"], upto(0, i, g))
                for e in range(GRAPHS):
                    ins = pool_.tensor_tensor(
                        tri_d[g][:, e * W:(e + 1) * W].rearrange("p (h n) -> p h n", h=H0),
                        s("after").unsqueeze(1).to_broadcast([128, H0, N]),
                        gsm[g][:, 5, e * H0:(e + 1) * H0].unsqueeze(2).to_broadcast([128, H0, N]), ALU.mult)
                ins.then_inc(sem["ssm_tri"], 1)

            def rms_y(pool, i, g):
                pool.wait_ge(sem["ssm_sq"], upto(0, i, g))
                pool_.tensor_tensor(vare[:, g, :], tot[:, g, 0:GRAPHS], s("eps")[:, 0:GRAPHS], ALU.add)\
                    .then_inc(sem["ssm_ms"], 1)
                pool.wait_ge(sem["ssm_ms"], upto(0, i, g))
                pool_.tensor_tensor(inv[:, g, 0:GRAPHS], vare[:, g, :], s("minus_half")[:, 0:GRAPHS], ALU.pow)\
                    .then_inc(sem["ssm_rstd"], 1)

            return [lambda p, i, g: ln_rstd(p, PH_SSM, i, g), bias, tri, rms_y]

        PH_MHA = 2
        adj_g = [Cc[g][:, W:2 * W].bitcast(I32) for g in range(NG)]
        bias1 = [Cc[g][:, W:2 * W] for g in range(NG)]
        q_odd = [odd_and_o[:, g, 0, :] for g in range(NG)]
        o_cat = [odd_and_o[:, g, 1, :] for g in range(NG)]
        SLOTS = [(j, e, p) for j in range(4) for e in range(2) for p in range(2)]

        def slot(t, n):
            return t[:, n * N:(n + 1) * N]

        def mha_sp(sp, i):
                for g in range(NG):
                    sp.wait_ge(sem["x_new"], x_before(PH_MHA, i, g))
                    sp.dma_start(adj_g[g].rearrange("p (e n) -> p e n", n=N),
                                 adj_dram[:, bass.ds(lin(i, NG * GRAPHS, g * GRAPHS), GRAPHS), :])\
                        .then_inc(turn("mha_adj", g), 16)

        def mha_pe():
            def qkv(pe, i, g):
                all_free(pe, PH_MHA, i, g)
                pe.wait_ge(sem["xnt_ready"], upto(PH_MHA, i, g))
                pe_.matmul(PS[g][1][:, :], s("q1"), xnt[g][:, :], start=True, stop=True)
                pe_.matmul(PS[g][2][:, :], s("k1"), xnt[g][:, :], start=True, stop=True)
                for e in range(GRAPHS):
                    ins = pe_.matmul(slot(PS[g][3], e), slot(xnt[g], e), s("v1"), start=True, stop=True)
                ins.then_inc(sem["mha_qkv"], 1)

            def score(hf):
                def step(pe, i, g):
                    if hf == 0:
                        pe.wait_ge(sem["mha_q"], upto(0, i, g))
                        pe.wait_ge(sem["mha_k"], upto(0, i, g))
                    else:
                        pe.wait_ge(turn("mha_o", g), step_at(i, 2, 0))
                    for e in range(2):
                        for p in range(2):
                            for j in range(4):
                                q = (xn[g][:, :, :].rearrange("p e n -> p (e n)"), q_odd[g])[p]
                                r = slice(32 * j, 32 * j + 32)
                                ins = pe_.matmul(slot(PS[g][j], e * 2 + p), slot(q[r, :], 2 * hf + e),
                                                 slot(xnt[g][r, :], 2 * hf + e), start=True, stop=True)
                    ins.then_inc(turn("mha_score", g), 1)
                return step

            def transpose(hf):
                def step(pe, i, g):
                    pe.wait_ge(turn("mha_exp", g), step_at(i, 2, hf))
                    for n, (j, e, p) in enumerate(SLOTS):
                        ins = pe_.transpose(slot(PS[g][j], e * 2 + p), slot(A[g], n), s("ident"))
                    ins.then_inc(turn("mha_pt", g), 1)
                return step

            def attend(hf):
                def step(pe, i, g):
                    pe.wait_ge(turn("mha_pta", g), step_at(i, 2, hf))
                    pe.wait_ge(turn("mha_ptc", g), step_at(i, 2, hf))
                    for n, (j, e, p) in enumerate(SLOTS):
                        h = 2 * j + p
                        ins = pe_.matmul(PS[g][0][:, e * N + h * DK1:e * N + (h + 1) * DK1], slot(Bb[g], n),
                                         Cc[g][:, (2 * hf + e) * N + h * DK1:(2 * hf + e) * N + (h + 1) * DK1],
                                         start=True, stop=True)
                    ins.then_inc(turn("mha_av", g), 1)
                return step

            def o_transpose(pe, i, g):
                pe.wait_ge(turn("mha_o", g), step_at(i, 2, 1))
                for e in range(GRAPHS):
                    ins = pe_.transpose(slot(PS[g][1], e), slot(o_cat[g], e), s("ident"))
                ins.then_inc(sem["mha_ot"], 1)

            def out_proj(pe, i, g):
                pe.wait_ge(sem["mha_otc"], upto(0, i, g))
                for e in range(GRAPHS):
                    ins = pe_.matmul(slot(PS[g][2], e), slot(A[g], e), s("o1"), start=True, stop=True)
                ins.then_inc(sem["mha_out"], 1)

            return [lambda pe, i, g: xn_transpose(pe, PH_MHA, i, g), qkv, score(0), transpose(0), attend(0),
                          score(1), transpose(1), attend(1), o_transpose, out_proj]

        def mha_act():
            def q_out(act, i, g):
                act.wait_ge(sem["mha_qkv"], upto(0, i, g))
                act_.activation(xn[g][:, :, :].rearrange("p e n -> p (e n)"), PS[g][1][:, :], ACT.Identity,
                                bias=q_fold[:, 1:2], scale=q_fold[:, 0:1])
                act_.activation(q_odd[g], PS[g][1][:, :], ACT.Identity, bias=q_fold[:, 3:4], scale=q_fold[:, 2:3])
                act_.activation(Cc[g][:, 0:W], PS[g][3][:, :], ACT.Copy).then_inc(sem["mha_q"], 1)

            def exps(hf):
                def step(act, i, g):
                    act.wait_ge(turn("mha_t", g), step_at(i, 2, hf))
                    for n in range(16):
                        ins = act_.activation(slot(A[g], n), slot(A[g], n), ACT.Exp, bias=row[:, g, n:n + 1], scale=-1.0,
                                              accum_out=tot[:, g, n:n + 1])
                    ins.then_inc(turn("mha_exp", g), 1)
                return step

            def copy_pt(hf):
                def step(act, i, g):
                    act.wait_ge(turn("mha_pt", g), step_at(i, 2, hf))
                    for j in range(2):
                        ins = act_.activation(Bb[g][:, j * W:(j + 1) * W], PS[g][j][:, :], ACT.Copy)
                    ins.then_inc(turn("mha_pta", g), 1)
                return step

            def copy_ot(act, i, g):
                act.wait_ge(sem["mha_ot"], upto(0, i, g))
                act_.activation(A[g][:, 0:W], PS[g][1][:, :], ACT.Copy).then_inc(sem["mha_otc"], 1)

            return [lambda act, i, g: xnt_copy(act, PH_MHA, i, g), q_out, exps(0), copy_pt(0),
                           exps(1), copy_pt(1), copy_ot]

        def mha_pool():
            def bias(pool, i, g):
                pool.wait_ge(sem["xn_ready"], upto(PH_MHA, i, g))
                pool_.tensor_tensor(xgroup(i, g), xgroup(i, g),
                                    bias_out1[:, :].unsqueeze(1).to_broadcast([128, GRAPHS, C]), ALU.add)\
                    .then_inc(sem["ssm_bias"], 1)

            return [lambda p, i, g: ln_rstd(p, PH_MHA, i, g), bias]

        def mha_dve():
            def bias(dve, i, g):
                dve.wait_ge(turn("mha_adj", g), lin(i, 16, 16))
                dve_.scalar_tensor_tensor(out=bias1[g].rearrange("p (e n) -> p e n", n=N),
                                          in0=adj_g[g].rearrange("p (e n) -> p e n", n=N),
                                          scalar=neg_dist[:, 0:1], in1=maskgroup(i, g), op0=ALU.mult, op1=ALU.add)\
                    .then_inc(sem["mha_bias"], 1)

            def k_out(dve, i, g):
                dve.wait_ge(sem["mha_qkv"], upto(0, i, g))
                dve_.tensor_scalar(xnt[g][:, :], PS[g][2][:, :], s("bk1"), None, ALU.add).then_inc(sem["mha_k"], 1)

            def masked_max(hf):
                def step(dve, i, g):
                    if hf == 0:
                        dve.wait_ge(sem["mha_bias"], upto(0, i, g))
                    dve.wait_ge(turn("mha_score", g), step_at(i, 2, hf))
                    dve_.memset(nothing[:, hf * NG + g:hf * NG + g + 1], 0.0)
                    for n, (j, e, p) in enumerate(SLOTS):
                        ins = dve_.tensor_tensor_reduce(
                            out=slot(A[g], n), in0=slot(PS[g][j], e * 2 + p), in1=slot(bias1[g], 2 * hf + e), scale=-1.0,
                            scalar=3.0e38, op0=ALU.add, op1=ALU.min, accum_out=row[:, g, n:n + 1])
                    ins.then_inc(turn("mha_t", g), 1)
                return step

            def copy_pt(hf):
                def step(dve, i, g):
                    dve.wait_ge(turn("mha_pt", g), step_at(i, 2, hf))
                    for j in range(2, 4):
                        ins = dve_.tensor_copy(Bb[g][:, j * W:(j + 1) * W], PS[g][j][:, :])
                    ins.then_inc(turn("mha_ptc", g), 1)
                    dve_.reciprocal(inv[:, g, :], tot[:, g, :]).then_inc(turn("mha_inv", g), 1)
                return step

            def normalise(hf):
                def step(dve, i, g):
                    dve.wait_ge(turn("mha_av", g), step_at(i, 2, hf))
                    dve.wait_ge(turn("mha_inv", g), step_at(i, 2, hf))
                    for e in range(2):
                        r = inv[:, g, :].rearrange("p (j e k) -> p j e k", j=4, e=2)[:, :, e, :]
                        ins = dve_.tensor_tensor(
                            slot(o_cat[g], 2 * hf + e).rearrange("p (j k d) -> p j k d", j=4, k=2),
                            slot(PS[g][0], e).rearrange("p (j k d) -> p j k d", j=4, k=2),
                            r.unsqueeze(3).to_broadcast([128, 4, 2, DK1]), ALU.mult)
                    ins.then_inc(turn("mha_o", g), 1)
                return step

            def update(dve, i, g):
                dve.wait_ge(sem["mha_out"], upto(0, i, g))
                dve.wait_ge(sem["ssm_bias"], upto(1, i, g))
                dve_.tensor_tensor(xgroup(i, g), PS[g][2][:, :].rearrange("p (e n) -> p e n", n=N), xgroup(i, g), ALU.add)\
                    .then_inc(sem["x_new"], 1)

            return [lambda d, i, g: ln_stats(d, PH_MHA, i, g), lambda d, i, g: ln_moments(d, PH_MHA, i, g),
                           lambda d, i, g: ln_apply(d, PH_MHA, i, g), bias, k_out, masked_max(0), copy_pt(0), normalise(0),
                           masked_max(1), copy_pt(1), normalise(1), update]

        def v3(a, e):
            return a.rearrange("p (g e) -> p g e", e=e)

        def per_graph(a, e):
            return a.unsqueeze(2).to_broadcast([128, GRAPHS, e])

        def gate_chain(before, ops):
            stages = []
            for n, (op, also) in enumerate(ops):
                def step(dve, i, g, n=n, op=op, also=also):
                    if n:
                        dve.wait_ge(turn("gate_step", g), gate_at(before, len(ops), i, g, n - 1))
                    for other, k in also:
                        dve.wait_ge(sem[other], upto(k, i, g))
                    op(i, g).then_inc(turn("gate_step", g), 1)
                stages.append(step)
            return stages

        def gate_at(before, count, i, g, n):
            return lin(i, count, ITER * before + n + 1)

        def softmax_ops(logits, bias, e):
            z = slice(0, GRAPHS * e)
            ops = []
            if bias is not None:
                ops.append(lambda i, g: dve_.tensor_tensor(v3(gsm[g][:, 0, z], e), v3(logits(g), e),
                                                           s(bias).unsqueeze(1).to_broadcast([128, GRAPHS, e]), ALU.add))
            else:
                ops.append(lambda i, g: dve_.tensor_copy(gsm[g][:, 0, z], logits(g)))
            ops.append(lambda i, g: dve_.tensor_reduce(gsm[g][:, 1, 0:GRAPHS], v3(gsm[g][:, 0, z], e), AX.X, ALU.max))
            ops.append(lambda i, g: dve_.tensor_tensor(v3(gsm[g][:, 2, z], e), v3(gsm[g][:, 0, z], e),
                                                       per_graph(gsm[g][:, 1, 0:GRAPHS], e), ALU.subtract))
            return ops

        def first_of_max_ops(src, top, eq, cand, best, sel, rank, e):
            z = slice(0, GRAPHS * e)
            return [
                lambda i, g: dve_.tensor_reduce(gsm[g][:, top, 0:GRAPHS], v3(gsm[g][:, src, z], e), AX.X, ALU.max),
                lambda i, g: dve_.tensor_tensor(v3(gsm[g][:, eq, z], e), v3(gsm[g][:, src, z], e),
                                                per_graph(gsm[g][:, top, 0:GRAPHS], e), ALU.is_equal),
                lambda i, g: dve_.tensor_tensor(v3(gsm[g][:, cand, z], e), v3(gsm[g][:, eq, z], e),
                                                s(rank).unsqueeze(1).to_broadcast([128, GRAPHS, e]), ALU.mult),
                lambda i, g: dve_.tensor_reduce(gsm[g][:, best, 0:GRAPHS], v3(gsm[g][:, cand, z], e), AX.X, ALU.max),
                lambda i, g: dve_.tensor_tensor(v3(gsm[g][:, sel, z], e), v3(gsm[g][:, cand, z], e),
                                                per_graph(gsm[g][:, best, 0:GRAPHS], e), ALU.is_equal),
            ]

        def probability_ops(e):
            z = slice(0, GRAPHS * e)
            return [
                lambda i, g: dve_.tensor_reduce(gsm[g][:, 5, 0:GRAPHS], v3(gsm[g][:, 3, z], e), AX.X, ALU.add),
                lambda i, g: dve_.reciprocal(gsm[g][:, 6, 0:GRAPHS], gsm[g][:, 5, 0:GRAPHS]),
                lambda i, g: dve_.tensor_tensor(v3(gsm[g][:, 4, z], e), v3(gsm[g][:, 3, z], e),
                                                per_graph(gsm[g][:, 6, 0:GRAPHS], e), ALU.mult),
            ]

        def rest_op(e):
            z = slice(0, GRAPHS * e)
            return [lambda i, g: dve_.scalar_tensor_tensor(out=gsm[g][:, 7, z], in0=gsm[g][:, 8, z], scalar=-2.0,
                                                           in1=gsm[g][:, 4, z], op0=ALU.mult, op1=ALU.add)]

        PH_ONE = 3
        GE1 = GRAPHS * E1
        one_ops = [[op, []] for op in softmax_ops(lambda g: PS[g][0][:, 0:GE1], "b_gate1", E1)]
        one_ops[0][1] = [("gate_logit", 0)]
        ONE_SUB = len(one_ops) - 1
        one_ops += [[op, []] for op in first_of_max_ops(0, 7, 8, 9, 10, 11, "rank8", E1)]
        one_ops += [[op, []] for op in probability_ops(E1)[0:2]]
        one_ops[-2][1] = [("gate_exp", 0)]
        one_ops += [[lambda i, g: dve_.tensor_tensor(v3(gsm[g][:, 12, 0:GE1], E1), v3(gsm[g][:, 11, 0:GE1], E1),
                                                     per_graph(gsm[g][:, 6, 0:GRAPHS], E1), ALU.mult), []]]
        ONE_N = len(one_ops)

        def hidden_high(g, j):
            return (C_r[g][:, W:2 * W], xn_r[g], odd_and_o_r[:, 2 * g * W:(2 * g + 1) * W],
                    odd_and_o_r[:, (2 * g + 1) * W:(2 * g + 2) * W])[j]

        def split_down1(dve):
            dve.wait_ge(sem["loaded_down1"], 16)
            dve_.tensor_copy(down1_high, down1).then_inc(sem["one_w"], 1)
            dve.wait_ge(sem["one_w"], 1)
            dve_.tensor_tensor(down1_low, down1, down1_high.bitcast(F32), ALU.subtract).then_inc(sem["one_w"], 1)

        def one_pe():
            def up(pe, i, g):
                pe.wait_ge(sem["xnt_ready"], upto(PH_ONE, i, g))
                for j in range(4):
                    ins = pe_.matmul(PS[g][j][:, :], s("up1")[:, j * 128:(j + 1) * 128], xnt[g][:, :], start=True, stop=True)
                ins.then_inc(sem["one_h"], 1)

            def logit(pe, i, g):
                pe.wait_ge(sem["one_act"], upto(0, i, g))
                for e in range(GRAPHS):
                    for j in range(4):
                        ins = pe_.matmul(PS[g][0][:, e * E1:(e + 1) * E1], A[g][:, j * W + e * N:j * W + (e + 1) * N],
                                         s("gate1")[:, j * E1:(j + 1) * E1], start=j == 0, stop=j == 3)
                ins.then_inc(sem["gate_logit"], 1)

            def gate_t(pe, i, g):
                pe.wait_ge(turn("gate_step", g), gate_at(0, ONE_N, i, g, ONE_N - 1))
                pe_.transpose(PS[g][1][0:GE1, 0:N], gsm[g][:, 12, 0:GE1], s("ident")).then_inc(sem["gate_gt"], 1)

            def down_bias(pe, i, g):
                pe.wait_ge(sem["gate_gtc"], upto(0, i, g))
                pe_.matmul(PS[g][0][:, :], Cc[g][0:GE1, 0:N], s("b_down1")[0:GE1, :], start=True, stop=True)\
                    .then_inc(sem["one_bd"], 1)

            def down(e):
                def step(pe, i, g):
                    if e == 0:
                        pe.wait_ge(sem["one_w"], 2)
                        pe.wait_ge(sem["one_low"], upto(0, i, g))
                    if e == 1:
                        pe.wait_ge(sem["one_xb"], upto(0, i, g))
                    if e >= 2:
                        pe.wait_ge(turn("expert_gated", g), step_at(i, 4, e - 2))
                    for b in range(2):
                        for j in range(4):
                            high, low = slot(hidden_high(g, j), e), slot(A_r[g], j * 4 + e)
                            parts = ((high, down1_high), (high, down1_low), (low, down1_high))
                            for n, (h, w) in enumerate(parts):
                                ins = pe_.matmul(PS[g][(2, 0)[e % 2] + b][:, :], h,
                                                 w[:, j * 2 * W + b * W:j * 2 * W + (b + 1) * W],
                                                 start=j == 0 and n == 0, stop=j == 3 and n == 2)
                    ins.then_inc(turn("expert_y", g), 1)
                return step

            return [lambda pe, i, g: xn_transpose(pe, PH_ONE, i, g), up, logit, down(0), gate_t, down_bias,
                          down(1), down(2), down(3)]

        def one_act():
            def gelu(act, i, g):
                act.wait_ge(sem["one_h"], upto(0, i, g))
                for j in range(4):
                    ins = act_.activation(A[g][:, j * W:(j + 1) * W], PS[g][j][:, :], ACT.Gelu, bias=s("b_up1")[:, j:j + 1])
                ins.then_inc(sem["one_act"], 1)

            def gate_exp(act, i, g):
                act.wait_ge(turn("gate_step", g), gate_at(0, ONE_N, i, g, ONE_SUB))
                act_.activation(gsm[g][:, 3, 0:GE1], gsm[g][:, 2, 0:GE1], ACT.Exp).then_inc(sem["gate_exp"], 1)

            def copy_gt(act, i, g):
                act.wait_ge(sem["gate_gt"], upto(0, i, g))
                act_.activation(Cc[g][0:GE1, 0:N], PS[g][1][0:GE1, 0:N], ACT.Copy).then_inc(sem["gate_gtc"], 1)

            return [lambda act, i, g: xnt_copy(act, PH_ONE, i, g), gelu, gate_exp, copy_gt]

        def gated(dve, before, g, e, i, banks, gate, buf, free):
            if free:
                dve.wait_ge(turn(free[0], g), free[1])
            dve.wait_ge(turn("expert_y", g), step_at(i, 4, e, before))
            for b, bank in enumerate(banks):
                ins = dve_.tensor_tensor(buf[:, b * W:(b + 1) * W].rearrange("p (x n) -> p x n", n=N),
                                         PS[g][bank][:, :].rearrange("p (x n) -> p x n", n=N),
                                         gate[:, b * 4:b * 4 + 4].unsqueeze(2).to_broadcast([128, 4, N]), ALU.mult)
            ins.then_inc(turn("expert_gated", g), 1)

        def one_dve():
            def add_bias(dve, i, g):
                dve.wait_ge(sem["one_bd"], upto(0, i, g))
                dve_.tensor_tensor(xgroup(i, g), PS[g][0][:, :].rearrange("p (e n) -> p e n", n=N), xgroup(i, g), ALU.add)\
                    .then_inc(sem["one_xb"], 1)

            def gate_y(e):
                def step(dve, i, g):
                    free = ("expert_sum", lin(i, 16, (e - 2) * 4 + 4)) if e >= 2 or not first(i) else None
                    gated(dve, 0, g, e, i, ((2, 3), (0, 1))[e % 2],
                          gsm[g][:, 12, e * E1:(e + 1) * E1], Bb[g][:, e % 2 * 1024:e % 2 * 1024 + 1024], free)
                return step

            def split_high(dve, i, g):
                dve.wait_ge(sem["one_act"], upto(0, i, g))
                for j in range(4):
                    ins = dve_.tensor_copy(hidden_high(g, j), A[g][:, j * W:(j + 1) * W])
                ins.then_inc(sem["one_high"], 1)

            def split_low(dve, i, g):
                dve.wait_ge(sem["one_high"], upto(0, i, g))
                dve.wait_ge(sem["gate_logit"], upto(0, i, g))
                for j in range(4):
                    ins = dve_.tensor_tensor(A_r[g][:, j * W:(j + 1) * W], A[g][:, j * W:(j + 1) * W],
                                             hidden_high(g, j).bitcast(F32), ALU.subtract)
                ins.then_inc(sem["one_low"], 1)

            return ([lambda d, i, g: ln_stats(d, PH_ONE, i, g), lambda d, i, g: ln_moments(d, PH_ONE, i, g),
                    lambda d, i, g: ln_apply(d, PH_ONE, i, g), split_high, split_low] + gate_chain(0, one_ops)
                    + [add_bias, gate_y(0), gate_y(1), gate_y(2), gate_y(3)])

        def one_pool():
            def add_up(e):
                def step(pool, i, g):
                    t = Bb[g][:, e % 2 * 1024:e % 2 * 1024 + 1024]
                    if e == 0:
                        pool.wait_ge(sem["one_xb"], upto(0, i, g))
                    pool.wait_ge(turn("expert_gated", g), step_at(i, 4, e))
                    for n, half in enumerate((512, 256, 128)):
                        pool_.tensor_tensor(t[:, 0:half], t[:, 0:half], t[:, half:2 * half], ALU.add)\
                            .then_inc(turn("expert_sum", g), 1)
                        pool.wait_ge(turn("expert_sum", g), step_at(i, 16, e * 4 + n))
                    ins = pool_.tensor_tensor(xg(i, g, e), xg(i, g, e), t[:, 0:C], ALU.add)
                    ins.then_inc(turn("expert_sum", g), 1)
                    if e == GRAPHS - 1:
                        pool.wait_ge(turn("expert_sum", g), step_at(i, 16, e * 4 + 3))
                        pool.sem_inc(sem["x_new"], 1)
                return step

            return [lambda p, i, g: ln_rstd(p, PH_ONE, i, g), add_up(0), add_up(1), add_up(2), add_up(3)]

        PH_TWO = 5
        GE2 = GRAPHS * E2
        two_ops = [[op, []] for op in softmax_ops(lambda g: PS[g][0][:, 0:GE2], "b_gate2", E2)]
        two_ops[0][1] = [("gate_logit", 1)]
        TWO_SUB = len(two_ops) - 1
        two_ops += [[op, []] for op in probability_ops(E2)]
        two_ops[TWO_SUB + 1][1] = [("gate_exp", 1)]
        two_ops += [[op, []] for op in first_of_max_ops(4, 9, 10, 11, 12, 8, "rank4", E2) + rest_op(E2)
                    + first_of_max_ops(7, 13, 10, 11, 12, 2, "rank4", E2)]
        two_ops += [[lambda i, g: dve_.tensor_tensor(gsm[g][:, 5, 0:4], gsm[g][:, 13, 0:4], gsm[g][:, 9, 0:4], ALU.subtract), []]]
        TWO_SUB2 = len(two_ops) - 1
        two_ops += [
            [lambda i, g: dve_.tensor_scalar(gsm[g][:, 10, 0:4], gsm[g][:, 6, 0:4], 1.0, None, ALU.add), [("two_exp2", 0)]],
            [lambda i, g: dve_.reciprocal(gsm[g][:, 11, 0:4], gsm[g][:, 10, 0:4]), []],
            [lambda i, g: dve_.tensor_tensor(gsm[g][:, 12, 0:4], gsm[g][:, 11, 0:4], gsm[g][:, 6, 0:4], ALU.mult), []],
            [lambda i, g: dve_.tensor_tensor(v3(gsm[g][:, 0, 0:GE2], E2), v3(gsm[g][:, 8, 0:GE2], E2),
                                             per_graph(gsm[g][:, 11, 0:4], E2), ALU.mult), []],
            [lambda i, g: dve_.tensor_tensor(v3(gsm[g][:, 1, 0:GE2], E2), v3(gsm[g][:, 2, 0:GE2], E2),
                                             per_graph(gsm[g][:, 12, 0:4], E2), ALU.mult), []],
            [lambda i, g: dve_.tensor_tensor(gsm[g][:, 3, 0:GE2], gsm[g][:, 0, 0:GE2], gsm[g][:, 1, 0:GE2], ALU.add), []],
        ]
        TWO_N = len(two_ops)
        NETS = range(1 + E2)

        def h1_bank(q):
            return 1 + 2 * (q % 2)

        def net_at(i, g, q):
            return step_at(i, 5, q)

        def two_pe():
            def logit(pe, i, g):
                all_free(pe, PH_TWO, i, g)
                pe.wait_ge(sem["xnt_ready"], upto(PH_TWO, i, g))
                for e in range(GRAPHS):
                    ins = pe_.matmul(PS[g][0][:, e * E2:(e + 1) * E2], slot(xnt[g], e), s("gate2"), start=True, stop=True)
                ins.then_inc(sem["gate_logit"], 1)

            def hidden1(q):
                def step(pe, i, g):
                    if q >= 2:
                        pe.wait_ge(turn("two_h1c", g), net_at(i, g, q - 2))
                    w = s("s1") if q == 0 else s("e1")[:, (q - 1) * 128:q * 128]
                    pe_.matmul(PS[g][h1_bank(q)][:, :], w, xnt[g][:, :], start=True, stop=True).then_inc(turn("two_h1", g), 1)
                return step

            def hidden2(q):
                def step(pe, i, g):
                    pe.wait_ge(turn("two_h1c", g), net_at(i, g, q))
                    if q:
                        pe.wait_ge(turn("two_h2c", g), net_at(i, g, q - 1))
                    w = s("s2") if q == 0 else s("e2")[:, (q - 1) * EH2:q * EH2]
                    m = 128 if q == 0 else EH2
                    pe_.matmul(PS[g][2][0:m, :], w, A[g][:, q % 2 * W:(q % 2 + 1) * W], start=True, stop=True)\
                        .then_inc(turn("two_h2", g), 1)
                return step

            def gate_t(pe, i, g):
                pe.wait_ge(turn("gate_step", g), gate_at(ONE_N, TWO_N, i, g, TWO_N - 1))
                pe_.transpose(PS[g][0][0:GE2, 0:N], gsm[g][:, 3, 0:GE2], s("ident")).then_inc(sem["gate_gt"], 1)

            def shared_out(pe, i, g):
                pe.wait_ge(sem["gate_gtc"], upto(1, i, g))
                pe.wait_ge(turn("two_h2c", g), net_at(i, g, 0))
                pe_.matmul(PS[g][0][:, :], Cc[g][0:GE2, W:W + N], s("eb3")[0:GE2, :], start=True, stop=False)
                for e in range(GRAPHS):
                    ins = pe_.matmul(slot(PS[g][0], e), Cc[g][:, e * N:(e + 1) * N], s("s3"), start=False, stop=e == GRAPHS - 1)
                ins.then_inc(sem["two_sh"], 1)

            def expert_out(e):
                bank = (1, 2, 3, 1)[e]

                def step(pe, i, g):
                    if e == 0:
                        pe.wait_ge(turn("two_h2c", g), net_at(i, g, E2))
                    if e == 3:
                        pe.wait_ge(turn("expert_gated", g), step_at(i, 4, 0, ITER * 4))
                    for q in range(E2):
                        ins = pe_.matmul(slot(PS[g][bank], q), Bb[g][0:EH2, q * W + e * N:q * W + (e + 1) * N],
                                         s("e3")[0:EH2, q * 128:(q + 1) * 128], start=True, stop=True)
                    ins.then_inc(turn("expert_y", g), 1)
                return step

            return [lambda pe, i, g: xn_transpose(pe, PH_TWO, i, g), logit, hidden1(0), hidden1(1), hidden2(0),
                          hidden1(2), hidden2(1), hidden1(3), hidden2(2), hidden1(4), hidden2(3), hidden2(4),
                          gate_t, shared_out, expert_out(0), expert_out(1), expert_out(2), expert_out(3)]

        def two_act():
            def relu1(q):
                def step(act, i, g):
                    act.wait_ge(turn("two_h1", g), net_at(i, g, q))
                    if q >= 2:
                        act.wait_ge(turn("two_h2", g), net_at(i, g, q - 2))
                    b = s("sb1") if q == 0 else s("eb1")[:, q - 1:q]
                    act_.activation(A[g][:, q % 2 * W:(q % 2 + 1) * W], PS[g][h1_bank(q)][:, :], ACT.Relu, bias=b)\
                        .then_inc(turn("two_h1c", g), 1)
                return step

            def gate_exp(act, i, g):
                act.wait_ge(turn("gate_step", g), gate_at(ONE_N, TWO_N, i, g, TWO_SUB))
                act_.activation(gsm[g][:, 3, 0:GE2], gsm[g][:, 2, 0:GE2], ACT.Exp).then_inc(sem["gate_exp"], 1)

            def gate_exp2(act, i, g):
                act.wait_ge(turn("gate_step", g), gate_at(ONE_N, TWO_N, i, g, TWO_SUB2))
                act_.activation(gsm[g][:, 6, 0:4], gsm[g][:, 5, 0:4], ACT.Exp).then_inc(sem["two_exp2"], 1)

            def copy_gt(act, i, g):
                act.wait_ge(sem["gate_gt"], upto(1, i, g))
                act_.activation(Cc[g][0:GE2, W:W + N], PS[g][0][0:GE2, 0:N], ACT.Copy).then_inc(sem["gate_gtc"], 1)

            return [lambda act, i, g: xnt_copy(act, PH_TWO, i, g), relu1(0), relu1(1), gate_exp, relu1(2), relu1(3),
                           relu1(4), gate_exp2, copy_gt]

        def two_dve():
            def relu2(q):
                def step(dve, i, g):
                    dve.wait_ge(turn("two_h2", g), net_at(i, g, q))
                    m = 128 if q == 0 else EH2
                    b = s("sb2") if q == 0 else s("eb2")[0:m, q - 1:q]
                    o = Cc[g][:, 0:W] if q == 0 else Bb[g][0:m, (q - 1) * W:q * W]
                    dve_.tensor_scalar(o, PS[g][2][0:m, :], b, 0.0, ALU.add, ALU.max).then_inc(turn("two_h2c", g), 1)
                return step

            def add_shared(dve, i, g):
                dve.wait_ge(sem["two_sh"], upto(0, i, g))
                dve_.tensor_tensor(xgroup(i, g), PS[g][0][:, :].rearrange("p (e n) -> p e n", n=N), xgroup(i, g), ALU.add)\
                    .then_inc(sem["two_xs"], 1)

            def gate_y(e):
                def step(dve, i, g):
                    gated(dve, ITER * 4, g, e, i, ((1, 2, 3, 1)[e],), gsm[g][:, 3, e * E2:(e + 1) * E2],
                          A[g][:, e * W:(e + 1) * W], None)
                return step

            chain = gate_chain(ONE_N, two_ops)
            steps = [lambda d, i, g: ln_stats(d, PH_TWO, i, g), lambda d, i, g: ln_moments(d, PH_TWO, i, g),
                     lambda d, i, g: ln_apply(d, PH_TWO, i, g)] + chain[0:TWO_SUB + 1] + [relu2(0)]
            rest = chain[TWO_SUB + 1:]
            until_exp = TWO_SUB2 - TWO_SUB
            cuts = [until_exp * q // 3 for q in range(4)]
            for q in range(1, 4):
                steps += [relu2(q)] + rest[cuts[q - 1]:cuts[q]]
            steps += [relu2(4)] + rest[until_exp:]
            steps += [add_shared, gate_y(0), gate_y(1), gate_y(2), gate_y(3)]
            return steps

        def two_pool():
            def add_up(e):
                def step(pool, i, g):
                    t = A[g][:, e * W:(e + 1) * W]
                    if e == 0:
                        pool.wait_ge(sem["two_xs"], upto(0, i, g))
                    pool.wait_ge(turn("expert_gated", g), step_at(i, 4, e, ITER * 4))
                    for n, half in enumerate((256, 128)):
                        pool_.tensor_tensor(t[:, 0:half], t[:, 0:half], t[:, half:2 * half], ALU.add)\
                            .then_inc(turn("expert_sum", g), 1)
                        pool.wait_ge(turn("expert_sum", g), step_at(i, 12, e * 3 + n, ITER * 16))
                    pool_.tensor_tensor(xg(i, g, e), xg(i, g, e), t[:, 0:C], ALU.add).then_inc(turn("expert_sum", g), 1)
                    if e == GRAPHS - 1:
                        pool.wait_ge(turn("expert_sum", g), step_at(i, 12, e * 3 + 2, ITER * 16))
                        pool.sem_inc(sem["x_new"], 1)
                return step

            return [lambda p, i, g: ln_rstd(p, PH_TWO, i, g), add_up(0), add_up(1), add_up(2), add_up(3)]

        PH_AT = 7
        GE3 = GRAPHS * E3
        at_ops = [[op, []] for op in softmax_ops(lambda g: PS[g][0][:, 0:GE3], None, E3)]
        at_ops[0][1] = [("gate_logit", 2)]
        AT_SUB = len(at_ops) - 1
        at_ops += [[op, []] for op in probability_ops(E3)]
        at_ops[AT_SUB + 1][1] = [("gate_exp", 2)]
        at_ops += [[op, []] for op in first_of_max_ops(4, 9, 10, 11, 12, 8, "rank8", E3) + rest_op(E3)
                   + first_of_max_ops(7, 13, 10, 11, 12, 2, "rank8", E3)]
        at_ops += [
            [lambda i, g: dve_.scalar_tensor_tensor(out=gsm[g][:, 5, 0:4], in0=gsm[g][:, 9, 0:4], scalar=1e-9,
                                                    in1=gsm[g][:, 13, 0:4], op0=ALU.add, op1=ALU.add), []],
            [lambda i, g: dve_.reciprocal(gsm[g][:, 6, 0:4], gsm[g][:, 5, 0:4]), []],
            [lambda i, g: dve_.tensor_tensor(gsm[g][:, 0, 0:GE3], gsm[g][:, 8, 0:GE3], gsm[g][:, 2, 0:GE3], ALU.add), []],
            [lambda i, g: dve_.tensor_tensor(gsm[g][:, 1, 0:GE3], gsm[g][:, 0, 0:GE3], gsm[g][:, 4, 0:GE3], ALU.mult), []],
            [lambda i, g: dve_.tensor_tensor(v3(weights3[:, bass.ds(lin(i, NG * GE3, g * GE3), GE3)], E3),
                                             v3(gsm[g][:, 1, 0:GE3], E3), per_graph(gsm[g][:, 6, 0:4], E3), ALU.mult),
             [("at_xadd", 0), ("at_store", 0)]],
        ]
        AT_N = len(at_ops)

        def at_pe():
            def rope_in(pe, i, g):
                pe.wait_ge(sem["xnt_ready"], upto(PH_AT, i, g))
                for b, w in enumerate(("q3", "q3r", "k3", "k3r")):
                    ins = pe_.matmul(PS[g][b][:, :], s(w), xnt[g][:, :], start=True, stop=True)
                ins.then_inc(sem["at_rope"], 1)

            def v_in(pe, i, g):
                pe.wait_ge(sem["at_ropem"], upto(0, i, g))
                for e in range(GRAPHS):
                    ins = pe_.matmul(PS[g][0][:, e * 64:(e + 1) * 64], slot(xnt[g], e), s("v3"), start=True, stop=True)
                ins.then_inc(sem["at_v"], 1)

            def score(pe, i, g):
                pe.wait_ge(sem["at_qk"], upto(0, i, g))
                pe.wait_ge(sem["at_vc"], upto(0, i, g))
                for h in range(NH3):
                    pe_.matmul(PS[g][h][:, :].rearrange("p (e n) -> p e n", n=N), ident_bf[:, :],
                               future_bf[:, :].unsqueeze(1).to_broadcast([128, GRAPHS, N]), start=True, stop=False)
                for e in range(GRAPHS):
                    for h in range(NH3):
                        r = slice(32 * h, 32 * h + 32)
                        ins = pe_.matmul(slot(PS[g][h], e), Bb[g][r, e * N:(e + 1) * N], Bb[g][r, W + e * N:W + (e + 1) * N],
                                         start=False, stop=e == GRAPHS - 1)
                ins.then_inc(sem["gat_score"], 1)

            def transpose(pe, i, g):
                pe.wait_ge(sem["gat_exp"], upto(3, i, g))
                for h in range(NH3):
                    for e in range(GRAPHS):
                        ins = pe_.transpose(slot(PS[g][h], e), slot(A[g], h * 4 + e), s("ident"))
                ins.then_inc(sem["gat_pt"], 1)

            def attend(pe, i, g):
                pe.wait_ge(sem["at_pta"], upto(0, i, g))
                pe.wait_ge(sem["gat_ptc"], upto(3, i, g))
                for h in range(NH3):
                    for e in range(GRAPHS):
                        ins = pe_.matmul(PS[g][0][:, e * N + h * HD3:e * N + (h + 1) * HD3], slot(Bb[g], h * 4 + e),
                                         Cc[g][:, W + e * 64 + h // 2 * HD3:W + e * 64 + (h // 2 + 1) * HD3],
                                         start=True, stop=True)
                ins.then_inc(sem["at_av"], 1)

            def y_transpose(pe, i, g):
                pe.wait_ge(sem["at_y"], upto(0, i, g))
                for e in range(GRAPHS):
                    ins = pe_.transpose(slot(PS[g][1], e), xn[g][:, e, :], s("ident"))
                ins.then_inc(sem["at_yt"], 1)

            def out_proj(pe, i, g):
                pe.wait_ge(sem["at_ytc"], upto(0, i, g))
                for e in range(GRAPHS):
                    ins = pe_.matmul(slot(PS[g][2], e), slot(xnt[g], e), s("o3"), start=True, stop=True)
                ins.then_inc(sem["at_o"], 1)

            def f_transpose(pe, i, g):
                pe.wait_ge(sem["at_f"], upto(0, i, g))
                for e in range(GRAPHS):
                    ins = pe_.transpose(slot(PS[g][3], e), slot(A[g], e), s("ident"))
                ins.then_inc(sem["at_ft"], 1)

            def router(pe, i, g):
                pe.wait_ge(sem["at_ftc"], upto(0, i, g))
                for e in range(GRAPHS):
                    ins = pe_.matmul(PS[g][0][:, e * E3:(e + 1) * E3], slot(xnt[g], e), s("router3"), start=True, stop=True)
                ins.then_inc(sem["gate_logit"], 1)

            return [lambda pe, i, g: xn_transpose(pe, PH_AT, i, g), rope_in, v_in, score, transpose, attend,
                          y_transpose, out_proj, f_transpose, router]

        def at_act():
            def copy_v(act, i, g):
                act.wait_ge(sem["at_v"], upto(0, i, g))
                act_.activation(Cc[g][:, W:W + 256], PS[g][0][:, 0:256], ACT.Copy).then_inc(sem["at_vc"], 1)

            def exps(act, i, g):
                act.wait_ge(sem["at_nmax"], upto(0, i, g))
                for h in range(NH3):
                    for e in range(GRAPHS):
                        n = h * 4 + e
                        ins = act_.activation(slot(A[g], n), slot(PS[g][h], e), ACT.Exp, bias=neg_row[:, g, n:n + 1],
                                              scale=SCALE3, accum_out=tot[:, g, n:n + 1])
                ins.then_inc(sem["gat_exp"], 1)

            def copy_pt(act, i, g):
                act.wait_ge(sem["gat_pt"], upto(3, i, g))
                for h in range(2):
                    ins = act_.activation(Bb[g][:, h * W:(h + 1) * W], PS[g][h][:, :], ACT.Copy)
                ins.then_inc(sem["at_pta"], 1)

            def copy_yt(act, i, g):
                act.wait_ge(sem["at_yt"], upto(0, i, g))
                act_.activation(xnt[g][:, :], PS[g][1][:, :], ACT.Copy).then_inc(sem["at_ytc"], 1)

            def square(act, i, g):
                act.wait_ge(sem["at_x1"], upto(0, i, g))
                for e in range(GRAPHS):
                    ins = act_.activation(slot(Bb[g], e), xn[g][:, e, :], ACT.Square, accum_out=tot[:, g, e:e + 1])
                ins.then_inc(sem["at_sq"], 1)

            def copy_ft(act, i, g):
                act.wait_ge(sem["at_ft"], upto(0, i, g))
                act_.activation(xnt[g][:, :], PS[g][3][:, :], ACT.Copy).then_inc(sem["at_ftc"], 1)

            def gate_exp(act, i, g):
                act.wait_ge(turn("gate_step", g), gate_at(ONE_N + TWO_N, AT_N, i, g, AT_SUB))
                act_.activation(gsm[g][:, 3, 0:GE3], gsm[g][:, 2, 0:GE3], ACT.Exp).then_inc(sem["gate_exp"], 1)

            return [lambda act, i, g: xnt_copy(act, PH_AT, i, g), copy_v, exps, copy_pt, copy_yt, square, copy_ft,
                           gate_exp]

        def at_dve():
            def norms(dve, i, g):
                dve.wait_ge(turn("at_rms", g), step_at(i, 5, 4))
                for e in range(GRAPHS):
                    dve_.tensor_scalar(slot(Cc[g], e), xg(i, g, e), moments[:, g, e, 0:1], rstd[:, g, e:e + 1],
                                       ALU.subtract, ALU.mult)
                    ins = dve_.tensor_scalar(xn[g][:, e, :], xg(i, g, e), moments[:, g, e, 0:1], rms[:, g, 3, e:e + 1],
                                             ALU.subtract, ALU.mult)
                ins.then_inc(sem["xn_ready"], 1)

            def rope(dve, i, g):
                dve.wait_ge(sem["at_rope"], upto(0, i, g))
                for b in range(4):
                    table = s("cos") if b % 2 == 0 else s("sin")
                    ins = dve_.tensor_tensor(A[g][:, b * W:(b + 1) * W].rearrange("p (e n) -> p e n", n=N),
                                             PS[g][b][:, :].rearrange("p (e n) -> p e n", n=N),
                                             table.unsqueeze(1).to_broadcast([128, GRAPHS, N]), ALU.mult)
                ins.then_inc(sem["at_ropem"], 1)

            def row_max(dve, i, g):
                dve.wait_ge(sem["gat_score"], upto(3, i, g))
                for h in range(NH3):
                    ins = dve_.tensor_reduce(row[:, g, h * 4:h * 4 + 4], PS[g][h][:, :].rearrange("p (e n) -> p e n", n=N),
                                             AX.X, ALU.max)
                ins.then_inc(sem["gat_max"], 1)

            def copy_pt(dve, i, g):
                dve.wait_ge(sem["gat_pt"], upto(3, i, g))
                for h in range(2, 4):
                    ins = dve_.tensor_copy(Bb[g][:, h * W:(h + 1) * W], PS[g][h][:, :])
                ins.then_inc(sem["gat_ptc"], 1)
                dve_.reciprocal(inv[:, g, :], tot[:, g, :]).then_inc(sem["gat_inv"], 1)

            def normalise(dve, i, g):
                dve.wait_ge(sem["at_av"], upto(0, i, g))
                dve.wait_ge(sem["gat_inv"], upto(3, i, g))
                dve_.tensor_tensor(xn[g][:, :, :].rearrange("p e (h d) -> p e h d", h=NH3),
                                   PS[g][0][:, :].rearrange("p (e h d) -> p e h d", e=GRAPHS, h=NH3),
                                   inv[:, g, :].rearrange("p (h e) -> p e h", h=NH3).unsqueeze(3)
                                   .to_broadcast([128, GRAPHS, NH3, HD3]), ALU.mult).then_inc(sem["at_y"], 1)

            def x1(dve, i, g):
                dve.wait_ge(sem["at_o"], upto(0, i, g))
                dve_.tensor_tensor(xn[g][:, :, :].rearrange("p e n -> p (e n)"), PS[g][2][:, :], Cc[g][:, 0:W], ALU.add)\
                    .then_inc(sem["at_x1"], 1)

            def f(dve, i, g):
                dve.wait_ge(sem["at_rstd"], upto(0, i, g))
                for e in range(GRAPHS):
                    ins = dve_.tensor_scalar(slot(A[g], e), xn[g][:, e, :], rstd[:, g, e:e + 1], float(C) ** 0.5,
                                             ALU.mult, ALU.mult)
                ins.then_inc(sem["at_f"], 1)

            def finish(dve, i, g):
                dve.wait_ge(turn("gate_step", g), gate_at(ONE_N + TWO_N, AT_N, i, g, 0))
                dve.wait_ge(sem["at_xadd"], upto(0, i, g))
                dve.wait_ge(sem["at_store"], upto(0, i, g))
                dve.sem_inc(sem["x_new"], 1)

            at_gate = gate_chain(ONE_N + TWO_N, at_ops)
            return [lambda d, i, g: ln_stats(d, PH_AT, i, g), lambda d, i, g: ln_moments(d, PH_AT, i, g), norms,
                           rope, row_max, copy_pt, normalise, x1, f] + at_gate[0:1] + [finish] + at_gate[1:]

        def at_pool():
            def rms_of_ln(pool, i, g):
                pool.wait_ge(sem["ln_rstd"], upto(PH_AT, i, g))
                pool_.tensor_tensor(rms[:, g, 0, :], rstd[:, g, :], rstd[:, g, :], ALU.mult).then_inc(turn("at_rms", g), 1)
                pool.wait_ge(turn("at_rms", g), step_at(i, 5, 0))
                pool_.tensor_tensor(rms[:, g, 1, :], rms[:, g, 0, :], moments[:, g, :, 1], ALU.mult).then_inc(turn("at_rms", g), 1)
                pool.wait_ge(turn("at_rms", g), step_at(i, 5, 1))
                pool_.tensor_tensor(rms[:, g, 2, :], rms[:, g, 1, :], s("eps")[:, GRAPHS:2 * GRAPHS], ALU.add).then_inc(turn("at_rms", g), 1)
                pool.wait_ge(turn("at_rms", g), step_at(i, 5, 2))
                pool_.tensor_tensor(rms[:, g, 0, :], rms[:, g, 2, :], s("minus_half")[:, 0:GRAPHS], ALU.pow)\
                    .then_inc(turn("at_rms", g), 1)
                pool.wait_ge(turn("at_rms", g), step_at(i, 5, 3))
                pool_.tensor_tensor(rms[:, g, 3, :], rms[:, g, 0, :], rstd[:, g, :], ALU.mult).then_inc(turn("at_rms", g), 1)

            def add_rope(pool, i, g):
                pool.wait_ge(sem["at_ropem"], upto(0, i, g))
                for b in range(2):
                    ins = pool_.tensor_tensor(Bb[g][:, b * W:(b + 1) * W], A[g][:, 2 * b * W:(2 * b + 1) * W],
                                              A[g][:, (2 * b + 1) * W:(2 * b + 2) * W], ALU.add)
                ins.then_inc(sem["at_qk"], 1)

            def neg_max(pool, i, g):
                pool.wait_ge(sem["gat_max"], upto(3, i, g))
                pool_.tensor_tensor(neg_row[:, g, :], row[:, g, :], s("scale3"), ALU.mult).then_inc(sem["at_nmax"], 1)

            def add_x(pool, i, g):
                pool.wait_ge(sem["at_x1"], upto(0, i, g))
                pool_.tensor_tensor(xgroup(i, g), xgroup(i, g), xn[g][:, :, :], ALU.add).then_inc(sem["at_xadd"], 1)

            def rms_x1(pool, i, g):
                pool.wait_ge(sem["at_sq"], upto(0, i, g))
                pool_.tensor_tensor(vare[:, g, :], tot[:, g, 0:GRAPHS], s("eps")[:, 2 * GRAPHS:3 * GRAPHS], ALU.add)\
                    .then_inc(sem["at_ms"], 1)
                pool.wait_ge(sem["at_ms"], upto(0, i, g))
                pool_.tensor_tensor(rstd[:, g, :], vare[:, g, :], s("minus_half")[:, 0:GRAPHS], ALU.pow)\
                    .then_inc(sem["at_rstd"], 1)

            def store_f(pool, i, g):
                pool.wait_ge(sem["at_ftc"], upto(0, i, g))
                pool.wait_ge(sem["x_new"], x_phase_done(PH_AT))
                pool_.tensor_copy(late[:, bass.ds(lin(i, NG * W, g * W), W)], xnt[g][:, :]).then_inc(sem["at_store"], 1)

            return [lambda p, i, g: ln_rstd(p, PH_AT, i, g), rms_of_ln, add_rope, neg_max, rms_x1, add_x, store_f]

        PH_BIG = 8
        NC3 = len(CHUNKS3)

        UP = ((PS[0][0], PS[0][1]), (PS[0][2], PS[0][3]), (PS[1][0], PS[1][1]))
        SILU = (Cc[0][:, 0:W], Cc[0][:, W:2 * W], Cc[1][:, 0:W])
        assert NC3 == len(UP) and NG == 2 and ITER > 1

        def nth(at, factor=1, more=0):
            e, i, g = at
            return lin(i, NG * factor, (e * GROUPS + g) * factor + more)

        def before(at, k):
            e, (register, ahead), g = at
            if g >= k:
                return e, (register, ahead), g - k
            if register is None and ahead == 0:
                return (e - 1, (None, ITER - 1), g - k + NG) if e else None
            return e, (register, ahead - 1), g - k + NG

        def hidden(g, c):
            return A[g][:, c * W:(c + 1) * W]

        def f_high(g):
            return B_r[g][:, 0:W]

        def f_low(g):
            return B_r[g][:, W:2 * W]

        def f_all(at):
            return late[:, bass.ds(lin(at[1], NG * W, at[2] * W), W)]

        def w_whole(e, name, memory=big):
            a = BIG3[name][0] + e * HID3
            return memory[:, a:a + HID3]

        def w_low(e, name):
            return w_whole(e, name, big_r)

        def w_high(e, name):
            a = 2 * W + (0, HID3)[name == "w3"]
            return B_r[e % 2][:, a:a + HID3]

        def big_loop(eng, visit, between, rest):
            for e in range(E3):
                for g in range(NG):
                    visit((e, (None, 0), g))
                between(e)
                with eng.Fori(0, ITER - 1) as i:
                    for g in range(NG):
                        visit((e, (i, 1), g))
            rest()

        LAST = (E3 - 1, (None, ITER - 1), NG - 1)

        def big_pe(pe):
            pe.sem_inc(sem["big_y"], 1)
            pe.sem_inc(sem["big_y"], 1)
            pe.wait_ge(sem["x_new"], x_phase_done(PH_BIG))

            def up(at, c):
                e, i, g = at
                c0, m = CHUNKS3[c]
                if c == 0:
                    pe.wait_ge(sem["big_flow"], nth(at, 1, 1))
                    if i[0] is None and g == 0:
                        pe.wait_ge(sem["big_wlow"], e + 1)
                pe.wait_ge(sem["big_hh"], nth(at, NC3, c + 1))
                for bank, name in zip(UP[c], ("w1", "w3")):
                    parts = [(w_high(e, name), f_high(g)), (w_high(e, name), f_low(g)), (w_low(e, name), f_high(g))]
                    for n, (w, f) in enumerate(parts):
                        ins = pe_.matmul(bank[0:m, :], w[:, c0:c0 + m], f,
                                         start=n == 0, stop=n == 2)
                ins.then_inc(sem["big_up"], 1)

            def down(at):
                e, i, g = at
                pe.wait_ge(sem["big_hh"], nth(at, NC3, 2 * NC3))
                pe.wait_ge(sem["big_x"], nth(at, 1, 1))
                a = BIG3["w2"][0]
                for q in range(GRAPHS):
                    for c, (c0, m) in enumerate(CHUNKS3):
                        ins = pe_.matmul(slot(PS[1][2 + g], q), hidden(g, c)[0:m, q * N:(q + 1) * N],
                                         big[0:m, a + (e * NC3 + c) * C:a + (e * NC3 + c + 1) * C],
                                         start=c == 0, stop=c == NC3 - 1)
                ins.then_inc(sem["big_y"], 1)

            def visit(at):
                up(at, 0)
                up(at, 1)
                if before(at, 1):
                    down(before(at, 1))
                up(at, 2)

            big_loop(pe, visit, lambda e: None, lambda: down(LAST))

        def big_act(act):
            def visit(at):
                for c, (_, m) in enumerate(CHUNKS3):
                    act.wait_ge(sem["big_up"], nth(at, NC3, c + 1))
                    act_.activation(SILU[c][0:m, :], UP[c][0][0:m, :], ACT.Silu).then_inc(sem["big_silu"], 1)

            act.wait_ge(sem["x_new"], x_phase_done(PH_BIG))
            big_loop(act, visit, lambda e: None, lambda: None)

        def big_pool(pool):
            pool.wait_ge(sem["x_new"], x_phase_done(PH_BIG))

            def weights_low(e):
                pool.wait_ge(sem["big_whigh"], e + 1)
                for name in ("w1", "w3"):
                    ins = pool_.tensor_tensor(w_low(e, name), w_whole(e, name), w_high(e, name).bitcast(F32), ALU.subtract)
                ins.then_inc(sem["big_wlow"], 1)

            def visit(at):
                pool.wait_ge(sem["big_fhigh"], nth(at, 1, 1))
                pool_.tensor_tensor(f_low(at[2]), f_all(at), f_high(at[2]).bitcast(F32), ALU.subtract).then_inc(sem["big_flow"], 1)

            weights_low(0)
            big_loop(pool, visit, lambda e: weights_low(e + 1) if e + 1 < E3 else None, lambda: None)

        def big_dve(dve):
            for _ in range(NC3):
                dve.sem_inc(sem["big_hh"], 1)
            for _ in range(2):
                dve.sem_inc(sem["big_x"], 1)
            dve.wait_ge(sem["x_new"], x_phase_done(PH_BIG))
            dve.wait_ge(sem["const_bias"], 1)
            for g in range(NG):
                dve.wait_ge(turn("gate_step", g), ITER * (ONE_N + TWO_N + AT_N))

            def weights_high(e):
                if e >= 2:
                    dve.wait_ge(sem["big_up"], (e - 1) * GROUPS * NC3)
                for name in ("w1", "w3"):
                    ins = dve_.tensor_copy(w_high(e, name), w_whole(e, name))
                ins.then_inc(sem["big_whigh"], 1)

            def inputs_high(at):
                e, i, g = at
                if before(at, 2):
                    dve.wait_ge(sem["big_up"], nth(before(at, 2), NC3, NC3))
                dve_.tensor_copy(f_high(g), f_all(at)).then_inc(sem["big_fhigh"], 1)

            def gate_weights(at):
                e, i, g = at
                dve.wait_ge(sem["big_x"], nth(at, 1, 1))
                dve_.tensor_copy(gsm[g][:, 0, 0:GE3], weights3[:, bass.ds(lin(i, NG * GE3, g * GE3), GE3)])\
                    .then_inc(sem["big_w"], 1)

            def multiply(at, c):
                e, i, g = at
                m = CHUNKS3[c][1]
                if c == 0:
                    dve.wait_ge(sem["big_y"], nth(at, 1, 1))
                dve.wait_ge(sem["big_silu"], nth(at, NC3, c + 1))
                dve_.tensor_tensor(hidden(g, c)[0:m, :], UP[c][1][0:m, :], SILU[c][0:m, :], ALU.mult)\
                    .then_inc(sem["big_hh"], 1)

            def add(at):
                e, i, g = at
                dve.wait_ge(sem["big_w"], nth(at, 1, 1))
                dve.wait_ge(sem["big_y"], nth(at, 1, 3))
                for q in range(GRAPHS):
                    ins = dve_.scalar_tensor_tensor(out=xg(i, g, q), in0=slot(PS[1][2 + g], q),
                                                    scalar=gsm[g][:, 0, q * E3 + e:q * E3 + e + 1], in1=xg(i, g, q),
                                                    op0=ALU.mult, op1=ALU.add)
                ins.then_inc(sem["big_x"], 1)
                if e == E3 - 1:
                    dve.wait_ge(sem["big_x"], nth(at, 1, 3))
                    dve.sem_inc(sem["x_new"], 1)

            def visit(at):
                one, two = before(at, 1), before(at, 2)
                inputs_high(at)
                if one:
                    multiply(one, 1)
                if two:
                    add(two)
                if one:
                    multiply(one, 2)
                gate_weights(at)
                multiply(at, 0)

            def rest():
                multiply(LAST, 1)
                add(before(LAST, 1))
                multiply(LAST, 2)
                add(LAST)

            weights_high(0)
            big_loop(dve, visit, lambda e: weights_high(e + 1) if e + 1 < E3 else None, rest)

        GAT_WAY = "D1.0 D.3 P.5 D.6 T.5 A.7 T.5 T1.0 A.7 A.3 D.9 A1.3 T.5 D.6 T.5 D.8"
        SSM_WAY = ("D1.0 D.3 P.5 D.6 P0 T.5 A.7 T1.5 A1.5 D0 D0 A.2 A.2 D1.0 D.1 D.1 D1.0 P1.0 D1.0 A1.2 D1.2 T.9 A1.2 D1.2 T1.4 D1.2 "
                   "T.6 T.6 A.6 A.6 T.6 D.5 A.6 D.5 T.6 D.5 A.6 D.5 T3.0 D1.2 A.5 T1.0 P.5 A1.2 T1.0 D.8")
        MHA_WAY = ("D1.0 D.3 P.5 D.6 P0 T.5 A.7 D.5 T1.5 A1.8 D0 T1.8 D3.3 A4.6 T1.8 A.6 D.6 T1.0 D.5 "
                   "T1.8 D3.3 A4.6 T1.8 A.6 D.6 T1.0 D.5 T.5 A.6 T.9 D.6")
        ONE_WAY = ("D1.0 D.3 P.5 D.6 T.5 A.7 T3.5 A2.4 D1.4 T1.8 D2.4 D.2 D.2 D.2 T5.3 A.3 D.2 D.2 D.2 D.2 D.2 D.2 D.2 D.2 T.2 A.2 T.5 D.6 "
                   "T5.3 D1.2 P0 T5.3 D1.2 P0 T5.3 D1.2 P0 D1.2 P3.0")
        TWO_WAY = ("D1.0 D.3 P.5 D.6 T.5 A.7 T.4 T.4 A.6 T.4 D.1 D.1 D.1 T.4 A.6 A.2 D.6 T.4 A.6 T.4 D.6 " + "D.1 " * 5
                   + "T.4 T.4 A.6 D.6 " + "D.1 " * 5 + "T.4 T.4 A.6 D.6 T.4 " + "D.1 " * 5 + "A.2 D.6 " + "D.2 " * 6 + "T.2 A.2 T.9 D.6 T.5 D.6 P0 T.5 D.6 P0 T.5 D.6 P0 T.5 D.6 P1.4")
        AT_WAY = ("D1.0 D.3 P.5 P1.0 D1.0 T.5 A.7 T1.8 D2.2 T.5 P2.2 A.4 T2.7 D2.2 P.4 A4.6 T1.8 D1.2 A0 T1.8 D.6 T.5 A.6 T.5 D.6 A1.2 P.5 P1 "
                  "D.6 T.5 A.6 T.5 P0 D.2 D.2 D.2 A.2 " + "D.2 " * 20)

        def way(text):
            times, at = {}, 0.0
            for word in text.split():
                times.setdefault(word[0], []).append(at)
                at += float(word[1:])
            return times, at

        SHIFT = [0.25, 0, 0, 0, 0.25, 0.4, 0.25, 0]
        AHEAD = [3.0, 3.0, 3.5, 6.0, 3.0, 3.0, 3.0, 2.5]
        WAYS = [way(GAT_WAY), way(SSM_WAY), way(MHA_WAY), way(ONE_WAY), way(GAT_WAY), way(TWO_WAY), way(GAT_WAY), way(AT_WAY)]

        def run_phases(eng, letter, stages, before=(), rest_loaded=None):
            before = dict(before)
            left = []

            def emit(todo):
                for _, g, stage, i in sorted(todo, key=lambda t: t[0]):
                    stage(eng, i, g)

            for k, (listed, (times, whole)) in enumerate(zip(stages, WAYS)):
                if k in before:
                    before[k]()
                length = whole - AHEAD[k]
                mine = times.get(letter, [])
                assert len(mine) == len(listed), (letter, k, len(mine), len(listed))
                now, later = [], []
                for g in range(NG):
                    for at, stage in zip(mine, listed):
                        at += whole * g * SHIFT[k]
                        (now if at < length else later).append((at, g, stage))
                emit([(share + g * SHIFT[k], g, *rest) for share, g, *rest in left]
                     + [(at / whole, g, stage, (None, 0)) for at, g, stage in now])
                if k == 0 and rest_loaded:
                    rest_loaded()
                if ITER > 1:
                    with eng.Fori(0, ITER - 1) as i:
                        emit([(at, g, stage, (i, 1)) for at, g, stage in now]
                             + [(at - length, g, stage, (i, 0)) for at, g, stage in later])
                left = [(at / whole - 1 - g * SHIFT[k], g, stage, (None, ITER - 1)) for at, g, stage in later]
            emit(left)

        @block.sync
        def _(sp):
            sp.dma_start(small[:, :], small_in).then_inc(sem["loaded_small"], 16)
            c = NG * GRAPHS
            adj_b = adj.rearrange("p (b n) -> p b n", b=B)
            sp.dma_start(adj_b[:, 0:c, :], adj_dram[:, 0:c, :]).then_inc(sem["loaded_adj"], 16)
            sp.dma_start(x[:, 0:c, :], x_dram[:, 0:c, :]).then_inc(sem["loaded_x"], 16)
            sp.wait_ge(sem["loaded_adj"], 16)
            sp.dma_start(adj_b[:, c:B, :], adj_dram[:, c:B, :]).then_inc(sem["loaded_adj"], 16)
            sp.wait_ge(sem["loaded_x"], 16)
            sp.dma_start(x[:, c:B, :], x_dram[:, c:B, :]).then_inc(sem["loaded_x"], 16)
            if PHASES > 2:
                mha_sp(sp, (None, 0))
                sp.wait_ge(sem["x_new"], x_phase_done(PH_MHA))
                sp.dma_start(big[:, 0:4 * E1 * C], down1_in).then_inc(sem["loaded_down1"], 16)
                with sp.Fori(1, ITER) as i:
                    mha_sp(sp, (i, 0))
            if PHASES > 4:
                sp.wait_ge(sem["x_new"], x_phase_done(4))
                sp.dma_start(big[:, :], big3_in).then_inc(sem["loaded_big3"], 16)
            with sp.Fori(0, ITER) as i:
                c = NG * GRAPHS
                sp.wait_ge(sem["x_new"], lin((i, 0), NG, (PHASES - 1) * GROUPS + 2 * NG))
                sp.dma_start(out_dram[:, bass.ds(lin((i, 0), c, 0), c), :], x[:, bass.ds(lin((i, 0), c, 0), c), :])\
                    .then_inc(sem["stored"], 16)
            sp.wait_ge(sem["stored"], 16 * ITER)

        @block.gpsimd
        def _(pool):
            for _ in range(NG):
                pool.sem_inc(sem["x_new"], 1)
            pool.wait_ge(sem["loaded_small"], 16)
            run_phases(pool, "P", [ln_pool(0), ssm_pool(), mha_pool(), one_pool(), ln_pool(4), two_pool(), ln_pool(6),
                                   at_pool()][0:PHASES])
            if PHASES > 8:
                big_pool(pool)

        @block.scalar
        def _(act):
            act.wait_ge(sem["loaded_small"], 16)
            act_.activation(neg_a[:, :], s("a_log"), ACT.Exp).then_inc(sem["const_exp"], 1)
            run_phases(act, "A", [gat_act(0, 0), ssm_act(), mha_act(), one_act(), gat_act(4, 1), two_act(), gat_act(6, 2),
                                  at_act()][0:PHASES])
            if PHASES > 8:
                big_act(act)

        @block.vector
        def _(dve):
            dve.wait_ge(sem["loaded_small"], 16)
            dve_.tensor_copy(ident_bf[:, :], s("ident"))
            dve_.tensor_copy(future_bf[:, :], s("future"))
            dve_.tensor_copy(past_bf[:, :], s("past")).then_inc(sem["const_bf"], 1)
            for l in range(3):
                for j in range(2):
                    dve_.tensor_copy(a_rep[:, 2 * l + j, :], s(f"gat{l}_a")[:, j:j + 1].to_broadcast([128, 128]))
            dve_.tensor_copy(bv_rep[:, :], s("bv1").to_broadcast([128, 128])).then_inc(sem["const_rows"], 1)
            for name in ("in_z", "conv_w", "conv_b"):
                dve_.tensor_scalar(s(name), s(name), 0.5, None, ALU.mult)
            for name in ("q3", "q3r", "k3", "k3r", "v3"):
                dve_.tensor_scalar(s(name), s(name), s("ln1"), None, ALU.mult)
            dve_.tensor_scalar(s("router3"), s("router3"), s("ln2"), None, ALU.mult)
            dve_.tensor_scalar(neg_dist[:, :], s("dist"), -1.0, None, ALU.mult)
            for n, name in enumerate(("even", "odd")):
                dve_.tensor_scalar(q_fold[:, 2 * n:2 * n + 1], s(name), 0.25, None, ALU.mult)
                dve_.tensor_scalar(q_fold[:, 2 * n + 1:2 * n + 2], s("bq1"), s(name), 0.25, ALU.mult, ALU.mult)
            for j in range(2):
                dve_.tensor_scalar(diag_d[:, j, :], s("ident"), s("d_chan")[:, j:j + 1], None, ALU.mult)
            dve_.tensor_tensor(s("eb3"), s("eb3"), s("sb3"), ALU.add).then_inc(sem["const_folds"], 1)
            dve.wait_ge(sem["const_exp"], 1)
            dve_.tensor_scalar(neg_a[:, :], neg_a[:, :], -1.0, None, ALU.mult).then_inc(sem["const_a"], 1)
            dve.wait_ge(sem["const_score_psum"], 1)
            for l in range(3):
                dve_.tensor_copy(score_w[:, l, :, :], PS[0][l][:, 0:256].rearrange("p (j n) -> p j n", j=2))
            for j in range(2):
                dve_.tensor_scalar(mix[:, j, :], PS[1][j][:, 0:128], s("norm_w")[:, j:j + 1], None, ALU.mult)
            dve_.tensor_tensor(bias_out1[:, :], PS[1][2][:, 0:128], s("bo1"), ALU.add).then_inc(sem["const_score"], 1)
            def make_mask(a, b):
                dve_.tensor_scalar(late[:, 0:B * N // 2].bitcast(BF16)[:, a:b], adj[:, a:b], 0.0, NEG, ALU.is_le, ALU.mult)\
                    .then_inc(sem["const_mask"], 1)

            def rest_loaded():
                dve.wait_ge(sem["loaded_adj"], 32)
                make_mask(NG * W, B * N)
                dve.wait_ge(sem["loaded_x"], 32)

            dve.wait_ge(sem["loaded_adj"], 16)
            make_mask(0, NG * W)
            dve.wait_ge(sem["const_folds"], 1)
            dve.wait_ge(sem["const_a"], 1)
            dve.wait_ge(sem["const_score"], 1)
            dve.wait_ge(sem["loaded_x"], 16)

            def scale_big3():
                dve.wait_ge(sem["loaded_big3"], 16)
                a, b = BIG3["w1"][0], BIG3["w3"][1]
                dve_.tensor_scalar(big[:, a:b], big[:, a:b], s("ln2"), None, ALU.mult).then_inc(sem["const_bias"], 1)

            run_phases(dve, "D", [gat_dve(0, 0), ssm_dve(), mha_dve(), one_dve(), gat_dve(4, 1), two_dve(), gat_dve(6, 2),
                                  at_dve()][0:PHASES], {3: lambda: split_down1(dve), 6: scale_big3}, rest_loaded)
            if PHASES > 8:
                big_dve(dve)

        @block.tensor
        def _(pe):
            pe.wait_ge(sem["const_rows"], 1)
            for l in range(3):
                for j in range(2):
                    pe_.matmul(PS[0][l][:, j * 128:(j + 1) * 128], s(f"gat{l}_wt"), a_rep[:, 2 * l + j, :],
                               start=True, stop=True)
            for j in range(2):
                pe_.matmul(PS[1][j][:, 0:128], s("out_t")[:, j * 128:(j + 1) * 128], s("lin"), start=True, stop=True)
            pe_.matmul(PS[1][2][:, 0:128], bv_rep[:, :], s("o1"), start=True, stop=True)\
                .then_inc(sem["const_score_psum"], 1)
            pe.wait_ge(sem["const_score"], 1)
            pe.wait_ge(sem["const_folds"], 1)
            pe.wait_ge(sem["const_mask"], 1)
            run_phases(pe, "T", [gat_pe(0, 0), ssm_pe(), mha_pe(), one_pe(), gat_pe(4, 1), two_pe(), gat_pe(6, 2),
                                 at_pe()][0:PHASES], (), lambda: pe.wait_ge(sem["const_mask"], 2))
            if PHASES > 8:
                big_pe(pe)


def kernel(**inputs):
    import concourse.bacc as bacc
    from concourse.bass_utils import run_bass_kernel_spmd

    v = {k: np.asarray(a) for k, a in inputs.items()}
    f = np.float32
    tri = np.arange(128)
    HD = HD3
    inv_freq = 1.0 / 10000.0 ** (np.arange(0, HD, 2, dtype=np.float32) / HD)
    freqs = np.outer(np.arange(N, dtype=np.float32), inv_freq)
    emb = np.concatenate([freqs, freqs], axis=-1)
    sign = np.where(np.arange(HD) < HD // 2, -1.0, 1.0).astype(f)
    half = np.concatenate([np.arange(HD // 2, HD), np.arange(HD // 2)])
    rot = np.concatenate([h * HD + half for h in range(NH3)])

    def rows(a, n=128):
        return np.tile(a.reshape(1, -1), (n, 1))

    def pad(a):
        return np.concatenate([a, np.zeros((128 - a.shape[0], a.shape[1]), a.dtype)]) if a.shape[0] < 128 else a

    def blocks(a):
        e = a.shape[0]
        out = np.zeros((GRAPHS * e, GRAPHS * 128), a.dtype)
        for g in range(GRAPHS):
            out[g * e:(g + 1) * e, g * 128:(g + 1) * 128] = a
        return out

    w_in = v["L0_ffn_W_in"]
    k3 = v["L3_ffn_wk"].reshape(2, HD, C)[[0, 0, 1, 1]].reshape(128, C)
    parts = {
        "ident": np.eye(128, dtype=f), "upto": (tri[:, None] <= tri[None]).astype(f),
        "after": (tri[:, None] > tri[None]).astype(f),
        "future": np.where(tri[None] > tri[:, None], f(NEG), f(0)), "past": np.where(tri[:, None] > tri[None], f(NEG), f(0)),
        "cos": np.tile(np.cos(emb).T, (NH3, 1)), "sin": np.tile((np.sin(emb) * sign).T, (NH3, 1)),
        "rank8": rows(np.arange(8, 0, -1).astype(f)), "rank4": rows(np.arange(4, 0, -1).astype(f)),
        "even": (tri // DK1 % 2 == 0).astype(f)[:, None], "odd": (tri // DK1 % 2 == 1).astype(f)[:, None],
        "minus_half": np.full((128, 8), -0.5, f),
        "eps": rows(np.repeat(np.array([EPS_LN, EPS_RMS3, C * EPS_RMS3], f), GRAPHS)),
        "scale3": np.full((128, 16), -SCALE3, f),
        "in_xbc": w_in[:, 256:640], "in_z": w_in[:, 0:256], "in_dt": w_in[:, 640:644],
        "conv_w": v["L0_ffn_conv_w"].reshape(3, 128, 4).transpose(1, 0, 2).reshape(128, 12),
        "conv_b": v["L0_ffn_conv_b"].reshape(3, 128).T, "dt_bias": rows(v["L0_ffn_dt_bias"]),
        "a_log": rows(v["L0_ffn_A_log"]), "d_chan": np.repeat(v["L0_ffn_D"], P0).reshape(2, 128).T,
        "norm_w": v["L0_ffn_norm_w"].reshape(2, 128).T, "out_t": v["L0_ffn_W_out"].T, "lin": v["L0_ffn_W_lin"],
        "b_lin": rows(v["L0_ffn_b_lin"]),
        "q1": v["L1_gnn_W_q"], "k1": v["L1_gnn_W_k"], "v1": v["L1_gnn_W_v"], "o1": v["L1_gnn_W_o"],
        "bq1": v["L1_gnn_b_q"][:, None], "bk1": v["L1_gnn_b_k"][:, None], "bv1": v["L1_gnn_b_v"][:, None],
        "bo1": rows(v["L1_gnn_b_o"]), "dist": rows(v["L1_gnn_dist_scale"].reshape(1)),
        "up1": v["L1_ffn_W1"], "b_up1": v["L1_ffn_b1"].reshape(4, 128).T,
        "gate1": v["L1_ffn_Wg"].reshape(4, 128, E1).transpose(1, 0, 2).reshape(128, 4 * E1),
        "b_gate1": rows(v["L1_ffn_bg"]), "b_down1": pad(blocks(v["L1_ffn_bd"])),
        "s1": v["L2_ffn_sW1"], "s2": v["L2_ffn_sW2"], "s3": v["L2_ffn_sW3"], "sb1": v["L2_ffn_sb1"][:, None],
        "sb2": v["L2_ffn_sb2"][:, None], "e1": v["L2_ffn_eW1"].transpose(1, 0, 2).reshape(128, E2 * 128),
        "eb1": v["L2_ffn_eb1"].T, "e2": v["L2_ffn_eW2"].transpose(1, 0, 2).reshape(128, E2 * EH2),
        "eb2": pad(v["L2_ffn_eb2"].T), "e3": pad(v["L2_ffn_eW3"].transpose(1, 0, 2).reshape(EH2, E2 * 128)),
        "eb3": pad(blocks(v["L2_ffn_eb3"])), "sb3": pad(blocks(rows(v["L2_ffn_sb3"], E2))),
        "gate2": v["L2_ffn_gW"], "b_gate2": rows(v["L2_ffn_gb"]),
        "ln1": v["L3_ffn_ln1_w"][:, None], "ln2": v["L3_ffn_ln2_w"][:, None],
        "q3": v["L3_ffn_wq"].T, "q3r": v["L3_ffn_wq"][rot].T, "k3": k3.T, "k3r": k3[rot].T,
        "v3": v["L3_ffn_wv"].T, "o3": v["L3_ffn_wo"].T, "router3": v["L3_ffn_router_w"].T,
    }
    for l, n in enumerate(("L0", "L2", "L3")):
        w, a = v[f"{n}_gnn_W"], v[f"{n}_gnn_a"]
        w = w.T if n == "L2" else w
        parts[f"gat{l}_w"], parts[f"gat{l}_wt"] = w, w.T
        parts[f"gat{l}_a"] = a.reshape(2, 128).T
    small = np.concatenate([parts[name] for name, _ in SMALL], axis=1)
    down1 = v["L1_ffn_Wd"].reshape(E1, 4, 128, C).transpose(2, 1, 0, 3).reshape(128, 4 * E1 * C)
    w2 = v["L3_ffn_w2"].transpose(0, 2, 1)
    w2 = np.pad(w2, ((0, 0), (0, 3 * CHUNK3 - HID3), (0, 0))).reshape(E3, 3, CHUNK3, C)
    w2 = np.pad(w2, ((0, 0), (0, 0), (0, 128 - CHUNK3), (0, 0)))
    big3 = np.concatenate([v["L3_ffn_w1"].transpose(2, 0, 1).reshape(C, E3 * HID3),
                           v["L3_ffn_w3"].transpose(2, 0, 1).reshape(C, E3 * HID3),
                           w2.transpose(2, 0, 1, 3).reshape(128, E3 * 3 * C)], axis=1)

    arrays = {"x_dram": v["x"], "adj_dram": v["adj"], "small_dram": small, "down1_dram": down1, "big3_dram": big3}
    arrays = {n: np.ascontiguousarray(a) for n, a in arrays.items()}
    nc = bacc.Bacc("TRN2", target_bir_lowering=False, num_devices=1)
    args = [nc.dram_tensor(n, a.shape, mybir.dt.from_np(a.dtype), kind="ExternalInput").ap() for n, a in arrays.items()]
    args.append(nc.dram_tensor("out_dram", v["x"].shape, F32, kind="ExternalOutput").ap())
    program(nc, *args)
    r = run_bass_kernel_spmd(nc, [arrays], core_ids=[0])
    return r.results[0]["out_dram"]
```
